# Optimizing a Trainium2 kernel written in Bass

```python
import numpy as np
import jax
import jax.numpy as jnp

def _softmax(x, axis=-1):
    return jax.nn.softmax(x, axis=axis)

def _gelu(x):
    return jax.nn.gelu(x, approximate=True)

def _silu(x):
    return jax.nn.silu(x)

def _sigmoid(x):
    return jax.nn.sigmoid(x)

def _layernorm(x, axis=-1, eps=1e-05):
    m = jnp.mean(x, axis=axis, keepdims=True)
    v = jnp.var(x, axis=axis, keepdims=True)
    return (x - m) / jnp.sqrt(v + eps)

def _scatter_add(tgt, idx, src, axis=0):
    return tgt.at[idx].add(src)

def _segment_sum(src, seg, n):
    return jax.ops.segment_sum(src, seg, n)
kernel_name = 'mk_hybrid_d1_jaxref_r8_c68f3c'

def setup_inputs(seed: int=0):
    np.random.seed(seed)
    _w = jnp.asarray

    def _L0_attn_a_setup():
        import math
        import jax, jax.numpy as jnp
        import numpy as np
        from jax import lax
        D_MODEL = 128
        N_LAYERS = 2
        D_STATE = 16
        D_CONV = 4
        EXPAND = 2
        D_INNER = EXPAND * D_MODEL
        DT_RANK = math.ceil(D_MODEL / 16)
        BATCH = 2
        SEQLEN = 128
        BETA = 0.6
        ALPHA = 1.0
        EPS = 1e-05
        DT_MIN, DT_MAX, DT_FLOOR = (0.001, 0.1, 0.0001)

        def _rmsnorm(x, w):
            return x * jax.lax.rsqrt(jnp.mean(x * x, axis=-1, keepdims=True) + EPS) * w

        def _block(x, in_w, cw, cb, xp_w, dtw, dtb, a_log, dp, ow):
            B, L, _ = x.shape
            xz = jnp.einsum('bld,ed->ble', x, in_w)
            xb, z = jnp.split(xz, 2, axis=-1)
            xc = lax.conv_general_dilated(xb.transpose(0, 2, 1), cw[:, None, :], window_strides=(1,), padding=[(D_CONV - 1, 0)], dimension_numbers=('NCH', 'OIH', 'NCH'), feature_group_count=D_INNER)
            xb = jax.nn.silu((xc + cb[None, :, None]).transpose(0, 2, 1))
            dbc = jnp.einsum('ble,re->blr', xb, xp_w)
            delta = dbc[..., :DT_RANK]
            Bm = dbc[..., DT_RANK:DT_RANK + D_STATE]
            Cm = dbc[..., DT_RANK + D_STATE:]
            delta = jax.nn.softplus(jnp.einsum('blr,er->ble', delta, dtw) + dtb)
            dA = jnp.exp(delta[..., None] * -jnp.exp(a_log))
            mi = ALPHA * delta[..., None] * Bm[:, :, None, :] * xb[..., None]

            def scan_fn(carry, inp):
                h, v = carry
                dA_t, mi_t, C_t = inp
                v = BETA * v + mi_t
                h = dA_t * h + v
                y_t = jnp.einsum('ben,bn->be', h, C_t)
                return ((h, v), y_t)
            h0 = jnp.zeros((B, D_INNER, D_STATE), dtype=x.dtype)
            _, ys = lax.scan(scan_fn, (h0, h0), (dA.transpose(1, 0, 2, 3), mi.transpose(1, 0, 2, 3), Cm.transpose(1, 0, 2)))
            y = ys.transpose(1, 0, 2) + dp * xb
            y = y * jax.nn.silu(z)
            return jnp.einsum('ble,de->bld', y, ow)
        key = jax.random.key(seed)
        ks = jax.random.split(key, 10)
        std = 0.02
        nl = N_LAYERS
        x = jax.random.normal(ks[0], (BATCH, SEQLEN, D_MODEL), dtype=jnp.float32)
        in_proj_w = jax.random.normal(ks[1], (nl, 2 * D_INNER, D_MODEL), dtype=jnp.float32) * std
        conv_w = jax.random.normal(ks[2], (nl, D_INNER, D_CONV), dtype=jnp.float32) * std
        conv_b = jnp.zeros((nl, D_INNER), dtype=jnp.float32)
        x_proj_w = jax.random.normal(ks[3], (nl, DT_RANK + 2 * D_STATE, D_INNER), dtype=jnp.float32) * std
        dt_std = DT_RANK ** (-0.5)
        dt_w = jax.random.uniform(ks[4], (nl, D_INNER, DT_RANK), dtype=jnp.float32, minval=-dt_std, maxval=dt_std)
        dt = jnp.exp(jax.random.uniform(ks[5], (nl, D_INNER), dtype=jnp.float32) * (math.log(DT_MAX) - math.log(DT_MIN)) + math.log(DT_MIN))
        dt = jnp.clip(dt, DT_FLOOR, None)
        dt_b = dt + jnp.log(-jnp.expm1(-dt))
        A_log = jnp.broadcast_to(jnp.log(jnp.arange(1, D_STATE + 1, dtype=jnp.float32)), (nl, D_INNER, D_STATE)).copy()
        Dp = jnp.ones((nl, D_INNER), dtype=jnp.float32)
        out_w = jax.random.normal(ks[6], (nl, D_MODEL, D_INNER), dtype=jnp.float32) * std
        norm_w = jnp.ones((nl, D_MODEL), dtype=jnp.float32)
        return {'x': x, 'norm_w': norm_w, 'in_proj_w': in_proj_w, 'conv_w': conv_w, 'conv_b': conv_b, 'x_proj_w': x_proj_w, 'dt_w': dt_w, 'dt_b': dt_b, 'A_log': A_log, 'Dp': Dp, 'out_w': out_w}
    _L0_attn_a_in = _L0_attn_a_setup()

    def _L0_attn_b_setup():
        import jax, jax.numpy as jnp
        from jax import lax
        import numpy as np
        D = 128
        H = 16
        DK = D // 2 // H
        DV = D // H
        GATE_NORM = 16.0
        SCALE = DK ** (-0.5)
        EPS = 1e-05

        def _split_heads(x, dh):
            B, L, _ = x.shape
            return x.reshape(B, L, H, dh).transpose(0, 2, 1, 3)

        def _gla_scan(q, k, v, log_gate):
            B = q.shape[0]
            qt = jnp.moveaxis(q, 2, 0)
            kt = jnp.moveaxis(k, 2, 0)
            vt = jnp.moveaxis(v, 2, 0)
            gt = jnp.exp(jnp.moveaxis(log_gate, 2, 0))

            def step(state, inp):
                qq, kk, vv, gg = inp
                state = state * gg[..., None] + kk[..., :, None] * vv[..., None, :]
                out = jnp.einsum('bhd,bhde->bhe', qq, state)
                return (state, out)
            init = jnp.zeros((B, H, DK, DV), dtype=q.dtype)
            _, outs = lax.scan(step, init, (qt, kt, vt, gt))
            return jnp.moveaxis(outs, 0, 2)
        key = jax.random.key(seed)
        ks = jax.random.split(key, 10)
        s = 0.02
        return {'inputs': jax.random.normal(ks[0], (4, 512, D), dtype=jnp.float32), 'Wq': jax.random.normal(ks[1], (D, D // 2), dtype=jnp.float32) * s, 'Wk': jax.random.normal(ks[2], (D, D // 2), dtype=jnp.float32) * s, 'Wg1': jax.random.normal(ks[3], (D, 16), dtype=jnp.float32) * s, 'Wg2': jax.random.normal(ks[4], (16, D // 2), dtype=jnp.float32) * s, 'Wv': jax.random.normal(ks[5], (D, D), dtype=jnp.float32) * s, 'Wg': jax.random.normal(ks[6], (D, D), dtype=jnp.float32) * s, 'bg': jax.random.normal(ks[7], (D,), dtype=jnp.float32) * s, 'Wo': jax.random.normal(ks[8], (D, D), dtype=jnp.float32) * s}
    _L0_attn_b_in = _L0_attn_b_setup()

    def _L0_ffn_setup():
        import jax, jax.numpy as jnp
        import numpy as np
        B, S, D = (4, 256, 128)
        E = 8
        DFF = 512
        CAP_FACTOR = 1.25
        key = jax.random.key(seed)
        ks = jax.random.split(key, 4)
        std_gate = float(np.sqrt(0.1 / D))
        inputs = jax.random.normal(ks[0], (B, S, D), dtype=jnp.float32)
        gate_w = jax.random.normal(ks[1], (E, D), dtype=jnp.float32) * std_gate
        w1 = jax.random.normal(ks[2], (E, D, DFF), dtype=jnp.float32) * (1.0 / np.sqrt(D))
        b1 = jnp.zeros((E, DFF), dtype=jnp.float32)
        w2 = jax.random.normal(ks[3], (E, DFF, D), dtype=jnp.float32) * (1.0 / np.sqrt(DFF))
        b2 = jnp.zeros((E, D), dtype=jnp.float32)
        return {'inputs': inputs, 'gate_w': gate_w, 'w1': w1, 'b1': b1, 'w2': w2, 'b2': b2}
    _L0_ffn_in = _L0_ffn_setup()
    _d = {'L0_attn_a_x': _L0_attn_a_in['x'], 'L0_attn_a_norm_w': _L0_attn_a_in['norm_w'], 'L0_attn_a_in_proj_w': _L0_attn_a_in['in_proj_w'], 'L0_attn_a_conv_w': _L0_attn_a_in['conv_w'], 'L0_attn_a_conv_b': _L0_attn_a_in['conv_b'], 'L0_attn_a_x_proj_w': _L0_attn_a_in['x_proj_w'], 'L0_attn_a_dt_w': _L0_attn_a_in['dt_w'], 'L0_attn_a_dt_b': _L0_attn_a_in['dt_b'], 'L0_attn_a_A_log': _L0_attn_a_in['A_log'], 'L0_attn_a_Dp': _L0_attn_a_in['Dp'], 'L0_attn_a_out_w': _L0_attn_a_in['out_w'], 'L0_attn_b_Wq': _L0_attn_b_in['Wq'], 'L0_attn_b_Wk': _L0_attn_b_in['Wk'], 'L0_attn_b_Wg1': _L0_attn_b_in['Wg1'], 'L0_attn_b_Wg2': _L0_attn_b_in['Wg2'], 'L0_attn_b_Wv': _L0_attn_b_in['Wv'], 'L0_attn_b_Wg': _L0_attn_b_in['Wg'], 'L0_attn_b_bg': _L0_attn_b_in['bg'], 'L0_attn_b_Wo': _L0_attn_b_in['Wo'], 'L0_ffn_gate_w': _L0_ffn_in['gate_w'], 'L0_ffn_w1': _L0_ffn_in['w1'], 'L0_ffn_b1': _L0_ffn_in['b1'], 'L0_ffn_w2': _L0_ffn_in['w2'], 'L0_ffn_b2': _L0_ffn_in['b2']}
    _x0 = _d['L0_attn_a_x']
    _d['L0_attn_a_x'] = jax.random.normal(jax.random.fold_in(jax.random.key(seed), 1), (4, 512, 128), dtype=_x0.dtype)
    del _x0
    return _d

def reference(L0_attn_a_x, L0_attn_a_norm_w, L0_attn_a_in_proj_w, L0_attn_a_conv_w, L0_attn_a_conv_b, L0_attn_a_x_proj_w, L0_attn_a_dt_w, L0_attn_a_dt_b, L0_attn_a_A_log, L0_attn_a_Dp, L0_attn_a_out_w, L0_attn_b_Wq, L0_attn_b_Wk, L0_attn_b_Wg1, L0_attn_b_Wg2, L0_attn_b_Wv, L0_attn_b_Wg, L0_attn_b_bg, L0_attn_b_Wo, L0_ffn_gate_w, L0_ffn_w1, L0_ffn_b1, L0_ffn_w2, L0_ffn_b2):

    def _L0_attn_a_ref(x, norm_w, in_proj_w, conv_w, conv_b, x_proj_w, dt_w, dt_b, A_log, Dp, out_w):
        import math
        import jax, jax.numpy as jnp
        import numpy as np
        from jax import lax
        D_MODEL = 128
        N_LAYERS = 2
        D_STATE = 16
        D_CONV = 4
        EXPAND = 2
        D_INNER = EXPAND * D_MODEL
        DT_RANK = math.ceil(D_MODEL / 16)
        BATCH = 2
        SEQLEN = 128
        BETA = 0.6
        ALPHA = 1.0
        EPS = 1e-05
        DT_MIN, DT_MAX, DT_FLOOR = (0.001, 0.1, 0.0001)

        def _rmsnorm(x, w):
            return x * jax.lax.rsqrt(jnp.mean(x * x, axis=-1, keepdims=True) + EPS) * w

        def _block(x, in_w, cw, cb, xp_w, dtw, dtb, a_log, dp, ow):
            B, L, _ = x.shape
            xz = jnp.einsum('bld,ed->ble', x, in_w)
            xb, z = jnp.split(xz, 2, axis=-1)
            xc = lax.conv_general_dilated(xb.transpose(0, 2, 1), cw[:, None, :], window_strides=(1,), padding=[(D_CONV - 1, 0)], dimension_numbers=('NCH', 'OIH', 'NCH'), feature_group_count=D_INNER)
            xb = jax.nn.silu((xc + cb[None, :, None]).transpose(0, 2, 1))
            dbc = jnp.einsum('ble,re->blr', xb, xp_w)
            delta = dbc[..., :DT_RANK]
            Bm = dbc[..., DT_RANK:DT_RANK + D_STATE]
            Cm = dbc[..., DT_RANK + D_STATE:]
            delta = jax.nn.softplus(jnp.einsum('blr,er->ble', delta, dtw) + dtb)
            dA = jnp.exp(delta[..., None] * -jnp.exp(a_log))
            mi = ALPHA * delta[..., None] * Bm[:, :, None, :] * xb[..., None]

            def scan_fn(carry, inp):
                h, v = carry
                dA_t, mi_t, C_t = inp
                v = BETA * v + mi_t
                h = dA_t * h + v
                y_t = jnp.einsum('ben,bn->be', h, C_t)
                return ((h, v), y_t)
            h0 = jnp.zeros((B, D_INNER, D_STATE), dtype=x.dtype)
            _, ys = lax.scan(scan_fn, (h0, h0), (dA.transpose(1, 0, 2, 3), mi.transpose(1, 0, 2, 3), Cm.transpose(1, 0, 2)))
            y = ys.transpose(1, 0, 2) + dp * xb
            y = y * jax.nn.silu(z)
            return jnp.einsum('ble,de->bld', y, ow)
        for i in range(N_LAYERS):
            x = x + _block(_rmsnorm(x, norm_w[i]), in_proj_w[i], conv_w[i], conv_b[i], x_proj_w[i], dt_w[i], dt_b[i], A_log[i], Dp[i], out_w[i])
        return x

    def _L0_attn_b_ref(inputs, Wq, Wk, Wg1, Wg2, Wv, Wg, bg, Wo):
        import jax, jax.numpy as jnp
        from jax import lax
        import numpy as np
        D = 128
        H = 16
        DK = D // 2 // H
        DV = D // H
        GATE_NORM = 16.0
        SCALE = DK ** (-0.5)
        EPS = 1e-05

        def _split_heads(x, dh):
            B, L, _ = x.shape
            return x.reshape(B, L, H, dh).transpose(0, 2, 1, 3)

        def _gla_scan(q, k, v, log_gate):
            B = q.shape[0]
            qt = jnp.moveaxis(q, 2, 0)
            kt = jnp.moveaxis(k, 2, 0)
            vt = jnp.moveaxis(v, 2, 0)
            gt = jnp.exp(jnp.moveaxis(log_gate, 2, 0))

            def step(state, inp):
                qq, kk, vv, gg = inp
                state = state * gg[..., None] + kk[..., :, None] * vv[..., None, :]
                out = jnp.einsum('bhd,bhde->bhe', qq, state)
                return (state, out)
            init = jnp.zeros((B, H, DK, DV), dtype=q.dtype)
            _, outs = lax.scan(step, init, (qt, kt, vt, gt))
            return jnp.moveaxis(outs, 0, 2)
        B, L, _ = inputs.shape
        q = _split_heads(inputs @ Wq, DK)
        k = _split_heads(inputs @ Wk * SCALE, DK)
        kg = _split_heads(inputs @ Wg1 @ Wg2, DK)
        v = _split_heads(inputs @ Wv, DV)
        gate = jax.nn.silu(inputs @ Wg + bg)
        log_gate = jax.nn.log_sigmoid(kg) / GATE_NORM
        o = _gla_scan(q, k, v, log_gate)
        mu = jnp.mean(o, axis=-1, keepdims=True)
        var = jnp.var(o, axis=-1, keepdims=True)
        o = (o - mu) * lax.rsqrt(var + EPS)
        o = o.transpose(0, 2, 1, 3).reshape(B, L, D)
        return gate * o @ Wo

    def _L0_ffn_ref(inputs, gate_w, w1, b1, w2, b2):
        import jax, jax.numpy as jnp
        import numpy as np
        B, S, D = (4, 256, 128)
        E = 8
        DFF = 512
        CAP_FACTOR = 1.25
        d_model = inputs.shape[-1]
        tokens = inputs.reshape(-1, d_model)
        T = tokens.shape[0]
        num_experts = gate_w.shape[0]
        capacity = int(np.ceil(CAP_FACTOR * T / num_experts))
        logits = jnp.einsum('td,ed->te', tokens.astype(jnp.float32), gate_w)
        probs = jax.nn.softmax(logits, axis=-1)
        expert_idx = jnp.argmax(probs, axis=-1)
        mask = jax.nn.one_hot(expert_idx, num_experts, dtype=jnp.float32)
        ranks = jnp.cumsum(mask, axis=0) - 1.0
        keep = (ranks < capacity) * mask
        pos = ranks.astype(jnp.int32)
        sec_mask = jax.nn.one_hot(pos, capacity, dtype=jnp.float32) * keep[:, :, None]
        combine_weights = probs[:, :, None] * sec_mask
        dispatch = jnp.einsum('tec,td->ecd', sec_mask, tokens)
        h = jax.nn.relu(jnp.einsum('ecd,edh->ech', dispatch, w1) + b1[:, None, :])
        expert_out = jnp.einsum('ech,ehd->ecd', h, w2) + b2[:, None, :]
        ans = jnp.einsum('tec,ecd->td', combine_weights, expert_out)
        return ans.reshape(inputs.shape)
    x = L0_attn_a_x
    x = x + _L0_attn_a_ref(_layernorm(x, axis=-1), L0_attn_a_norm_w, L0_attn_a_in_proj_w, L0_attn_a_conv_w, L0_attn_a_conv_b, L0_attn_a_x_proj_w, L0_attn_a_dt_w, L0_attn_a_dt_b, L0_attn_a_A_log, L0_attn_a_Dp, L0_attn_a_out_w)
    x = x + _L0_ffn_ref(_layernorm(x, axis=-1), L0_ffn_gate_w, L0_ffn_w1, L0_ffn_b1, L0_ffn_w2, L0_ffn_b2)
    x = x + _L0_attn_b_ref(_layernorm(x, axis=-1), L0_attn_b_Wq, L0_attn_b_Wk, L0_attn_b_Wg1, L0_attn_b_Wg2, L0_attn_b_Wv, L0_attn_b_Wg, L0_attn_b_bg, L0_attn_b_Wo)
    x = x + _L0_ffn_ref(_layernorm(x, axis=-1), L0_ffn_gate_w, L0_ffn_w1, L0_ffn_b1, L0_ffn_w2, L0_ffn_b2)
    return x

_drawn_inputs = setup_inputs


def setup_inputs(seed=0):
    import zlib

    import numpy as np

    out = dict(_drawn_inputs(seed))
    spreads = {'L0_attn_a_norm_w': (1.0, 0.6),
     'L0_attn_a_conv_b': (0.0, 0.8),
     'L0_attn_a_Dp': (1.0, 0.6),
     'L0_ffn_b1': (0.0, 2.0),
     'L0_ffn_b2': (0.0, 2.0)}
    factors = {'L0_attn_a_in_proj_w': 8.0,
     'L0_attn_a_conv_w': 8.0,
     'L0_attn_a_x_proj_w': 8.0,
     'L0_attn_a_dt_w': 8.0,
     'L0_attn_a_dt_b': 8.0,
     'L0_attn_a_A_log': 8.0,
     'L0_attn_a_out_w': 8.0,
     'L0_attn_b_Wq': 29.021,
     'L0_attn_b_Wk': 29.3,
     'L0_attn_b_Wg1': 64.0,
     'L0_attn_b_Wg2': 64.0,
     'L0_attn_b_Wv': 28.531,
     'L0_attn_b_Wg': 31.376,
     'L0_attn_b_bg': 64.0,
     'L0_attn_b_Wo': 28.95,
     'L0_ffn_gate_w': 8.0,
     'L0_ffn_w1': 8.0,
     'L0_ffn_w2': 8.0}
    for name, (base, spread) in spreads.items():
        noise = np.random.default_rng([zlib.crc32(name.encode()), seed]).standard_normal(out[name].shape)
        drawn = base * np.exp(spread * noise) if base else spread * noise
        out[name] = jnp.asarray(drawn.astype(out[name].dtype))
    for name, factor in factors.items():
        out[name] = (out[name] * factor).astype(out[name].dtype)
    return out
```

```python
from contextlib import ExitStack

import numpy as np

import concourse.bass as bass
from concourse import mybir

P = 128
D = 128
B, SEQ = 4, 512
TOK = B * SEQ
NCH = 4
CH = TOK // NCH
LAYERS = 2
HALVES = 2
NST = 16
DTR = 8
KCONV = 4
BETA = 0.6
QTOK = 1024
EXP, DFF, CAP = 8, 512, 320
SLOTS = EXP * CAP
NBLK = TOK // P
TILES = [(0, 128), (128, 128), (256, 64)]
NT = len(TILES)
FJ = DFF // P
HEADS, DK, DV = 16, 4, 8
GT = HEADS * DK * DV // P
EPS = 1e-5
FAR = 4096.0

F32 = mybir.dt.float32
BF16 = mybir.dt.bfloat16
U32 = mybir.dt.uint32
ALU = mybir.AluOpType
ACT = mybir.ActivationFunctionType
AX = mybir.AxisListType

SM = {}
_at = 0
for _name, _n in (("conv_w", LAYERS * HALVES * KCONV), ("conv_b", LAYERS * HALVES), ("dt_b", LAYERS * HALVES),
                  ("dp", LAYERS * HALVES), ("norm_w", LAYERS), ("a_log", LAYERS * HALVES * NST),
                  ("b1", EXP * FJ), ("bg", 1), ("gate", EXP)):
    SM[_name] = _at
    _at += _n
SMALL = _at
C_ID, C_AVG, C_AVG8, C_TRI, C_ONE, C_RAMP, C_EBASE = range(7)
NCONST = 7
XW = 3 * 2 * NST + DTR
GQ, GK, GV, GG, GO, GG1, GEND = 0, 512, 1024, 1536, 1664, 1792, 1808
NORMS = [(True, None), (False, 0), (False, 1), (True, None), (True, None), (True, None), (True, None)]


def centred_before(k):
    return sum(c for c, _ in NORMS[:k])


def build(nc, io):
    with ExitStack() as ctx:
        def sb(name, shape, dt=F32):
            return ctx.enter_context(nc.sbuf_tensor(name, shape, dt))

        sems = {}

        def sem(name):
            if name not in sems:
                sems[name] = ctx.enter_context(nc.semaphore(name))
            return sems[name]

        X = sb("X", [P, TOK])
        XN = sb("XN", [P, TOK])
        F = sb("F", [P, 8 * TOK])
        T = sb("T", [P, 7 * TOK])
        COEF = sb("COEF", [P, TOK])
        STK = sb("STK", [P, TOK], BF16)
        SEL = sb("SEL", [P, 2 * NST, P], BF16)
        W1 = sb("W1", [P, EXP, DFF])
        W2 = sb("W2", [P, EXP, FJ, P])
        WIN = sb("WIN", [P, LAYERS, 4 * P])
        XPW = sb("XPW", [P, LAYERS, HALVES, XW])
        DTW = sb("DTW", [P, LAYERS, HALVES * P])
        WOUT = sb("WOUT", [P, LAYERS, HALVES, P])
        SMT = sb("SMT", [P, SMALL])
        CST = sb("CST", [P, NCONST, P])
        NEGA = sb("NEGA", [P, LAYERS * HALVES, NST])
        RT = sb("RT", [P, 10, P])
        RTS = sb("RTS", [P, 8, NBLK])
        IDX = sb("IDX", [P, 2, NBLK], U32)
        PS = ctx.enter_context(nc.psum_tensor("PS", [P, 8, CH], F32))

        ident = CST[:, C_ID, :]
        avg_all = CST[:, C_AVG, :]

        def tile(k):
            return T[:, k * TOK:(k + 1) * TOK]

        def small(name, k=0):
            return SMT[:, SM[name] + k:SM[name] + k + 1]

        def ch(ap, c):
            return ap[:, c * CH:(c + 1) * CH]

        def flat(ap):
            return ap.rearrange("p a b -> p (a b)")

        xs = F[:, 0:2 * TOK].rearrange("p (m t) -> p m t", m=HALVES)
        zs = F[:, 2 * TOK:4 * TOK].rearrange("p (m t) -> p m t", m=HALVES)
        delta = F[:, 4 * TOK:6 * TOK].rearrange("p (m t) -> p m t", m=HALVES)
        u = F[:, 6 * TOK:8 * TOK].rearrange("p (m t) -> p m t", m=HALVES)
        xpad = T[:, 0:HALVES * B * (SEQ + 3)].rearrange("p (m b t) -> p m b t", m=HALVES, b=B)
        drs = XN
        brow = [XN[:, 0:QTOK], XN[:, QTOK:2 * QTOK]]
        rows_in = F[:, 0:EXP * NT * P].rearrange("p (k d) -> p k d", d=P)
        rows_out = F[:, 3072:3072 + EXP * NT * P].rearrange("p (k d) -> p k d", d=P)
        xdisp = F[:, 6144:6144 + SLOTS]
        hid = [F[:, 8704 + k * FJ * CAP:8704 + (k + 1) * FJ * CAP].rearrange("p (j s) -> p j s", j=FJ) for k in (0, 1)]
        xtok = F[:, 11264:11264 + TOK].rearrange("p (k d) -> p k d", d=P)
        fetched = F[:, 13312:13312 + TOK].rearrange("p (k d) -> p k d", d=P)
        diag = tile(3).rearrange("p (k d) -> p k d", d=P)
        B2R = STK[:, :].bitcast(F32).rearrange("p (e d) -> p e d", e=EXP)
        GW = flat(SEL[:, :, :]).bitcast(F32)
        RED = COEF[:, 0:GT * P].rearrange("p (g m) -> p g m", g=GT)
        SPR = COEF[:, GT * P:2 * GT * P].rearrange("p (g m) -> p g m", g=GT)
        WG2 = COEF[:, 2 * GT * P:2 * GT * P + HEADS * DK]

        slots_in = [nc.dram_tensor(f"slots_in{k}", (SLOTS, D), F32, kind="Internal").ap() for k in (0, 1)]
        slots_out = [nc.dram_tensor(f"slots_out{k}", (SLOTS, D), F32, kind="Internal").ap() for k in (0, 1)]

        def norm_input(k, c):
            if k == 0:
                return [(sem("x_loaded"), 16)]
            if k == 1:
                return [(sem("norm_out"), c + 1)]
            if k == 2:
                return [(sem("outproj_added"), 2)]
            if k == 3:
                return [(sem("stream_added"), 1)]
            if k == 4:
                return [(sem("moe_added"), c + 1)]
            if k == 5:
                return [(sem("o_copied"), c // 2 + 1)]
            return [(sem("attn_added"), c + 1)]

        def norm_buffers(k):
            src = T[:, 6 * TOK:7 * TOK] if k == 5 else X[:, :]
            dst = X[:, :] if k == 0 else (T[:, 6 * TOK:7 * TOK] if k == 5 else XN[:, :])
            return src, dst, tile(3), tile(4), tile(5)

        def norm_pe(pe, k):
            src, _, _, sq, _ = norm_buffers(k)
            avg = CST[:, C_AVG8, :] if k == 5 else avg_all
            if NORMS[k][0]:
                for c in range(NCH):
                    for s, v in norm_input(k, c):
                        pe.wait_ge(s, v)
                    pe.matmul(PS[:, c, :], avg, ch(src, c), start=True, stop=True).then_inc(sem("mean_ps"), 1)
            for c in range(NCH):
                pe.wait_ge(sem("squared"), NCH * k + c + 1)
                pe.matmul(PS[:, 4 + c, :], avg, ch(sq, c), start=True, stop=True).then_inc(sem("var_ps"), 1)

        def norm_act(act, k):
            src, _, xc, sq, rs = norm_buffers(k)
            for c in range(NCH):
                if NORMS[k][0]:
                    act.wait_ge(sem("centred"), NCH * centred_before(k) + c + 1)
                    a = xc
                else:
                    for s, v in norm_input(k, c):
                        act.wait_ge(s, v)
                    a = src
                nc.scalar.activation(ch(sq, c), ch(a, c), ACT.Square).then_inc(sem("squared"), 1)
            for c in range(NCH):
                act.wait_ge(sem("var_ps"), NCH * k + c + 1)
                nc.scalar.activation(ch(rs, c), PS[:, 4 + c, :], ACT.Ln, bias=eps_col).then_inc(sem("log_var"), 1)
            for c in range(NCH):
                act.wait_ge(sem("log_var"), NCH * k + c + 1)
                nc.scalar.activation(ch(rs, c), ch(rs, c), ACT.Exp, scale=-0.5).then_inc(sem("rstd"), 1)

        def norm_dve(dve, k):
            src, dst, xc, _, rs = norm_buffers(k)
            centre, w = NORMS[k]
            if centre:
                for c in range(NCH):
                    dve.wait_ge(sem("mean_ps"), NCH * centred_before(k) + c + 1)
                    nc.vector.tensor_tensor(ch(xc, c), ch(src, c), PS[:, c, :], ALU.subtract).then_inc(sem("centred"), 1)
            for c in range(NCH):
                dve.wait_ge(sem("rstd"), NCH * k + c + 1)
                if centre:
                    dve.wait_ge(sem("centred"), NCH * centred_before(k) + c + 1)
                    nc.vector.tensor_tensor(ch(dst, c), ch(xc, c), ch(rs, c), ALU.mult).then_inc(sem("norm_out"), 1)
                else:
                    nc.vector.scalar_tensor_tensor(out=ch(dst, c), in0=ch(src, c), scalar=small("norm_w", w),
                                                   in1=ch(rs, c), op0=ALU.mult, op1=ALU.mult).then_inc(sem("norm_out"), 1)

        def norm_done(k, c=NCH - 1):
            return NCH * k + c + 1

        eps_tile = sb("EPSC", [P, 2])
        eps_col = eps_tile[:, 0:1]

        block = ctx.enter_context(nc.Block())

        @block.sync
        def _(sp):
            sp.dma_start(CST[:, :, :], io["consts"]).then_inc(sem("consts_loaded"), 16)
            sp.dma_start(X[:, :], io["x"]).then_inc(sem("x_loaded"), 16)
            sp.dma_start(SMT[:, :], io["small"]).then_inc(sem("small_loaded"), 16)
            sp.dma_start(WIN[:, :, :], io["w_in"]).then_inc(sem("mamba_loaded"), 16)
            sp.dma_start(XPW[:, :, :, :], io["w_x"]).then_inc(sem("mamba_loaded"), 16)
            sp.dma_start(DTW[96:96 + DTR, :, :], io["w_dt"]).then_inc(sem("mamba_loaded"), 16)
            sp.dma_start(WOUT[:, :, :, :], io["w_out"]).then_inc(sem("mamba_loaded"), 16)
            sp.dma_start(F[0:96, 0:2 * NST * P], io["sel"]).then_inc(sem("sel_loaded"), 16)
            sp.dma_start(W1[:, :, :], io["w1"]).then_inc(sem("experts_loaded"), 16)
            sp.dma_start(W2[:, :, :, :], io["w2"]).then_inc(sem("experts_loaded"), 16)
            sp.wait_ge(sem("zeros"), 1)
            for k in (0, 1):
                sp.dma_start(slots_in[k].rearrange("(p r) d -> p (r d)", p=P),
                             F[:, 6144:6144 + SLOTS]).then_inc(sem("slots_zeroed"), 16)
            sp.wait_ge(sem("outproj_added"), 2 * LAYERS)
            sp.dma_start(XN[:, :], io["x"]).then_inc(sem("x_again"), 16)
            sp.dma_start(flat(B2R), io["b2"]).then_inc(sem("b2_loaded"), 16)
            sp.dma_start(GW[:, 0:GEND], io["w_gla"]).then_inc(sem("gla_loaded"), 16)
            sp.dma_start(COEF[:, 0:2 * GT * P + HEADS * DK], io["gla_consts"]).then_inc(sem("gla_loaded"), 16)
            for k in (0, 1):
                sp.wait_ge(sem("scattered"), 16 * NBLK * (k + 1))
                for e in range(EXP):
                    sp.dma_start(rows_in[:, NT * e:NT * e + 2, :],
                                 slots_in[k][e * CAP:e * CAP + 256, :].rearrange("(j p) d -> p j d", p=P)
                                 ).then_inc(sem(f"rows_loaded{e}"), 16)
                    sp.dma_start(rows_in[0:64, NT * e + 2, :],
                                 slots_in[k][e * CAP + 256:(e + 1) * CAP, :]).then_inc(sem(f"rows_loaded{e}"), 16)
                for e in range(EXP):
                    sp.wait_ge(sem("rows_made"), NT * (EXP * k + e + 1))
                    sp.dma_start(slots_out[k][e * CAP:e * CAP + 256, :].rearrange("(j p) d -> p j d", p=P),
                                 rows_out[:, NT * e:NT * e + 2, :]).then_inc(sem("rows_stored"), 16)
                    sp.dma_start(slots_out[k][e * CAP + 256:(e + 1) * CAP, :],
                                 rows_out[0:64, NT * e + 2, :]).then_inc(sem("rows_stored"), 16)
            for c in range(NCH):
                sp.wait_ge(sem("moe_added"), NCH + c + 1)
                sp.dma_start(io["out"][:, c * CH:(c + 1) * CH], ch(X[:, :], c)).then_inc(sem("out_stored"), 16)
            sp.wait_ge(sem("slots_zeroed"), 32)
            sp.wait_ge(sem("rows_stored"), 16 * 2 * EXP * 2)
            sp.wait_ge(sem("out_stored"), 16 * NCH)

        @block.gpsimd
        def _(pool):
            nc.gpsimd.memset(eps_tile[:, :], EPS).then_inc(sem("eps_set"), 1)
            nc.gpsimd.memset(F[:, 6144:6144 + SLOTS], 0.0).then_inc(sem("zeros"), 1)
            pool.wait_ge(sem("sel_loaded"), 16)
            nc.gpsimd.tensor_copy(flat(SEL[0:96, :, :]), F[0:96, 0:2 * NST * P]).then_inc(sem("sel_ready"), 1)
            nc.gpsimd.memset(COEF[:, :], BETA).then_inc(sem("coef_filled"), 1)
            pool.wait_ge(sem("coef_filled"), 1)
            nc.gpsimd.memset(COEF[:, :].rearrange("p (s t) -> p s t", t=SEQ)[:, :, 0:1], 0.0).then_inc(sem("coef_ready"), 1)
            for L in range(LAYERS):
                pool.wait_ge(sem("norm_out"), norm_done(1 + L))
                nc.gpsimd.memset(flat(xpad.rearrange("p m b t -> p (m b) t"))[:, :].rearrange(
                    "p (s t) -> p s t", t=SEQ + 3)[:, :, 0:3], 0.0).then_inc(sem("pad_zeroed"), 1)
                for m in range(HALVES):
                    pool.wait_ge(sem("delta_ready"), HALVES * L + m + 1)
                    nc.gpsimd.tensor_tensor(u[:, m, :], delta[:, m, :], xs[:, m, :], ALU.mult).then_inc(sem("u_ready"), 1)
                pool.wait_ge(sem("u_ready"), HALVES * (L + 1))
                pool.wait_ge(sem("da_zeroed"), L + 1)
                for th in range(2):
                    g0 = (2 * L + th) * NST

                    def step(k, n):
                        pool.wait_ge(sem("b_rows"), g0 + n + 1)
                        if k is not None:
                            pool.wait_ge(sem("state_done"), g0 + n - 1)
                        nc.gpsimd.tensor_tensor(
                            tile(2 + (n if k is None else k) % 2).rearrange("p (m t) -> p m t", m=HALVES),
                            u[:, :, th * QTOK:(th + 1) * QTOK],
                            brow[(n if k is None else k) % 2].unsqueeze(1).to_broadcast([P, HALVES, QTOK]),
                            ALU.mult).then_inc(sem("mi_done"), 1)

                    if g0:
                        pool.wait_ge(sem("state_done"), g0)
                    step(None, 0)
                    step(None, 1)
                    with pool.Fori(1, NST // 2) as pair:
                        step(0, 2 * pair)
                        step(1, 2 * pair + 1)
            for k in (0, 1):
                pool.wait_ge(sem("slots_zeroed"), 32)
                for t in range(NBLK):
                    if t == 0:
                        pool.wait_ge(sem("indices_ready"), k + 1)
                    pool.wait_ge(sem("token_rows"), NCH * k + t // 4 + 1)
                    nc.gpsimd.indirect_dma_start(
                        out=slots_in[k], out_offset=bass.IndirectOffsetOnAxis(ap=IDX[:, 0, t:t + 1], axis=0),
                        in_=xtok[:, t, :], in_offset=None, bounds_check=SLOTS - 1, oob_is_err=False
                    ).then_inc(sem("scattered"), 16)
                pool.wait_ge(sem("rows_stored"), 16 * 2 * EXP * (k + 1))
                for t in range(NBLK):
                    nc.gpsimd.indirect_dma_start(
                        out=fetched[:, t, :], out_offset=None,
                        in_=slots_out[k], in_offset=bass.IndirectOffsetOnAxis(ap=IDX[:, 1, t:t + 1], axis=0),
                        bounds_check=SLOTS - 1, oob_is_err=False).then_inc(sem(f"fetched{t // 4}"), 16)

        @block.scalar
        def _(act):
            chain = [0]

            def link(ins):
                chain[0] += 1
                ins.then_inc(sem("act_chain"), 1)
                act.wait_ge(sem("act_chain"), chain[0])

            act.wait_ge(sem("eps_set"), 1)
            act.wait_ge(sem("small_loaded"), 16)
            a0 = SM["a_log"]
            nc.scalar.activation(flat(NEGA[:, :, :]), SMT[:, a0:a0 + LAYERS * HALVES * NST], ACT.Exp).then_inc(sem("a_exp"), 1)
            norm_act(act, 0)
            for L in range(LAYERS):
                norm_act(act, 1 + L)
                act.wait_ge(sem("pad_zeroed"), L + 1)
                if L == 0:
                    act.wait_ge(sem("slots_zeroed"), 32)
                    act.wait_ge(sem("sel_ready"), 1)
                for i in range(16):
                    m, c = divmod(i, NCH)
                    act.wait_ge(sem("inproj_ps"), 16 * L + i + 1)
                    dst = xpad[:, m, c, 3:3 + SEQ] if m < HALVES else ch(zs[:, m - HALVES, :], c)
                    nc.scalar.activation(dst, PS[:, i % 8, :], ACT.Copy if m < HALVES else ACT.Silu
                                         ).then_inc(sem("inproj_out"), 1)
                for m in range(HALVES):
                    act.wait_ge(sem("conv_done"), HALVES * L + m + 1)
                    nc.scalar.activation(xs[:, m, :], tile(3 + m), ACT.Silu).then_inc(sem("xs_ready"), 1)
                act.wait_ge(sem("xproj_ps"), NCH * (L + 1))
                nc.scalar.activation(drs[96:96 + DTR, :], flat(PS[96:96 + DTR, 0:4, :]), ACT.Copy).then_inc(sem("rank_ready"), 1)
                for m in range(HALVES):
                    q = HALVES * L + m
                    act.wait_ge(sem("dt_ps"), NCH * (q + 1))
                    if m or L:
                        act.wait_ge(sem("delta_ready"), q)
                    src = flat(PS[:, 4:8, :] if m == 0 else PS[:, 0:4, :])
                    nc.scalar.activation(tile(0), src, ACT.Identity, bias=small("dt_b", q)).then_inc(sem("dt_read"), 1)
                    link(nc.scalar.activation(tile(1), src, ACT.Abs, bias=small("dt_b", q)))
                    nc.scalar.activation(tile(2), tile(1), ACT.Exp, scale=-1.0).then_inc(sem("sp_e"), 1)
                    act.wait_ge(sem("sp_u"), q + 1)
                    link(nc.scalar.activation(tile(4), tile(3), ACT.Ln))
                    nc.scalar.activation(tile(5), tile(4), ACT.Exp, scale=-1.0).then_inc(sem("sp_r"), 1)
                act.wait_ge(sem("da_zeroed"), L + 1)
                act.wait_ge(sem("u_ready"), HALVES * (L + 1))
                for th in range(2):
                    g0 = (2 * L + th) * NST

                    def step(k, n):
                        par = (n if k is None else k) % 2
                        act.wait_ge(sem("b_ps"), g0 + n + 1)
                        if k is not None:
                            act.wait_ge(sem("mi_done"), g0 + n - 1)
                        nc.scalar.activation(brow[par], flat(PS[:, 0:2, :]), ACT.Copy).then_inc(sem("b_rows"), 1)
                        if k is not None:
                            act.wait_ge(sem("state_done"), g0 + n - 1)
                        for m in range(HALVES):
                            ins = nc.scalar.activation(
                                tile(par).rearrange("p (s t) -> p s t", t=SEQ)[:, 2 * m:2 * m + 2, 1:SEQ],
                                delta[:, m, th * QTOK:(th + 1) * QTOK].rearrange("p (s t) -> p s t", t=SEQ)[:, :, 1:SEQ],
                                ACT.Exp, scale=NEGA[:, HALVES * L + m, (n if k is None else bass.ds(n, 1))]
                                if k is not None else NEGA[:, HALVES * L + m, n:n + 1])
                        ins.then_inc(sem("decay_done"), 1)

                    if g0:
                        act.wait_ge(sem("mi_done"), g0)
                        act.wait_ge(sem("state_done"), g0)
                    step(None, 0)
                    step(None, 1)
                    with act.Fori(1, NST // 2) as pair:
                        step(0, 2 * pair)
                        step(1, 2 * pair + 1)

            def moe(k):
                norm_act(act, 3 if k == 0 else 6)
                act.wait_ge(sem("shifted"), k + 1)
                nc.scalar.activation(RT[:, 1, :], RT[:, 0, :], ACT.Exp).then_inc(sem("route_exp"), 1)
                for c in range(NCH):
                    act.wait_ge(sem("rows_ps"), NCH * k + c + 1)
                    nc.scalar.activation(flat(xtok[:, 4 * c:4 * c + 4, :]), PS[:, 4 + c, :], ACT.Copy
                                         ).then_inc(sem("token_rows"), 1)
                for e in range(EXP):
                    for j in range(FJ):
                        act.wait_ge(sem("hid_ps"), FJ * (EXP * k + e) + j + 1)
                        if e >= 2 and j == 0:
                            act.wait_ge(sem("rows_made"), NT * (EXP * k + e - 1))
                        nc.scalar.activation(hid[e % 2][:, j, :], PS[:, 2 + j, 0:CAP], ACT.Relu,
                                             bias=small("b1", FJ * e + j)).then_inc(sem("hidden"), 1)

            moe(0)
            norm_act(act, 4)
            act.wait_ge(sem("gla_loaded"), 32)
            act.wait_ge(sem("rank16_ps"), NCH)
            nc.scalar.activation(tile(5)[0:16, :], flat(PS[0:16, 0:4, :]), ACT.Copy).then_inc(sem("rank16"), 1)
            kr = HEADS * DK
            act.wait_ge(sem("kg_ps"), NCH)
            src = flat(PS[0:kr, 4:8, :])
            link(nc.scalar.activation(tile(0)[0:kr, :], src, ACT.Abs))
            link(nc.scalar.activation(tile(0)[0:kr, :], tile(0)[0:kr, :], ACT.Exp, scale=-1.0))
            nc.scalar.activation(tile(1)[0:kr, :], tile(0)[0:kr, :], ACT.Ln, bias=1.0).then_inc(sem("kg_log"), 1)
            act.wait_ge(sem("log_gate"), 1)
            nc.scalar.activation(tile(0)[0:kr, :], tile(2)[0:kr, :], ACT.Exp, scale=1.0 / 16).then_inc(sem("gla_decay"), 1)
            for c in range(NCH):
                act.wait_ge(sem("gate_ps"), c + 1)
                nc.scalar.activation(ch(xs[:, 0, :], c), PS[:, c, :], ACT.Silu, bias=small("bg")).then_inc(sem("gate_out"), 1)
            for i in range(2 * GT):
                act.wait_ge(sem("v_ps"), i + 1)
                nc.scalar.activation(zs[:, 0, (i % 2) * QTOK:(i % 2 + 1) * QTOK], flat(PS[:, 2:4, :]), ACT.Copy
                                     ).then_inc(sem("v_out"), 1)
                if i % GT == GT - 1:
                    th = i // GT
                    act.wait_ge(sem("o_ps"), th + 1)
                    nc.scalar.activation(tile(6)[:, th * QTOK:(th + 1) * QTOK], flat(PS[:, 6:8, :]), ACT.Copy
                                         ).then_inc(sem("o_copied"), 1)
            norm_act(act, 5)
            moe(1)

        @block.vector
        def _(dve):
            chain = [0]

            def link(ins):
                chain[0] += 1
                ins.then_inc(sem("dve_chain"), 1)
                dve.wait_ge(sem("dve_chain"), chain[0])

            dve.wait_ge(sem("a_exp"), 1)
            nc.vector.tensor_scalar(flat(NEGA[:, :, :]), flat(NEGA[:, :, :]), -1.0, None, ALU.mult).then_inc(sem("nega"), 1)
            norm_dve(dve, 0)
            for L in range(LAYERS):
                norm_dve(dve, 1 + L)
                dve.wait_ge(sem("pad_zeroed"), L + 1)
                for m in range(HALVES):
                    q = HALVES * L + m
                    dve.wait_ge(sem("inproj_out"), 16 * L + NCH * (m + 1))
                    acc = tile(3 + m).rearrange("p (b t) -> p b t", b=B)
                    for j in range(KCONV):
                        tap = xpad[:, m, :, j:j + SEQ]
                        w = small("conv_w", KCONV * q + j)
                        if j == 0:
                            link(nc.vector.tensor_scalar(acc, tap, w, small("conv_b", q), ALU.mult, ALU.add))
                        else:
                            ins = nc.vector.scalar_tensor_tensor(out=acc, in0=tap, scalar=w, in1=acc, op0=ALU.mult, op1=ALU.add)
                            if j < KCONV - 1:
                                link(ins)
                    ins.then_inc(sem("conv_done"), 1)
                dve.wait_ge(sem("xproj_ps"), NCH * (L + 1))
                bc = flat(PS[0:96, 0:4, :])
                mid = tile(5)[0:96, :].bitcast(BF16)[:, 0:TOK]
                link(nc.vector.tensor_copy(STK[0:96, :], bc))
                nc.vector.tensor_tensor(tile(6)[0:96, :], bc, STK[0:96, :], ALU.subtract).then_inc(sem("split_read"), 1)
                dve.wait_ge(sem("split_read"), L + 1)
                link(nc.vector.tensor_copy(mid, tile(6)[0:96, :]))
                nc.vector.tensor_copy(STK[32:64, :], mid[32:64, :])
                nc.vector.tensor_tensor(STK[64:96, :], tile(6)[64:96, :], mid[64:96, :], ALU.subtract).then_inc(sem("split_done"), 1)
                for m in range(HALVES):
                    q = HALVES * L + m
                    dve.wait_ge(sem("sp_e"), q + 1)
                    nc.vector.tensor_scalar(tile(3), tile(2), 1.0, None, ALU.add).then_inc(sem("sp_u"), 1)
                    dve.wait_ge(sem("sp_u"), q + 1)
                    link(nc.vector.scalar_tensor_tensor(out=tile(6), in0=tile(3), scalar=-1.0, in1=tile(2),
                                                        op0=ALU.add, op1=ALU.subtract))
                    dve.wait_ge(sem("sp_r"), q + 1)
                    link(nc.vector.tensor_tensor(tile(6), tile(6), tile(5), ALU.mult))
                    link(nc.vector.tensor_tensor(tile(6), tile(4), tile(6), ALU.subtract))
                    nc.vector.scalar_tensor_tensor(out=delta[:, m, :], in0=tile(0), scalar=0.0, in1=tile(6),
                                                   op0=ALU.max, op1=ALU.add).then_inc(sem("delta_ready"), 1)
                dve.wait_ge(sem("delta_ready"), HALVES * (L + 1))
                nc.vector.memset(T[:, 0:2 * TOK].rearrange("p (s t) -> p s t", t=SEQ)[:, :, 0:1], 0.0).then_inc(sem("da_zeroed"), 1)
                dve.wait_ge(sem("coef_ready"), 1)
                for th in range(2):
                    q = 2 * L + th
                    g0 = q * NST

                    def step(k, n):
                        par = (n if k is None else k) % 2
                        dve.wait_ge(sem("mi_done"), g0 + n + 1)
                        nc.vector.tensor_tensor_scan(tile(2 + par), COEF[:, :], tile(2 + par), 0.0, ALU.mult, ALU.add
                                                     ).then_inc(sem("momentum_done"), 1)
                        dve.wait_ge(sem("decay_done"), g0 + n + 1)
                        dve.wait_ge(sem("momentum_done"), g0 + n + 1)
                        nc.vector.tensor_tensor_scan(tile(4), tile(par), tile(2 + par), 0.0, ALU.mult, ALU.add
                                                     ).then_inc(sem("state_done"), 1)
                        dve.wait_ge(sem("c_ps"), g0 + n + 1)
                        if k is not None:
                            dve.wait_ge(sem("y_summed"), g0 + n - 1)
                        dve.wait_ge(sem("state_done"), g0 + n + 1)
                        nc.vector.tensor_tensor(tile(5 + par).rearrange("p (m t) -> p m t", m=HALVES),
                                                tile(4).rearrange("p (m t) -> p m t", m=HALVES),
                                                flat(PS[:, 2:4, :]).unsqueeze(1).to_broadcast([P, HALVES, QTOK]),
                                                ALU.mult).then_inc(sem("readout"), 1)

                    if g0:
                        dve.wait_ge(sem("y_summed"), g0)
                    step(None, 0)
                    step(None, 1)
                    with dve.Fori(1, NST // 2) as pair:
                        step(0, 2 * pair)
                        step(1, 2 * pair + 1)
                    dve.wait_ge(sem("y_summed"), g0 + NST)
                    for m in range(HALVES):
                        h = HALVES * L + m
                        part = slice(th * QTOK, (th + 1) * QTOK)
                        yt = tile(4)[:, m * QTOK:(m + 1) * QTOK]
                        link(nc.vector.scalar_tensor_tensor(out=yt, in0=xs[:, m, part], scalar=small("dp", h),
                                                            in1=flat(PS[:, 4 + 2 * m:6 + 2 * m, :]), op0=ALU.mult, op1=ALU.add))
                        nc.vector.tensor_tensor(yt, yt, zs[:, m, part], ALU.mult).then_inc(sem("gated"), 1)
                    dve.wait_ge(sem("outproj_ps"), q + 1)
                    xp = X[:, th * QTOK:(th + 1) * QTOK]
                    nc.vector.tensor_tensor(xp, xp, flat(PS[:, 0:2, :]), ALU.add).then_inc(sem("outproj_added"), 1)
            dve.wait_ge(sem("x_again"), 16)
            dve.wait_ge(sem("outproj_added"), 2 * LAYERS)
            nc.vector.tensor_tensor(X[:, :], X[:, :], XN[:, :], ALU.add).then_inc(sem("stream_added"), 1)

            def by_block(ap):
                return ap.rearrange("p (b e) -> p b e", e=EXP)

            def over(ap):
                return ap.unsqueeze(2).to_broadcast([P, NBLK, EXP])

            def moe(k):
                norm_dve(dve, 3 if k == 0 else 6)
                R = [RT[:, i, :] for i in range(10)]
                S = [RTS[:, i, :] for i in range(8)]
                dve.wait_ge(sem("logits_ps"), k + 1)
                lg = PS[:, 0, 0:P]
                link(nc.vector.tensor_reduce(S[0], by_block(lg), AX.X, ALU.max))
                nc.vector.tensor_tensor(by_block(R[0]), by_block(lg), over(S[0]), ALU.subtract).then_inc(sem("shifted"), 1)
                dve.wait_ge(sem("shifted"), k + 1)
                link(nc.vector.scalar_tensor_tensor(out=R[2], in0=R[0], scalar=0.0, in1=CST[:, C_RAMP, :],
                                                    op0=ALU.is_equal, op1=ALU.mult))
                link(nc.vector.tensor_reduce(S[1], by_block(R[2]), AX.X, ALU.max))
                nc.vector.tensor_tensor(by_block(R[3]), by_block(R[2]), over(S[1]), ALU.is_equal).then_inc(sem("chosen"), 1)
                dve.wait_ge(sem("route_exp"), k + 1)
                link(nc.vector.tensor_reduce(S[2], by_block(R[1]), AX.X, ALU.add))
                link(nc.vector.reciprocal(S[3], S[2]))
                dve.wait_ge(sem("counts_ps"), k + 1)
                tot = by_block(PS[:, 2, 0:P]).rearrange("p b e -> p e b")
                link(nc.vector.tensor_copy(R[4].rearrange("p (e b) -> p e b", b=NBLK), tot))
                link(nc.vector.memset(R[5], 1.0))
                link(nc.vector.memset(R[5].rearrange("p (e b) -> p e b", b=NBLK)[:, :, 0:1], 0.0))
                link(nc.vector.tensor_tensor_scan(R[6], R[5], R[4], 0.0, ALU.mult, ALU.add))
                link(nc.vector.tensor_tensor(R[6], R[6], R[4], ALU.subtract))
                link(nc.vector.tensor_tensor(by_block(R[7]), by_block(PS[:, 1, 0:P]),
                                             R[6].rearrange("p (e b) -> p b e", b=NBLK), ALU.add))
                link(nc.vector.scalar_tensor_tensor(out=R[8], in0=R[7], scalar=float(CAP), in1=R[3],
                                                    op0=ALU.is_le, op1=ALU.mult))
                link(nc.vector.tensor_tensor(R[7], R[7], CST[:, C_EBASE, :], ALU.add))
                link(nc.vector.tensor_tensor(R[7], R[7], R[8], ALU.mult))
                link(nc.vector.tensor_reduce(S[4], by_block(R[7]), AX.X, ALU.add))
                link(nc.vector.tensor_reduce(S[5], by_block(R[8]), AX.X, ALU.add))
                link(nc.vector.tensor_copy(IDX[:, 1, :], S[4]))
                link(nc.vector.tensor_scalar(S[6], S[5], -FAR, FAR, ALU.mult, ALU.add))
                link(nc.vector.tensor_tensor(S[6], S[6], S[4], ALU.add))
                nc.vector.tensor_copy(IDX[:, 0, :], S[6]).then_inc(sem("indices_ready"), 1)
                link(nc.vector.tensor_tensor(S[7], S[3], S[5], ALU.mult))
                for t in range(NBLK):
                    nc.vector.tensor_scalar(diag[:, t, :], ident, S[7][:, t:t + 1], None, ALU.mult).then_inc(sem("diagonals"), 1)
                for e in range(EXP):
                    dve.wait_ge(sem("disp_ps"), EXP * k + e + 1)
                    nc.vector.tensor_copy(xdisp[:, e * CAP:(e + 1) * CAP], PS[:, e % 2, 0:CAP]).then_inc(sem("dispatched"), 1)
                    if e >= 1:
                        made(k, e - 1)
                made(k, EXP - 1)
                for c in range(NCH):
                    dve.wait_ge(sem("moe_ps"), NCH * k + c + 1)
                    nc.vector.tensor_tensor(ch(X[:, :], c), ch(X[:, :], c), PS[:, 2 + c, :], ALU.add).then_inc(sem("moe_added"), 1)

            def made(k, e):
                if k == 0 and e == 0:
                    dve.wait_ge(sem("b2_loaded"), 16)
                dve.wait_ge(sem("rows2_ps"), EXP * k + e + 1)
                for i, (_, n) in enumerate(TILES):
                    nc.vector.tensor_tensor(rows_out[0:n, NT * e + i, :], PS[0:n, 6 + e % 2, i * P:(i + 1) * P],
                                            B2R[0:n, e, :], ALU.add).then_inc(sem("rows_made"), 1)

            moe(0)
            norm_dve(dve, 4)
            kr = HEADS * DK
            dve.wait_ge(sem("kg_log"), 1)
            nc.vector.scalar_tensor_tensor(out=tile(2)[0:kr, :], in0=flat(PS[0:kr, 4:8, :]), scalar=0.0,
                                           in1=tile(1)[0:kr, :], op0=ALU.min, op1=ALU.subtract).then_inc(sem("log_gate"), 1)
            dve.wait_ge(sem("gla_decay"), 1)
            nc.vector.memset(tile(0)[0:kr, :].rearrange("p (s t) -> p s t", t=SEQ)[:, :, 0:1], 0.0).then_inc(sem("gla_decay0"), 1)
            for i in range(2 * GT):
                vt = zs[:, 0, (i % 2) * QTOK:(i % 2 + 1) * QTOK]
                kv = tile(1)[:, 0:QTOK]
                st = tile(1)[:, QTOK:TOK]
                out = tile(2)[:, (i % 2) * QTOK:(i % 2 + 1) * QTOK]
                dve.wait_ge(sem("v_out"), i + 1)
                dve.wait_ge(sem("k_ps"), i + 1)
                nc.vector.scalar_tensor_tensor(out=kv, in0=flat(PS[:, 0:2, :]), scalar=DK ** -0.5, in1=vt,
                                               op0=ALU.mult, op1=ALU.mult).then_inc(sem("kv_done"), 1)
                dve.wait_ge(sem("decay_ps"), i + 1)
                dve.wait_ge(sem("kv_done"), i + 1)
                nc.vector.tensor_tensor_scan(st, flat(PS[:, 4:6, :]), kv, 0.0, ALU.mult, ALU.add).then_inc(sem("gla_state"), 1)
                dve.wait_ge(sem("q_ps"), i + 1)
                dve.wait_ge(sem("gla_state"), i + 1)
                if i >= 2:
                    dve.wait_ge(sem("o_part"), i - 1)
                nc.vector.tensor_tensor(out, st, flat(PS[:, 0:2, :]), ALU.mult).then_inc(sem("qs_done"), 1)
            norm_dve(dve, 5)
            dve.wait_ge(sem("gate_out"), NCH)
            dve.wait_ge(sem("norm_out"), norm_done(5))
            for c in range(NCH):
                nc.vector.tensor_tensor(ch(xs[:, 1, :], c), ch(tile(6), c), ch(xs[:, 0, :], c), ALU.mult).then_inc(sem("o_gated"), 1)
            for c in range(NCH):
                dve.wait_ge(sem("attn_ps"), c + 1)
                nc.vector.tensor_tensor(ch(X[:, :], c), ch(X[:, :], c), PS[:, c, :], ALU.add).then_inc(sem("attn_added"), 1)
            moe(1)

        @block.tensor
        def _(pe):
            def mm(out, lhsT, rhs, start=True, stop=True):
                return nc.tensor.matmul(out, lhsT, rhs, start=start, stop=stop)

            pe.wait_ge(sem("consts_loaded"), 16)
            norm_pe(pe, 0)
            for L in range(LAYERS):
                norm_pe(pe, 1 + L)
                if L == 0:
                    pe.wait_ge(sem("mamba_loaded"), 64)
                pe.wait_ge(sem("norm_out"), norm_done(1 + L))
                for i in range(16):
                    m, c = divmod(i, NCH)
                    if i >= 8:
                        pe.wait_ge(sem("inproj_out"), 16 * L + i - 7)
                    mm(PS[:, i % 8, :], WIN[:, L, m * P:(m + 1) * P], ch(XN[:, :], c)).then_inc(sem("inproj_ps"), 1)
                pe.wait_ge(sem("inproj_out"), 16 * (L + 1))
                pe.wait_ge(sem("xs_ready"), HALVES * (L + 1))
                for c in range(NCH):
                    for m in range(HALVES):
                        ins = mm(PS[0:XW, c, :], XPW[:, L, m, :], ch(xs[:, m, :], c), m == 0, m == HALVES - 1)
                    ins.then_inc(sem("xproj_ps"), 1)
                pe.wait_ge(sem("rank_ready"), L + 1)
                for m in range(HALVES):
                    if m == 1:
                        pe.wait_ge(sem("split_read"), L + 1)
                    for c in range(NCH):
                        mm(PS[:, (4 if m == 0 else 0) + c, :], DTW[96:96 + DTR, L, m * P:(m + 1) * P],
                           ch(drs[96:96 + DTR, :], c)).then_inc(sem("dt_ps"), 1)
                pe.wait_ge(sem("split_done"), L + 1)
                pe.wait_ge(sem("sel_ready"), 1)
                pe.wait_ge(sem("delta_ready"), HALVES * (L + 1))
                for th in range(2):
                    q = 2 * L + th
                    g0 = q * NST

                    def row(bank, n, base):
                        for j in range(2):
                            sel = SEL[0:96, base + n, :] if isinstance(n, int) else flat(SEL[0:96, bass.ds(n + base, 1), :])
                            ins = mm(PS[:, bank + j, :], sel, STK[0:96, th * QTOK + j * CH:th * QTOK + (j + 1) * CH])
                        return ins

                    def b_row(n):
                        pe.wait_ge(sem("b_rows"), g0 + n)
                        row(0, n, 0).then_inc(sem("b_ps"), 1)

                    def c_row(n):
                        pe.wait_ge(sem("readout"), g0 + n)
                        row(2, n, NST).then_inc(sem("c_ps"), 1)

                    def sum_y(n, par, first=False, last=False):
                        pe.wait_ge(sem("readout"), g0 + n + 1)
                        for j in range(4):
                            ins = nc.tensor.matmul(PS[:, 4 + j, :], ident, ch(tile(5 + par), j), start=first, stop=last,
                                                   skip_group_check=True)
                        ins.then_inc(sem("y_summed"), 1)

                    if q:
                        pe.wait_ge(sem("outproj_added"), q)
                    b_row(0)
                    b_row(1)
                    c_row(0)
                    for n in (0, 1):
                        b_row(n + 2)
                        c_row(n + 1)
                        sum_y(n, n, first=n == 0)
                    with pe.Fori(1, NST // 2 - 1) as pair:
                        for k in (0, 1):
                            b_row(2 * pair + k + 2)
                            c_row(2 * pair + k + 1)
                            sum_y(2 * pair + k, k)
                    c_row(NST - 1)
                    sum_y(NST - 2, 0)
                    sum_y(NST - 1, 1, last=True)
                    pe.wait_ge(sem("b_rows"), g0 + NST)
                    for m in range(HALVES):
                        pe.wait_ge(sem("gated"), HALVES * q + m + 1)
                        for j in range(2):
                            ins = nc.tensor.matmul(PS[:, j, :], WOUT[:, L, m, :],
                                                   tile(4)[:, m * QTOK + j * CH:m * QTOK + (j + 1) * CH],
                                                   start=m == 0, stop=m == HALVES - 1)
                    ins.then_inc(sem("outproj_ps"), 1)

            def moe(k):
                norm_pe(pe, 3 if k == 0 else 6)
                pe.wait_ge(sem("norm_out"), norm_done(3 if k == 0 else 6))
                for t in range(NBLK):
                    ins = mm(PS[:, 0, EXP * t:EXP * (t + 1)], XN[:, t * P:(t + 1) * P],
                             SMT[:, SM["gate"]:SM["gate"] + EXP])
                ins.then_inc(sem("logits_ps"), 1)
                for c in range(NCH):
                    for t in range(4):
                        ins = nc.tensor.transpose(PS[:, 4 + c, t * P:(t + 1) * P],
                                                  XN[:, (4 * c + t) * P:(4 * c + t + 1) * P], ident)
                    ins.then_inc(sem("rows_ps"), 1)
                pe.wait_ge(sem("chosen"), k + 1)
                mm(PS[:, 1, 0:P], CST[:, C_TRI, :], RT[:, 3, :])
                mm(PS[:, 2, 0:P], CST[:, C_ONE, :], RT[:, 3, :]).then_inc(sem("counts_ps"), 1)
                pe.wait_ge(sem("indices_ready"), k + 1)
                pe.wait_ge(sem("token_rows"), NCH * (k + 1))
                if k == 0:
                    pe.wait_ge(sem("experts_loaded"), 32)

                def gather(e):
                    pe.wait_ge(sem(f"rows_loaded{e}"), 32 * (k + 1))
                    if e >= 2:
                        pe.wait_ge(sem("dispatched"), EXP * k + e - 1)
                    for i, (a, n) in enumerate(TILES):
                        ins = nc.tensor.transpose(PS[:, e % 2, a:a + n], rows_in[0:n, NT * e + i, :], ident[0:n, 0:n])
                    ins.then_inc(sem("disp_ps"), 1)

                gather(0)
                for e in range(EXP):
                    if e + 1 < EXP:
                        gather(e + 1)
                    pe.wait_ge(sem("dispatched"), EXP * k + e + 1)
                    for j in range(FJ):
                        if e:
                            pe.wait_ge(sem("hidden"), FJ * (EXP * k + e - 1) + j + 1)
                        mm(PS[:, 2 + j, 0:CAP], W1[:, e, j * P:(j + 1) * P], xdisp[:, e * CAP:(e + 1) * CAP]
                           ).then_inc(sem("hid_ps"), 1)
                    pe.wait_ge(sem("hidden"), FJ * (EXP * k + e + 1))
                    if e >= 2:
                        pe.wait_ge(sem("rows_made"), NT * (EXP * k + e - 1))
                    for i, (a, n) in enumerate(TILES):
                        for j in range(FJ):
                            ins = mm(PS[0:n, 6 + e % 2, i * P:(i + 1) * P], hid[e % 2][:, j, a:a + n], W2[:, e, j, :],
                                     j == 0, j == FJ - 1)
                    ins.then_inc(sem("rows2_ps"), 1)
                for c in range(NCH):
                    pe.wait_ge(sem(f"fetched{c}"), 64 * (k + 1))
                    pe.wait_ge(sem("diagonals"), NBLK * k + 4 * c + 4)
                    for t in range(4):
                        ins = mm(PS[:, 2 + c, t * P:(t + 1) * P], fetched[:, 4 * c + t, :], diag[:, 4 * c + t, :])
                    ins.then_inc(sem("moe_ps"), 1)

            moe(0)
            norm_pe(pe, 4)
            pe.wait_ge(sem("gla_loaded"), 32)
            pe.wait_ge(sem("norm_out"), norm_done(4))
            for c in range(NCH):
                mm(PS[0:16, c, :], GW[:, GG1:GG1 + 16], ch(XN[:, :], c)).then_inc(sem("rank16_ps"), 1)
            pe.wait_ge(sem("rank16"), 1)
            for c in range(NCH):
                mm(PS[0:HEADS * DK, 4 + c, :], WG2[0:16, :], ch(tile(5)[0:16, :], c)).then_inc(sem("kg_ps"), 1)
            for c in range(NCH):
                mm(PS[:, c, :], GW[:, GG:GG + P], ch(XN[:, :], c)).then_inc(sem("gate_ps"), 1)
            pe.wait_ge(sem("gate_out"), NCH)
            pe.wait_ge(sem("gla_decay0"), 1)

            def part(i, bank, w0):
                th, g = divmod(i, GT)
                for j in range(2):
                    a = th * QTOK + j * CH
                    ins = mm(PS[:, bank + j, :], GW[:, w0 + g * P:w0 + (g + 1) * P], XN[:, a:a + CH])
                return ins

            def read_out(i):
                th, g = divmod(i, GT)
                pe.wait_ge(sem("qs_done"), i + 1)
                if i == GT:
                    pe.wait_ge(sem("o_copied"), 1)
                for j in range(2):
                    ins = nc.tensor.matmul(PS[:, 6 + j, :], RED[:, g, :],
                                           tile(2)[:, (i % 2) * QTOK + j * CH:(i % 2) * QTOK + (j + 1) * CH],
                                           start=g == 0, stop=g == GT - 1)
                ins.then_inc(sem("o_part"), 1)
                if g == GT - 1:
                    pe.wait_ge(sem("o_part"), i + 1)
                    nc.tensor.matmul(PS[:, 5, 0:2], ident, ident[:, 0:2], start=True, stop=True).then_inc(sem("o_ps"), 1)

            for i in range(2 * GT):
                th, g = divmod(i, GT)
                if i >= 1:
                    pe.wait_ge(sem("v_out"), i)
                part(i, 2, GV).then_inc(sem("v_ps"), 1)
                if i >= 1:
                    pe.wait_ge(sem("qs_done"), i)
                part(i, 0, GK).then_inc(sem("k_ps"), 1)
                for j in range(2):
                    a = th * QTOK + j * CH
                    ins = mm(PS[:, 4 + j, :], SPR[0:HEADS * DK, g, :], tile(0)[0:HEADS * DK, a:a + CH])
                ins.then_inc(sem("decay_ps"), 1)
                pe.wait_ge(sem("kv_done"), i + 1)
                part(i, 0, GQ).then_inc(sem("q_ps"), 1)
                read_out(i)
            norm_pe(pe, 5)
            for c in range(NCH):
                pe.wait_ge(sem("o_gated"), c + 1)
                mm(PS[:, c, :], GW[:, GO:GO + P], ch(xs[:, 1, :], c)).then_inc(sem("attn_ps"), 1)
            moe(1)


_SHAPES = {
    "x": (P, TOK), "consts": (P, NCONST, P), "small": (P, SMALL), "w_in": (P, LAYERS, 4 * P),
    "w_x": (P, LAYERS, HALVES, XW), "w_dt": (DTR, LAYERS, HALVES * P), "w_out": (P, LAYERS, HALVES, P),
    "sel": (96, 2 * NST * P), "w1": (P, EXP, DFF), "w2": (P, EXP, FJ, P), "b2": (P, EXP * P),
    "w_gla": (P, GEND), "gla_consts": (P, 2 * GT * P + HEADS * DK),
}


def _constants():
    i = np.arange(P)
    c = np.zeros((P, NCONST, P), np.float32)
    c[:, C_ID] = np.eye(P)
    c[:, C_AVG] = 1.0 / D
    c[:, C_AVG8] = (i[:, None] // DV == i[None] // DV) / DV
    c[:, C_TRI] = i[:, None] <= i[None]
    c[:, C_ONE] = 1.0
    c[:, C_RAMP] = EXP - i % EXP
    c[:, C_EBASE] = (i % EXP) * CAP - 1
    k, r = np.arange(96), np.arange(2 * NST)
    sel = np.repeat((k[:, None] % 32 == r[None]).astype(np.float32)[:, :, None], P, 2).reshape(96, -1)
    g, row = np.arange(GT), np.arange(P)
    head = g[:, None] * (P // (DK * DV)) + row[None] // (DK * DV)
    dk, dv = row // DV % DK, row % DV
    red = (head[:, :, None] * DV + dv[None, :, None] == i).astype(np.float32)
    spr = (head[:, None, :] * DK + dk[None, None, :] == i[None, :, None]).astype(np.float32)
    return c, sel, red.transpose(1, 0, 2).reshape(P, -1), spr.transpose(1, 0, 2).reshape(P, -1)


def kernel(**inputs):
    import concourse.bacc as bacc
    from concourse.bass_utils import run_bass_kernel_spmd

    a = {k: np.asarray(v) for k, v in inputs.items()}
    ma = {k[len("L0_attn_a_"):]: v for k, v in a.items() if k.startswith("L0_attn_a_")}
    at = {k[len("L0_attn_b_"):]: v for k, v in a.items() if k.startswith("L0_attn_b_")}
    ff = {k[len("L0_ffn_"):]: v for k, v in a.items() if k.startswith("L0_ffn_")}
    consts, sel, red, spr = _constants()

    def halves(v):
        v = v.reshape(LAYERS, HALVES, P, -1)
        return v.transpose(2, 0, 1, 3).reshape(P, -1)

    small = np.concatenate([
        halves(ma["conv_w"]), halves(ma["conv_b"]), halves(ma["dt_b"]), halves(ma["Dp"]), ma["norm_w"].T,
        halves(ma["A_log"]), ff["b1"].reshape(EXP, FJ, P).transpose(2, 0, 1).reshape(P, -1),
        at["bg"].reshape(P, 1), ff["gate_w"].T], 1)
    xp = ma["x_proj_w"]
    bc = xp[:, DTR:]
    xw = np.concatenate([bc, bc, bc, xp[:, :DTR]], 1)
    rep_k = np.repeat(np.arange(HEADS * DK), DV)
    rep_v = (np.arange(HEADS)[:, None, None] * DV + np.zeros((1, DK, 1), int) + np.arange(DV)).reshape(-1)
    wg2 = np.zeros((P, HEADS * DK), np.float32)
    wg2[0:16] = at["Wg2"]
    arrays = {
        "x": ma["x"].reshape(TOK, D).T,
        "consts": consts,
        "small": small,
        "w_in": ma["in_proj_w"].transpose(2, 0, 1),
        "w_x": xw.reshape(LAYERS, XW, HALVES, P).transpose(3, 0, 2, 1),
        "w_dt": ma["dt_w"].transpose(2, 0, 1),
        "w_out": ma["out_w"].reshape(LAYERS, P, HALVES, P).transpose(3, 0, 2, 1),
        "sel": sel,
        "w1": ff["w1"].transpose(1, 0, 2),
        "w2": ff["w2"].reshape(EXP, FJ, P, D).transpose(2, 0, 1, 3),
        "b2": np.repeat(ff["b2"].reshape(1, -1), P, 0),
        "w_gla": np.concatenate([at["Wq"][:, rep_k], at["Wk"][:, rep_k], at["Wv"][:, rep_v], at["Wg"], at["Wo"], at["Wg1"]], 1),
        "gla_consts": np.concatenate([red, spr, wg2], 1),
    }
    nc = bacc.Bacc("TRN2", target_bir_lowering=False, num_devices=1)
    io, host = {}, {}
    for name, shape in _SHAPES.items():
        host[f"in_{name}"] = np.ascontiguousarray(arrays[name])
        assert host[f"in_{name}"].shape == shape, (name, host[f"in_{name}"].shape, shape)
        io[name] = nc.dram_tensor(f"in_{name}", shape, F32, kind="ExternalInput").ap()
    io["out"] = nc.dram_tensor("out_x", (P, TOK), F32, kind="ExternalOutput").ap()
    build(nc, io)
    r = run_bass_kernel_spmd(nc, [host], core_ids=[0])
    return np.ascontiguousarray(r.results[0]["out_x"].T).reshape(B, SEQ, D)
```

```python
from contextlib import ExitStack

import numpy as np

import concourse.bass as bass
from concourse import mybir

P = 128
D = 128
B, SEQ = 4, 512
TOK = B * SEQ
NCH = 4
CH = TOK // NCH
LAYERS = 2
HALVES = 2
NST = 16
DTR = 8
KCONV = 4
BETA = 0.6
QTOK = 1024
SPAN = 64
UNITS = TOK // SPAN
UPB = SEQ // SPAN
GRP = 4
EXP, DFF, CAP = 8, 512, 320
SLOTS = EXP * CAP
NBLK = TOK // P
ST = SLOTS // P
GS = 4
NT = 3
FJ = DFF // P
HEADS, DK, DV = 16, 4, 8
GT = HEADS * DK * DV // P
EPS = 1e-5
FAR = 4096.0

F32 = mybir.dt.float32
BF16 = mybir.dt.bfloat16
U32 = mybir.dt.uint32
ALU = mybir.AluOpType
ACT = mybir.ActivationFunctionType
AX = mybir.AxisListType

SM = {}
_at = 0
for _name, _n in (("conv_w", LAYERS * HALVES * KCONV), ("conv_b", LAYERS * HALVES), ("dt_b", LAYERS * HALVES),
                  ("dp", LAYERS * HALVES), ("norm_w", LAYERS), ("a_log", LAYERS * HALVES * NST),
                  ("b1", EXP * FJ), ("bg", 1), ("gate", EXP)):
    SM[_name] = _at
    _at += _n
SMALL = _at
C_ID, C_AVG, C_AVG8, C_TRI, C_ONE, C_RAMP, C_EBASE, C_MASK, C_IOTA = range(9)
NCONST = 9
XW = 3 * 2 * NST + DTR
GQ, GK, GV, GG, GO, GG1, GEND = 0, 512, 1024, 1536, 1664, 1792, 1808
NORMS = [(True, None), (False, 0), (False, 1), (True, None), (True, None), (True, None), (True, None)]


def pieces(e):
    a = e * CAP
    out = []
    while a < (e + 1) * CAP:
        n = min(P - a % P, (e + 1) * CAP - a)
        out.append((a // P, a % P, n, a - e * CAP))
        a += n
    return out


def centred_before(k):
    return sum(c for c, _ in NORMS[:k])


def build(nc, io):
    with ExitStack() as ctx:
        def sb(name, shape, dt=F32):
            return ctx.enter_context(nc.sbuf_tensor(name, shape, dt))

        sems = {}

        def sem(name):
            if name not in sems:
                sems[name] = ctx.enter_context(nc.semaphore(name))
            return sems[name]

        X = sb("X", [P, TOK])
        F = sb("F", [P, 8 * TOK])
        BIG = sb("BIG", [P, 12 * TOK])
        STK = sb("STK", [P, TOK], BF16)
        SEL = sb("SEL", [P, NST, P], BF16)
        AUX = sb("AUX", [P, TOK])
        WIN = sb("WIN", [P, LAYERS, 4 * P])
        XPW = sb("XPW", [P, LAYERS, HALVES, XW])
        DTW = sb("DTW", [P, LAYERS, HALVES * P])
        WOUT = sb("WOUT", [P, LAYERS, HALVES, P])
        SMT = sb("SMT", [P, SMALL])
        CST = sb("CST", [P, NCONST, P])
        NEGA = sb("NEGA", [P, LAYERS * HALVES, NST])
        RTS = sb("RTS", [P, 8, NBLK])
        IDX = sb("IDX", [P, ST], U32)
        A0 = sb("A0", [P, HALVES * NST * (UNITS + 1)])
        PS = ctx.enter_context(nc.psum_tensor("PS", [P, 8, CH], F32))

        ident = CST[:, C_ID, :]
        avg_all = CST[:, C_AVG, :]

        W1 = BIG[:, 0:2 * TOK].rearrange("p (e f) -> p e f", e=EXP)
        W2 = BIG[:, 2 * TOK:4 * TOK].rearrange("p (e j d) -> p e j d", e=EXP, j=FJ)
        RT = AUX[:, 0:10 * P].rearrange("p (i d) -> p i d", d=P)

        def tile(k):
            return BIG[:, (4 + k) * TOK:(5 + k) * TOK]

        XN = tile(7)

        def small(name, k=0):
            return SMT[:, SM[name] + k:SM[name] + k + 1]

        def ch(ap, c):
            return ap[:, c * CH:(c + 1) * CH]

        def flat(ap):
            return ap.rearrange("p a b -> p (a b)")

        xs = F[:, 0:2 * TOK].rearrange("p (m t) -> p m t", m=HALVES)
        zs = F[:, 2 * TOK:4 * TOK].rearrange("p (m t) -> p m t", m=HALVES)
        delta = F[:, 4 * TOK:6 * TOK].rearrange("p (m t) -> p m t", m=HALVES)
        u = F[:, 6 * TOK:8 * TOK].rearrange("p (m t) -> p m t", m=HALVES)
        Y = u
        def slot(par, k):
            return BIG[:, (9 * par + k) * 1024:(9 * par + k + 1) * 1024].rearrange("p (m t) -> p m t", m=HALVES)

        def xpad(par):
            return BIG[:, (9 * par + 7) * 1024:(9 * par + 7) * 1024 + HALVES * (SEQ + 3)].rearrange(
                "p (m t) -> p m t", m=HALVES)

        def split_rest(par):
            return slot(par, 6)[0:96, 0, :]

        def split_mid(par):
            return slot(par, 5)[0:96, 0, :].bitcast(BF16)[:, 0:CH]

        def rank(par):
            return slot(par, 6)[:, 1, :]

        dec = [BIG[:, g * 8192:(g + 1) * 8192].rearrange("p (m j n t) -> p m j n t", m=HALVES, j=GRP, n=NST) for g in (0, 1)]
        state = BIG[:, 16384:18432].rearrange("p (m n t) -> p m n t", m=HALVES, n=NST)
        prod = [BIG[:, 18432 + k * 2048:20480 + k * 2048].rearrange("p (m n t) -> p m n t", m=HALVES, n=NST) for k in (0, 1)]
        rbm = [BIG[0:SPAN + NST, 22528 + k * 1024:23552 + k * 1024] for k in (0, 1)]
        ut = [AUX[0:SPAN + NST, k * 256:(k + 1) * 256] for k in (0, 1)]
        us = [AUX[:, 512 + k * 128:640 + k * 128].rearrange("p (m t) -> p m t", m=HALVES) for k in (0, 1)]
        bt = AUX[0:SPAN, 768:768 + UNITS * NST].rearrange("p (i n) -> p i n", n=NST)
        carry = AUX[:, 1280:1312].rearrange("p (m n) -> p m n", m=HALVES)
        zero_w = AUX[0:SPAN + NST, 1312:1328]
        one_e = BIG[:, 9216:13312].rearrange("p (m t) -> p m t", m=HALVES)
        above = BIG[:, 18432:22528].rearrange("p (m t) -> p m t", m=HALVES)
        a0 = A0[:, :].rearrange("p (m n i) -> p m n i", m=HALVES, n=NST)
        rows_in = F[:, 0:SLOTS].rearrange("p (k d) -> p k d", d=P)
        rows_out = F[:, 3072:3072 + SLOTS].rearrange("p (k d) -> p k d", d=P)
        xdisp = F[:, 6144:6144 + SLOTS]
        hid = [F[:, 8704 + k * FJ * CAP:8704 + (k + 1) * FJ * CAP].rearrange("p (j s) -> p j s", j=FJ) for k in (0, 1)]
        xtok = F[:, 11264:11264 + TOK].rearrange("p (k d) -> p k d", d=P)
        fetched = F[:, 13312:13312 + TOK].rearrange("p (k d) -> p k d", d=P)
        diag = tile(3).rearrange("p (k d) -> p k d", d=P)
        row_hot = tile(0).rearrange("p (k d) -> p k d", d=P)
        passed = RT[:, 0:3, :].rearrange("p a b -> p (a b)")[:, 0:NBLK * (ST + 1)].rearrange("p (b h) -> p b h", h=ST + 1)
        tile_hot = RT[:, 3:6, :].rearrange("p a b -> p (a b)")[:, 0:NBLK * ST].rearrange("p (b h) -> p b h", h=ST)
        B2R = STK[:, :].bitcast(F32).rearrange("p (e d) -> p e d", e=EXP)
        GC = F[:, 8192:8192 + 2 * GT * P + HEADS * DK]
        GW = F[:, 9472:9472 + GEND]
        RED = GC[:, 0:GT * P].rearrange("p (g m) -> p g m", g=GT)
        SPR = GC[:, GT * P:2 * GT * P].rearrange("p (g m) -> p g m", g=GT)
        WG2 = GC[:, 2 * GT * P:2 * GT * P + HEADS * DK]

        token_dram = [nc.dram_tensor(f"tokens{k}", (TOK, D), F32, kind="Internal").ap() for k in (0, 1)]
        result_dram = [nc.dram_tensor(f"results{k}", (TOK, D), F32, kind="Internal").ap() for k in (0, 1)]

        def norm_input(k, c):
            if k == 0:
                return [(sem("x_loaded"), 16)]
            if k == 1:
                return [(sem("norm_out"), c + 1)]
            if k == 2:
                return [(sem("outproj_added"), c + 1)]
            if k == 3:
                return [(sem("stream_added"), 1)]
            if k == 4:
                return [(sem("moe_added"), c + 1)]
            if k == 5:
                return [(sem("o_copied"), c // 2 + 1)]
            return [(sem("attn_added"), c + 1)]

        def norm_buffers(k):
            src = tile(6) if k == 5 else X[:, :]
            dst = X[:, :] if k == 0 else (tile(6) if k == 5 else XN[:, :])
            t = 4 if k in (1, 2) else 3
            return src, dst, tile(t), tile(t + 1), tile(t + 2)

        def norm_pe(pe, k):
            src, _, _, sq, _ = norm_buffers(k)
            avg = CST[:, C_AVG8, :] if k == 5 else avg_all
            if NORMS[k][0]:
                for c in range(NCH):
                    for s, v in norm_input(k, c):
                        pe.wait_ge(s, v)
                    pe.matmul(PS[:, c, :], avg, ch(src, c), start=True, stop=True).then_inc(sem("mean_ps"), 1)
            for c in range(NCH):
                pe.wait_ge(sem("squared"), NCH * k + c + 1)
                pe.matmul(PS[:, 4 + c, :], avg, ch(sq, c), start=True, stop=True).then_inc(sem("var_ps"), 1)

        def norm_act(act, k):
            src, _, xc, sq, rs = norm_buffers(k)
            for c in range(NCH):
                if NORMS[k][0]:
                    act.wait_ge(sem("centred"), NCH * centred_before(k) + c + 1)
                    a = xc
                else:
                    for s, v in norm_input(k, c):
                        act.wait_ge(s, v)
                    a = src
                nc.scalar.activation(ch(sq, c), ch(a, c), ACT.Square).then_inc(sem("squared"), 1)
            for c in range(NCH):
                act.wait_ge(sem("var_ps"), NCH * k + c + 1)
                nc.scalar.activation(ch(rs, c), PS[:, 4 + c, :], ACT.Ln, bias=eps_col).then_inc(sem("log_var"), 1)
            for c in range(NCH):
                act.wait_ge(sem("log_var"), NCH * k + c + 1)
                nc.scalar.activation(ch(rs, c), ch(rs, c), ACT.Exp, scale=-0.5).then_inc(sem("rstd"), 1)

        def norm_dve(dve, k):
            src, dst, xc, _, rs = norm_buffers(k)
            centre, w = NORMS[k]
            if centre:
                for c in range(NCH):
                    dve.wait_ge(sem("mean_ps"), NCH * centred_before(k) + c + 1)
                    nc.vector.tensor_tensor(ch(xc, c), ch(src, c), PS[:, c, :], ALU.subtract).then_inc(sem("centred"), 1)
            for c in range(NCH):
                dve.wait_ge(sem("rstd"), NCH * k + c + 1)
                if centre:
                    dve.wait_ge(sem("centred"), NCH * centred_before(k) + c + 1)
                    nc.vector.tensor_tensor(ch(dst, c), ch(xc, c), ch(rs, c), ALU.mult).then_inc(sem("norm_out"), 1)
                else:
                    nc.vector.scalar_tensor_tensor(out=ch(dst, c), in0=ch(src, c), scalar=small("norm_w", w),
                                                   in1=ch(rs, c), op0=ALU.mult, op1=ALU.mult).then_inc(sem("norm_out"), 1)

        def rows_until(k, h):
            return NT * EXP * k + sum(1 for e in range(EXP) for tl, _, _, _ in pieces(e) if tl <= h)

        def norm_done(k, c=NCH - 1):
            return NCH * k + c + 1

        eps_tile = sb("EPSC", [P, 2])
        eps_col = eps_tile[:, 0:1]

        block = ctx.enter_context(nc.Block())

        @block.sync
        def _(sp):
            sp.dma_start(CST[:, :, :], io["consts"]).then_inc(sem("consts_loaded"), 16)
            sp.dma_start(X[:, :], io["x"]).then_inc(sem("x_loaded"), 16)
            sp.dma_start(SMT[:, :], io["small"]).then_inc(sem("small_loaded"), 16)
            sp.dma_start(WIN[:, :, :], io["w_in"]).then_inc(sem("mamba_loaded"), 16)
            sp.dma_start(XPW[:, :, :, :], io["w_x"]).then_inc(sem("mamba_loaded"), 16)
            sp.dma_start(DTW[96:96 + DTR + 1, :, :], io["w_dt"]).then_inc(sem("mamba_loaded"), 16)
            sp.dma_start(WOUT[:, :, :, :], io["w_out"]).then_inc(sem("mamba_loaded"), 16)
            sp.dma_start(F[0:96, 0:NST * P], io["sel"]).then_inc(sem("sel_loaded"), 16)
            sp.wait_ge(sem("zeros"), 1)
            for k in (0, 1):
                sp.dma_start(result_dram[k].rearrange("(p r) d -> p (r d)", p=P),
                             F[:, 6144:6144 + TOK]).then_inc(sem("results_zeroed"), 16)
            for L in range(LAYERS):
                sp.wait_ge(sem("inproj_ps"), 4 * NCH * (L + 1))
                for k in (0, 1):
                    sp.dma_start(rbm[k][SPAN:SPAN + NST, :], io["momentum"]).then_inc(sem("momentum_rows"), 16)
            sp.wait_ge(sem("gated"), LAYERS * UNITS)
            sp.wait_ge(sem("state1"), LAYERS * UNITS)
            sp.dma_start(XN[:, :], io["x"]).then_inc(sem("x_again"), 16)
            sp.dma_start(W1[:, :, :], io["w1"]).then_inc(sem("experts_loaded"), 16)
            sp.dma_start(W2[:, :, :, :], io["w2"]).then_inc(sem("experts_loaded"), 16)
            sp.dma_start(flat(B2R), io["b2"]).then_inc(sem("b2_loaded"), 16)
            for k in (0, 1):
                for c in range(NCH):
                    sp.wait_ge(sem("token_rows"), NCH * k + c + 1)
                    sp.dma_start(token_dram[k][c * CH:(c + 1) * CH, :].rearrange("(j p) d -> p j d", p=P),
                                 xtok[:, 4 * c:4 * c + 4, :]).then_inc(sem("tokens_stored"), 16)
                sp.wait_ge(sem("scattered"), 16 * ST * (k + 1))
                for c in range(NCH):
                    sp.dma_start(fetched[:, 4 * c:4 * c + 4, :],
                                 result_dram[k][c * CH:(c + 1) * CH, :].rearrange("(j p) d -> p j d", p=P)
                                 ).then_inc(sem(f"fetched{c}"), 16)
                if k == 0:
                    sp.dma_start(GW, io["w_gla"]).then_inc(sem("gla_loaded"), 16)
                    sp.dma_start(GC, io["gla_consts"]).then_inc(sem("gla_loaded"), 16)
            for c in range(NCH):
                sp.wait_ge(sem("moe_added"), NCH + c + 1)
                sp.dma_start(io["out"][:, c * CH:(c + 1) * CH], ch(X[:, :], c)).then_inc(sem("out_stored"), 16)
            sp.wait_ge(sem("tokens_stored"), 16 * NCH * 2)
            sp.wait_ge(sem("results_zeroed"), 32)
            sp.wait_ge(sem("scattered"), 16 * ST * 2)
            sp.wait_ge(sem("out_stored"), 16 * NCH)

        @block.gpsimd
        def _(pool):
            nc.gpsimd.memset(eps_tile[:, :], EPS).then_inc(sem("eps_set"), 1)
            nc.gpsimd.memset(F[:, 6144:6144 + TOK], 0.0).then_inc(sem("zeros"), 1)
            pool.wait_ge(sem("sel_loaded"), 16)
            nc.gpsimd.tensor_copy(flat(SEL[0:96, :, :]), F[0:96, 0:NST * P]).then_inc(sem("sel_ready"), 1)
            for L in range(LAYERS):
                if L == 0:
                    pool.wait_ge(sem("norm_out"), norm_done(0))
                else:
                    pool.wait_ge(sem("state1"), L * UNITS)
                for par in (0, 1):
                    nc.gpsimd.memset(xpad(par)[:, :, 0:KCONV - 1], 0.0).then_inc(sem("pads_set"), 1)
                    pool.wait_ge(sem("pads_set"), 4 * L + 2 * par + 1)
                    nc.gpsimd.memset(rank(par)[96:P, :], 1.0).then_inc(sem("pads_set"), 1)
                    pool.wait_ge(sem("pads_set"), 4 * L + 2 * par + 2)
                if L == 0:
                    nc.gpsimd.memset(zero_w, 0.0).then_inc(sem("zero_set"), 1)
                for c in range(NCH):
                    q = NCH * L + c
                    pool.wait_ge(sem("split_rest"), q + 1)
                    rest, mid = split_rest(c % 2), split_mid(c % 2)
                    part = slice(c * CH, (c + 1) * CH)
                    nc.gpsimd.tensor_copy(mid, rest).then_inc(sem("split_mid"), 1)
                    pool.wait_ge(sem("split_mid"), q + 1)
                    nc.gpsimd.tensor_copy(STK[32:64, part], mid[32:64, :]).then_inc(sem("split_done"), 1)
                    pool.wait_ge(sem("split_done"), 2 * q + 1)
                    nc.gpsimd.tensor_tensor(STK[64:96, part], rest[64:96, :], mid[64:96, :], ALU.subtract).then_inc(sem("split_done"), 1)
                    pool.wait_ge(sem("split_done"), 2 * q + 2)
                for c in range(NCH):
                    part = slice(c * CH, (c + 1) * CH)
                    pool.wait_ge(sem("sp_low"), NCH * L + c + 1)
                    nc.gpsimd.tensor_tensor(above[:, :, part], above[:, :, part], delta[:, :, part], ALU.subtract).then_inc(sem("sp_rest"), 1)
                U0 = L * UNITS

                def inputs_of(s, base):
                    if not (isinstance(base, int) and base + s < 2):
                        pool.wait_ge(sem("ut_ps"), U0 + base + s - 1)
                    at = (base + s) * SPAN
                    sl = slice(at, at + SPAN) if isinstance(at, int) else bass.ds(at, SPAN)
                    nc.gpsimd.tensor_tensor(us[s % 2], delta[:, :, sl], xs[:, :, sl], ALU.mult).then_inc(sem("us_ready"), 1)

                def rows_of_b(s, base):
                    if not (isinstance(base, int) and base + s < 2):
                        pool.wait_ge(sem("v1_ps"), U0 + base + s - 1)
                        pool.wait_ge(sem("ut_ps"), U0 + base + s)
                    row = bt[:, base + s, :] if isinstance(base, int) else bt[:, bass.ds(base + s, 1), :].rearrange("p a n -> p (a n)")
                    nc.gpsimd.tensor_tensor(rbm[s % 2][0:SPAN, :].rearrange("p (n t) -> p n t", n=NST),
                                            CST[0:SPAN, C_MASK, 0:SPAN].unsqueeze(1).to_broadcast([SPAN, NST, SPAN]),
                                            row.unsqueeze(2).to_broadcast([SPAN, NST, SPAN]),
                                            ALU.mult).then_inc(sem("rb_ready"), 1)

                def fold(s, base):
                    p = prod[s % 2]
                    pool.wait_ge(sem("readout"), U0 + base + s + 1)
                    for h in (8, 4):
                        nc.gpsimd.tensor_tensor(p[:, :, 0:h, :], p[:, :, 0:h, :], p[:, :, h:2 * h, :], ALU.add
                                                ).then_inc(sem("folded"), 1)
                        if h == 8:
                            pool.wait_ge(sem("folded"), 2 * (U0 + base + s) + 1)

                def pool_slot(s, base, more=True):
                    if more:
                        inputs_of(s + 2, base)
                        rows_of_b(s + 2, base)
                    if not (isinstance(base, int) and base + s == 0):
                        fold(s - 1, base)

                pool.wait_ge(sem("bt_ready"), NCH * (L + 1))
                pool.wait_ge(sem("inproj_ps"), 4 * NCH * (L + 1))
                pool.wait_ge(sem("delta_ready"), NCH * L + 1)
                for s in (0, 1):
                    inputs_of(s, 0)
                    rows_of_b(s, 0)
                pool.wait_ge(sem("delta_ready"), NCH * (L + 1))
                pool_slot(0, 0)
                pool_slot(1, 0)
                with pool.Fori(0, B - 1) as b:
                    for s in range(2, UPB + 2):
                        pool_slot(s, UPB * b)
                for s in range(2, UPB):
                    pool_slot(s, UNITS - UPB, s + 2 < UPB)
                fold(UPB - 1, UNITS - UPB)
            for k in (0, 1):
                if k == 0:
                    pool.wait_ge(sem("gated"), LAYERS * UNITS)
                else:
                    pool.wait_ge(sem("attn_ps"), NCH)
                nc.gpsimd.memset(F[:, 0:SLOTS], 0.0).then_inc(sem("rows_zeroed"), 1)
                pool.wait_ge(sem("rows_zeroed"), k + 1)
                pool.wait_ge(sem("tokens_stored"), 16 * NCH * (k + 1))
                pool.wait_ge(sem("indices_ready"), k + 1)
                for h in range(ST):
                    nc.gpsimd.indirect_dma_start(
                        out=rows_in[:, h, :], out_offset=None,
                        in_=token_dram[k], in_offset=bass.IndirectOffsetOnAxis(ap=IDX[:, h:h + 1], axis=0),
                        bounds_check=TOK - 1, oob_is_err=False).then_inc(sem(f"gathered{h // GS}"), 16)
                pool.wait_ge(sem("results_zeroed"), 32)
                for h in range(ST):
                    pool.wait_ge(sem("rows_made"), rows_until(k, h))
                    nc.gpsimd.indirect_dma_start(
                        out=result_dram[k], out_offset=bass.IndirectOffsetOnAxis(ap=IDX[:, h:h + 1], axis=0),
                        in_=rows_out[:, h, :], in_offset=None, bounds_check=TOK - 1, oob_is_err=False
                    ).then_inc(sem("scattered"), 16)

        @block.scalar
        def _(act):
            chain = [0]

            def link(ins):
                chain[0] += 1
                ins.then_inc(sem("act_chain"), 1)
                act.wait_ge(sem("act_chain"), chain[0])

            act.wait_ge(sem("eps_set"), 1)
            act.wait_ge(sem("small_loaded"), 16)
            al = SM["a_log"]
            nc.scalar.activation(flat(NEGA[:, :, :]), SMT[:, al:al + LAYERS * HALVES * NST], ACT.Exp).then_inc(sem("a_exp"), 1)
            norm_act(act, 0)
            for L in range(LAYERS):
                norm_act(act, 1 + L)
                act.wait_ge(sem("pads_set"), 4 * (L + 1))
                if L == 0:
                    act.wait_ge(sem("results_zeroed"), 32)
                    act.wait_ge(sem("sel_ready"), 1)
                for c in range(NCH + 1):
                    if c < NCH:
                        q = NCH * L + c
                        for m in range(HALVES):
                            act.wait_ge(sem("inproj_ps"), 4 * q + m + 1)
                            if c >= 2:
                                act.wait_ge(sem("conv_done"), q - 1)
                            nc.scalar.activation(xpad(c % 2)[:, m, KCONV - 1:], PS[:, m, :], ACT.Copy).then_inc(sem("xb_out"), 1)
                        for m in range(HALVES):
                            act.wait_ge(sem("inproj_ps"), 4 * q + HALVES + m + 1)
                            nc.scalar.activation(ch(zs[:, m, :], c), PS[:, HALVES + m, :], ACT.Silu).then_inc(sem("z_out"), 1)
                    if c > 0:
                        q = NCH * L + c - 1
                        act.wait_ge(sem("xproj_ps"), q + 1)
                        nc.scalar.activation(rank((c - 1) % 2)[96:96 + DTR, :], PS[96:96 + DTR, 4, :], ACT.Copy).then_inc(sem("rank_ready"), 1)
                        act.wait_ge(sem("bt_ps"), q + 1)
                        nc.scalar.activation(flat(bt[:, UPB * (c - 1):UPB * c, :]), PS[0:SPAN, 5, 0:UPB * NST], ACT.Copy
                                             ).then_inc(sem("bt_ready"), 1)
                        act.wait_ge(sem("dt_ps"), q + 1)
                        nc.scalar.activation(delta[:, :, (c - 1) * CH:c * CH], PS[:, 6:8, :], ACT.Abs).then_inc(sem("sp_abs"), 1)
                        act.wait_ge(sem("xs_ready"), q + 1)
                        for m in range(HALVES):
                            nc.scalar.activation(Y[:, m, (c - 1) * CH:c * CH], xs[:, m, (c - 1) * CH:c * CH], ACT.Copy,
                                                 scale=small("dp", HALVES * L + m)).then_inc(sem("dx_ready"), 1)
                    if c < NCH:
                        act.wait_ge(sem("conv_done"), NCH * L + c + 1)
                        nc.scalar.activation(xs[:, :, c * CH:(c + 1) * CH], slot(c % 2, 0), ACT.Silu).then_inc(sem("xs_ready"), 1)
                for c in range(NCH):
                    part = slice(c * CH, (c + 1) * CH)
                    act.wait_ge(sem("sp_abs"), NCH * L + c + 1)
                    nc.scalar.activation(delta[:, :, part], delta[:, :, part], ACT.Exp, scale=-1.0).then_inc(sem("sp_e"), 1)
                for c in range(NCH):
                    part = slice(c * CH, (c + 1) * CH)
                    act.wait_ge(sem("sp_u"), NCH * L + c + 1)
                    act.wait_ge(sem("sp_low"), NCH * L + c + 1)
                    nc.scalar.activation(one_e[:, :, part], one_e[:, :, part], ACT.Ln).then_inc(sem("sp_log"), 1)
                act.wait_ge(sem("dec_zeroed"), 2 * L + 1)
                act.wait_ge(sem("delta_ready"), NCH * L + 1)
                U0 = L * UNITS

                def decays(gpar, part, tok0):
                    for j in range(8):
                        m, n = divmod(8 * part + j, NST)
                        sl = slice(tok0, tok0 + GRP * SPAN) if isinstance(tok0, int) else bass.ds(tok0, GRP * SPAN)
                        ins = nc.scalar.activation(
                            dec[gpar][:, m, :, n, 1:SPAN],
                            delta[:, m, sl].rearrange("p (j t) -> p j t", j=GRP)[:, :, 1:SPAN],
                            ACT.Exp, scale=NEGA[:, HALVES * L + m, n:n + 1])
                    if part == GRP - 1:
                        ins.then_inc(sem("decays_ready"), 1)

                def act_slot(s, base, group=True, turned=True):
                    if turned:
                        act.wait_ge(sem("ut_ps"), U0 + base + s + 3)
                        act.wait_ge(sem("v1_ps"), U0 + base + s + 1)
                        nc.scalar.activation(ut[s % 2], PS[0:SPAN + NST, 6, 0:256], ACT.Copy).then_inc(sem("ut_out"), 1)
                    if group:
                        g = s // GRP + 1
                        if s % GRP == 0 and not (isinstance(base, int) and base + s < GRP):
                            act.wait_ge(sem("state1"), U0 + base + s)
                        decays(g % 2, s % GRP, base * SPAN + g * GRP * SPAN)

                for part in range(GRP):
                    decays(0, part, 0)
                act.wait_ge(sem("dec_zeroed"), 2 * L + 2)
                act.wait_ge(sem("a0_arg"), L + 1)
                nc.scalar.activation(a0[:, :, :, 0:UNITS], a0[:, :, :, 0:UNITS], ACT.Exp).then_inc(sem("a0_exp"), 1)
                for i in (0, 1):
                    act.wait_ge(sem("ut_ps"), U0 + i + 1)
                    nc.scalar.activation(ut[i], PS[0:SPAN + NST, 6, 0:256], ACT.Copy).then_inc(sem("ut_out"), 1)
                act_slot(0, 0)
                act_slot(1, 0)
                with act.Fori(0, B - 1) as b:
                    for s in range(2, UPB + 2):
                        act_slot(s, UPB * b)
                for s in range(2, UPB):
                    act_slot(s, UNITS - UPB, s < GRP, s + 2 < UPB)

            def moe(k):
                norm_act(act, 3 if k == 0 else 6)
                act.wait_ge(sem("shifted"), k + 1)
                nc.scalar.activation(RT[:, 1, :], RT[:, 0, :], ACT.Exp).then_inc(sem("route_exp"), 1)
                for c in range(NCH):
                    act.wait_ge(sem("rows_ps"), NCH * k + c + 1)
                    nc.scalar.activation(flat(xtok[:, 4 * c:4 * c + 4, :]), PS[:, 4 + c, :], ACT.Copy
                                         ).then_inc(sem("token_rows"), 1)
                for e in range(EXP):
                    for j in range(FJ):
                        act.wait_ge(sem("hid_ps"), FJ * (EXP * k + e) + j + 1)
                        if e >= 2 and j == 0:
                            act.wait_ge(sem("rows_made"), NT * (EXP * k + e - 1))
                        nc.scalar.activation(hid[e % 2][:, j, :], PS[:, 2 + j, 0:CAP], ACT.Relu,
                                             bias=small("b1", FJ * e + j)).then_inc(sem("hidden"), 1)

            moe(0)
            norm_act(act, 4)
            act.wait_ge(sem("gla_loaded"), 32)
            act.wait_ge(sem("rank16_ps"), NCH)
            nc.scalar.activation(tile(5)[0:16, :], flat(PS[0:16, 0:4, :]), ACT.Copy).then_inc(sem("rank16"), 1)
            kr = HEADS * DK
            act.wait_ge(sem("kg_ps"), NCH)
            src = flat(PS[0:kr, 4:8, :])
            link(nc.scalar.activation(tile(0)[0:kr, :], src, ACT.Abs))
            link(nc.scalar.activation(tile(0)[0:kr, :], tile(0)[0:kr, :], ACT.Exp, scale=-1.0))
            nc.scalar.activation(tile(1)[0:kr, :], tile(0)[0:kr, :], ACT.Ln, bias=1.0).then_inc(sem("kg_log"), 1)
            act.wait_ge(sem("log_gate"), 1)
            nc.scalar.activation(tile(0)[0:kr, :], tile(2)[0:kr, :], ACT.Exp, scale=1.0 / 16).then_inc(sem("gla_decay"), 1)
            for c in range(NCH):
                act.wait_ge(sem("gate_ps"), c + 1)
                nc.scalar.activation(ch(xs[:, 0, :], c), PS[:, c, :], ACT.Silu, bias=small("bg")).then_inc(sem("gate_out"), 1)
            for i in range(2 * GT):
                act.wait_ge(sem("v_ps"), i + 1)
                nc.scalar.activation(zs[:, 0, (i % 2) * QTOK:(i % 2 + 1) * QTOK], flat(PS[:, 2:4, :]), ACT.Copy
                                     ).then_inc(sem("v_out"), 1)
                if i % GT == GT - 1:
                    th = i // GT
                    act.wait_ge(sem("o_ps"), th + 1)
                    nc.scalar.activation(tile(6)[:, th * QTOK:(th + 1) * QTOK], flat(PS[:, 6:8, :]), ACT.Copy
                                         ).then_inc(sem("o_copied"), 1)
            norm_act(act, 5)
            moe(1)

        @block.vector
        def _(dve):
            chain = [0]

            def link(ins):
                chain[0] += 1
                ins.then_inc(sem("dve_chain"), 1)
                dve.wait_ge(sem("dve_chain"), chain[0])

            taps = [0]
            dve.wait_ge(sem("a_exp"), 1)
            nc.vector.tensor_scalar(flat(NEGA[:, :, :]), flat(NEGA[:, :, :]), -1.0, None, ALU.mult).then_inc(sem("nega"), 1)
            norm_dve(dve, 0)
            for L in range(LAYERS):
                norm_dve(dve, 1 + L)
                for c in range(NCH + 1):
                    if c < NCH:
                        q = NCH * L + c
                        dve.wait_ge(sem("pads_set"), 4 * (L + 1))
                        if c >= 2:
                            dve.wait_ge(sem("xs_ready"), q - 1)
                        for j in range(KCONV):
                            for m in range(HALVES):
                                if j == 0:
                                    dve.wait_ge(sem("xb_out"), HALVES * q + m + 1)
                                tap = xpad(c % 2)[:, m, j:j + SEQ]
                                acc = slot(c % 2, 0)[:, m, :]
                                w = small("conv_w", KCONV * (HALVES * L + m) + j)
                                if j == 0:
                                    ins = nc.vector.tensor_scalar(acc, tap, w, small("conv_b", HALVES * L + m), ALU.mult, ALU.add)
                                else:
                                    ins = nc.vector.scalar_tensor_tensor(out=acc, in0=tap, scalar=w, in1=acc, op0=ALU.mult, op1=ALU.add)
                                if j < KCONV - 1:
                                    taps[0] += 1
                                    ins.then_inc(sem("taps"), 1)
                            if j < KCONV - 1:
                                dve.wait_ge(sem("taps"), taps[0])
                        ins.then_inc(sem("conv_done"), 1)
                    if c > 0:
                        q = NCH * L + c - 1
                        part = slice((c - 1) * CH, c * CH)
                        dve.wait_ge(sem("xproj_ps"), q + 1)
                        bc = PS[0:96, 4, :]
                        if c >= 3:
                            dve.wait_ge(sem("split_done"), 2 * (q - 1))
                        link(nc.vector.tensor_copy(STK[0:96, part], bc))
                        nc.vector.tensor_tensor(split_rest((c - 1) % 2), bc, STK[0:96, part], ALU.subtract).then_inc(sem("split_rest"), 1)
                        dve.wait_ge(sem("sp_abs"), q + 1)
                        nc.vector.tensor_scalar(above[:, :, part], PS[:, 6:8, :], 0.0, None, ALU.max).then_inc(sem("sp_max"), 1)
                dve.wait_ge(sem("split_done"), 2 * NCH * (L + 1))
                dve.wait_ge(sem("xs_ready"), NCH * (L + 1))
                dve.wait_ge(sem("dt_ps"), NCH * (L + 1))
                nc.vector.memset(BIG[:, 0:8192].rearrange("p (s t) -> p s t", t=SPAN)[:, :, 0:1], 0.0).then_inc(sem("dec_zeroed"), 1)
                nc.vector.memset(carry, 0.0).then_inc(sem("carried"), 1)
                for c in range(NCH):
                    q = NCH * L + c
                    part = slice(c * CH, (c + 1) * CH)
                    dve.wait_ge(sem("sp_e"), q + 1)
                    nc.vector.tensor_scalar(one_e[:, :, part], delta[:, :, part], 1.0, None, ALU.add).then_inc(sem("sp_u"), 1)
                    dve.wait_ge(sem("sp_u"), q + 1)
                    nc.vector.scalar_tensor_tensor(out=delta[:, :, part], in0=one_e[:, :, part], scalar=-1.0, in1=delta[:, :, part],
                                                   op0=ALU.add, op1=ALU.subtract).then_inc(sem("sp_low"), 1)
                for c in range(NCH):
                    q = NCH * L + c
                    part = slice(c * CH, (c + 1) * CH)
                    dve.wait_ge(sem("sp_log"), q + 1)
                    dve.wait_ge(sem("sp_rest"), q + 1)
                    nc.vector.tensor_tensor(delta[:, :, part], one_e[:, :, part], above[:, :, part], ALU.add).then_inc(sem("delta_ready"), 1)
                dve.wait_ge(sem("delta_ready"), NCH * (L + 1))
                nc.vector.memset(BIG[:, 8192:16384].rearrange("p (s t) -> p s t", t=SPAN)[:, :, 0:1], 0.0).then_inc(sem("dec_zeroed"), 1)
                for m in range(HALVES):
                    ins = nc.vector.tensor_tensor(
                        a0[:, m, :, 0:UNITS],
                        delta[:, m, :].rearrange("p (i t) -> p i t", t=SPAN)[:, :, 0].unsqueeze(1).to_broadcast([P, NST, UNITS]),
                        NEGA[:, HALVES * L + m, :].unsqueeze(2).to_broadcast([P, NST, UNITS]), ALU.mult)
                ins.then_inc(sem("a0_arg"), 1)
                dve.wait_ge(sem("a0_exp"), L + 1)
                nc.vector.memset(a0[:, :, :, 0:UNITS + 1:UPB], 0.0).then_inc(sem("a0_ready"), 1)
                dve.wait_ge(sem("a0_ready"), L + 1)
                U0 = L * UNITS

                def dve_slot(s, base, groups):
                    par = s % 2
                    if s % GRP == 0 or (isinstance(base, int) and base + s == 0):
                        dve.wait_ge(sem("decays_ready"), (U0 + s) // GRP + 1 + groups)
                    if not (isinstance(base, int) and base + s == 0):
                        dve.wait_ge(sem("readout"), U0 + base + s)
                    for m in range(HALVES):
                        dve.wait_ge(sem(f"v{m}_ps"), U0 + base + s + 1)
                        nc.vector.tensor_tensor_scan(
                            state[:, m].rearrange("p n t -> p (n t)"),
                            dec[s // GRP % 2][:, m, s % GRP].rearrange("p n t -> p (n t)"),
                            flat(PS[:, 2 * m:2 * m + 2, :]), 0.0, ALU.mult, ALU.add).then_inc(sem(f"state{m}"), 1)
                    dve.wait_ge(sem("state0"), U0 + base + s + 1)
                    dve.wait_ge(sem("state1"), U0 + base + s + 1)
                    nxt = a0[:, :, :, base + s + 1] if isinstance(base, int) else a0[:, :, :, bass.ds(base + s + 1, 1)].rearrange("p m n i -> p m (n i)")
                    nc.vector.tensor_tensor(carry, nxt, state[:, :, :, SPAN - 1], ALU.mult).then_inc(sem("carried"), 1)
                    dve.wait_ge(sem("c_ps"), U0 + base + s + 1)
                    if not (isinstance(base, int) and base + s < 2):
                        dve.wait_ge(sem("y_ps"), U0 + base + s - 1)
                    nc.vector.tensor_tensor(prod[par].rearrange("p m n t -> p m (n t)"), state.rearrange("p m n t -> p m (n t)"),
                                            flat(PS[:, 4:6, :]).unsqueeze(1).to_broadcast([P, HALVES, NST * SPAN]),
                                            ALU.mult).then_inc(sem("readout"), 1)
                    if not (isinstance(base, int) and base + s < 2):
                        gate(s - 2, base)

                def gate(s, base):
                    dve.wait_ge(sem("y_ps"), U0 + base + s + 1)
                    at = (base + s) * SPAN
                    sl = slice(at, at + SPAN) if isinstance(at, int) else bass.ds(at, SPAN)
                    nc.vector.tensor_tensor(Y[:, :, sl], PS[:, 7, 0:2 * SPAN].rearrange("p (m t) -> p m t", m=HALVES), zs[:, :, sl],
                                            ALU.mult).then_inc(sem("gated"), 1)

                dve_slot(0, 0, 0)
                dve_slot(1, 0, 0)
                with dve.Fori(0, B - 1) as b:
                    for s in range(2, UPB + 2):
                        dve_slot(s, UPB * b, UPB // GRP * b)
                for s in range(2, UPB):
                    dve_slot(s, UNITS - UPB, (UNITS - UPB) // GRP)
                gate(UPB - 2, UNITS - UPB)
                gate(UPB - 1, UNITS - UPB)
                for c in range(NCH):
                    dve.wait_ge(sem("outproj_ps"), NCH * L + c + 1)
                    nc.vector.tensor_tensor(ch(X[:, :], c), ch(X[:, :], c), PS[:, c, :], ALU.add).then_inc(sem("outproj_added"), 1)
            dve.wait_ge(sem("x_again"), 16)
            dve.wait_ge(sem("outproj_added"), NCH * LAYERS)
            nc.vector.tensor_tensor(X[:, :], X[:, :], XN[:, :], ALU.add).then_inc(sem("stream_added"), 1)

            def by_block(ap):
                return ap.rearrange("p (b e) -> p b e", e=EXP)

            def over(ap):
                return ap.unsqueeze(2).to_broadcast([P, NBLK, EXP])

            def moe(k):
                norm_dve(dve, 3 if k == 0 else 6)
                R = [RT[:, i, :] for i in range(10)]
                S = [RTS[:, i, :] for i in range(8)]
                dve.wait_ge(sem("logits_ps"), k + 1)
                lg = PS[:, 0, 0:P]
                link(nc.vector.tensor_reduce(S[0], by_block(lg), AX.X, ALU.max))
                nc.vector.tensor_tensor(by_block(R[0]), by_block(lg), over(S[0]), ALU.subtract).then_inc(sem("shifted"), 1)
                dve.wait_ge(sem("shifted"), k + 1)
                link(nc.vector.scalar_tensor_tensor(out=R[2], in0=R[0], scalar=0.0, in1=CST[:, C_RAMP, :],
                                                    op0=ALU.is_equal, op1=ALU.mult))
                link(nc.vector.tensor_reduce(S[1], by_block(R[2]), AX.X, ALU.max))
                nc.vector.tensor_tensor(by_block(R[3]), by_block(R[2]), over(S[1]), ALU.is_equal).then_inc(sem("chosen"), 1)
                dve.wait_ge(sem("route_exp"), k + 1)
                link(nc.vector.tensor_reduce(S[2], by_block(R[1]), AX.X, ALU.add))
                link(nc.vector.reciprocal(S[3], S[2]))
                dve.wait_ge(sem("counts_ps"), k + 1)
                tot = by_block(PS[:, 2, 0:P]).rearrange("p b e -> p e b")
                link(nc.vector.tensor_copy(R[4].rearrange("p (e b) -> p e b", b=NBLK), tot))
                link(nc.vector.memset(R[5], 1.0))
                link(nc.vector.memset(R[5].rearrange("p (e b) -> p e b", b=NBLK)[:, :, 0:1], 0.0))
                link(nc.vector.tensor_tensor_scan(R[6], R[5], R[4], 0.0, ALU.mult, ALU.add))
                link(nc.vector.tensor_tensor(R[6], R[6], R[4], ALU.subtract))
                link(nc.vector.tensor_tensor(by_block(R[7]), by_block(PS[:, 1, 0:P]),
                                             R[6].rearrange("p (e b) -> p b e", b=NBLK), ALU.add))
                link(nc.vector.scalar_tensor_tensor(out=R[8], in0=R[7], scalar=float(CAP), in1=R[3],
                                                    op0=ALU.is_le, op1=ALU.mult))
                link(nc.vector.tensor_tensor(R[7], R[7], CST[:, C_EBASE, :], ALU.add))
                link(nc.vector.tensor_tensor(R[7], R[7], R[8], ALU.mult))
                link(nc.vector.tensor_reduce(S[4], by_block(R[7]), AX.X, ALU.add))
                link(nc.vector.tensor_reduce(S[5], by_block(R[8]), AX.X, ALU.add))
                link(nc.vector.tensor_scalar(S[6], S[5], -FAR, FAR, ALU.mult, ALU.add))
                link(nc.vector.tensor_tensor(S[6], S[6], S[4], ALU.add))
                link(nc.vector.tensor_scalar(S[1], S[6], 1.0 / P, None, ALU.mult))
                link(nc.vector.tensor_tensor(passed, S[1].unsqueeze(2).to_broadcast([P, NBLK, ST + 1]),
                                             CST[:, C_IOTA, 0:ST + 1].unsqueeze(1).to_broadcast([P, NBLK, ST + 1]), ALU.is_ge))
                link(nc.vector.tensor_reduce(S[2], passed[:, :, 1:], AX.X, ALU.add))
                link(nc.vector.scalar_tensor_tensor(out=S[2], in0=S[2], scalar=-float(P), in1=S[6], op0=ALU.mult, op1=ALU.add))
                link(nc.vector.tensor_tensor(tile_hot, passed[:, :, 0:ST], passed[:, :, 1:], ALU.subtract))
                link(nc.vector.tensor_tensor(tile_hot, tile_hot,
                                             CST[:, C_MASK, 64:64 + NBLK].unsqueeze(2).to_broadcast([P, NBLK, ST]), ALU.mult))
                for t in range(NBLK):
                    nc.vector.tensor_scalar(row_hot[:, t, :], CST[:, C_IOTA, :], S[2][:, t:t + 1], None, ALU.is_equal
                                            ).then_inc(sem("row_hot"), 1)
                dve.wait_ge(sem("index_ps"), k + 1)
                nc.vector.tensor_scalar(IDX[:, :], PS[:, 3, 0:ST], FAR, None, ALU.add).then_inc(sem("indices_ready"), 1)
                link(nc.vector.tensor_tensor(S[7], S[3], S[5], ALU.mult))
                for t in range(NBLK):
                    nc.vector.tensor_scalar(diag[:, t, :], ident, S[7][:, t:t + 1], None, ALU.mult).then_inc(sem("diagonals"), 1)
                def turned(g):
                    dve.wait_ge(sem("disp_ps"), ST // GS * k + g + 1)
                    nc.vector.tensor_copy(xdisp[:, g * CH:(g + 1) * CH], PS[:, g % 2, :]).then_inc(sem("dispatched"), 1)

                turned(0)
                turned(1)
                for e in range(EXP):
                    made(k, e)
                    if e + 2 < ST // GS:
                        turned(e + 2)
                for c in range(NCH):
                    dve.wait_ge(sem("moe_ps"), NCH * k + c + 1)
                    nc.vector.tensor_tensor(ch(X[:, :], c), ch(X[:, :], c), PS[:, 2 + c, :], ALU.add).then_inc(sem("moe_added"), 1)

            def made(k, e):
                if k == 0 and e == 0:
                    dve.wait_ge(sem("b2_loaded"), 16)
                dve.wait_ge(sem("rows2_ps"), EXP * k + e + 1)
                for i, (h, a, n, _) in enumerate(pieces(e)):
                    nc.vector.tensor_tensor(rows_out[a:a + n, h, :], PS[a:a + n, 6 + e % 2, i * P:(i + 1) * P],
                                            B2R[a:a + n, e, :], ALU.add).then_inc(sem("rows_made"), 1)

            moe(0)
            norm_dve(dve, 4)
            kr = HEADS * DK
            dve.wait_ge(sem("kg_log"), 1)
            nc.vector.scalar_tensor_tensor(out=tile(2)[0:kr, :], in0=flat(PS[0:kr, 4:8, :]), scalar=0.0,
                                           in1=tile(1)[0:kr, :], op0=ALU.min, op1=ALU.subtract).then_inc(sem("log_gate"), 1)
            dve.wait_ge(sem("gla_decay"), 1)
            nc.vector.memset(tile(0)[0:kr, :].rearrange("p (s t) -> p s t", t=SEQ)[:, :, 0:1], 0.0).then_inc(sem("gla_decay0"), 1)
            for i in range(2 * GT):
                vt = zs[:, 0, (i % 2) * QTOK:(i % 2 + 1) * QTOK]
                kv = tile(1)[:, 0:QTOK]
                st = tile(1)[:, QTOK:TOK]
                out = tile(2)[:, (i % 2) * QTOK:(i % 2 + 1) * QTOK]
                dve.wait_ge(sem("v_out"), i + 1)
                dve.wait_ge(sem("k_ps"), i + 1)
                nc.vector.scalar_tensor_tensor(out=kv, in0=flat(PS[:, 0:2, :]), scalar=DK ** -0.5, in1=vt,
                                               op0=ALU.mult, op1=ALU.mult).then_inc(sem("kv_done"), 1)
                dve.wait_ge(sem("decay_ps"), i + 1)
                dve.wait_ge(sem("kv_done"), i + 1)
                nc.vector.tensor_tensor_scan(st, flat(PS[:, 4:6, :]), kv, 0.0, ALU.mult, ALU.add).then_inc(sem("gla_state"), 1)
                dve.wait_ge(sem("q_ps"), i + 1)
                dve.wait_ge(sem("gla_state"), i + 1)
                if i >= 2:
                    dve.wait_ge(sem("o_part"), i - 1)
                nc.vector.tensor_tensor(out, st, flat(PS[:, 0:2, :]), ALU.mult).then_inc(sem("qs_done"), 1)
            norm_dve(dve, 5)
            dve.wait_ge(sem("gate_out"), NCH)
            dve.wait_ge(sem("norm_out"), norm_done(5))
            for c in range(NCH):
                nc.vector.tensor_tensor(ch(xs[:, 1, :], c), ch(tile(6), c), ch(xs[:, 0, :], c), ALU.mult).then_inc(sem("o_gated"), 1)
            for c in range(NCH):
                dve.wait_ge(sem("attn_ps"), c + 1)
                nc.vector.tensor_tensor(ch(X[:, :], c), ch(X[:, :], c), PS[:, c, :], ALU.add).then_inc(sem("attn_added"), 1)
            moe(1)

        @block.tensor
        def _(pe):
            def mm(out, lhsT, rhs, start=True, stop=True):
                return nc.tensor.matmul(out, lhsT, rhs, start=start, stop=stop)

            pe.wait_ge(sem("consts_loaded"), 16)
            norm_pe(pe, 0)
            for L in range(LAYERS):
                norm_pe(pe, 1 + L)
                if L == 0:
                    pe.wait_ge(sem("mamba_loaded"), 64)
                for c in range(NCH + 1):
                    if c < NCH:
                        q = NCH * L + c
                        pe.wait_ge(sem("norm_out"), norm_done(1 + L, c))
                        for m in range(2 * HALVES):
                            if c > 0:
                                if m < HALVES:
                                    pe.wait_ge(sem("xb_out"), HALVES * (q - 1) + m + 1)
                                else:
                                    pe.wait_ge(sem("z_out"), HALVES * (q - 1) + m - HALVES + 1)
                            mm(PS[:, m, :], WIN[:, L, m * P:(m + 1) * P], ch(XN, c)).then_inc(sem("inproj_ps"), 1)
                    if c > 0:
                        q = NCH * L + c - 1
                        part = slice((c - 1) * CH, c * CH)
                        pe.wait_ge(sem("xs_ready"), q + 1)
                        if q % NCH:
                            pe.wait_ge(sem("rank_ready"), q)
                            pe.wait_ge(sem("split_rest"), q)
                            pe.wait_ge(sem("bt_ready"), q)
                        for m in range(HALVES):
                            ins = mm(PS[0:XW, 4, :], XPW[:, L, m, :], xs[:, m, part], m == 0, m == HALVES - 1)
                        ins.then_inc(sem("xproj_ps"), 1)
                        for k in range(UPB):
                            at = (c - 1) * CH + k * SPAN
                            for m in range(HALVES):
                                ins = mm(PS[0:SPAN, 5, k * NST:(k + 1) * NST], xs[:, m, at:at + SPAN], XPW[:, L, m, 0:NST],
                                         m == 0, m == HALVES - 1)
                        ins.then_inc(sem("bt_ps"), 1)
                        pe.wait_ge(sem("rank_ready"), q + 1)
                        if q % NCH:
                            pe.wait_ge(sem("sp_abs"), q)
                            pe.wait_ge(sem("sp_max"), q)
                        for m in range(HALVES):
                            ins = mm(PS[:, 6 + m, :], DTW[96:96 + DTR + 1, L, m * P:(m + 1) * P], rank((c - 1) % 2)[96:96 + DTR + 1, :])
                        ins.then_inc(sem("dt_ps"), 1)
                pe.wait_ge(sem("split_done"), 2 * NCH * (L + 1))
                pe.wait_ge(sem("sel_ready"), 1)
                pe.wait_ge(sem("zero_set"), 1)
                pe.wait_ge(sem("sp_abs"), NCH * (L + 1))
                pe.wait_ge(sem("sp_max"), NCH * (L + 1))
                pe.wait_ge(sem("dx_ready"), HALVES * NCH * (L + 1))
                pe.wait_ge(sem("momentum_rows"), 32 * (L + 1))
                U0 = L * UNITS

                def turn(s, base):
                    par = s % 2
                    pe.wait_ge(sem("us_ready"), U0 + base + s + 1)
                    if not (isinstance(base, int) and base + s == 0):
                        pe.wait_ge(sem("ut_out"), U0 + base + s)
                    if s % UPB == 0:
                        mm(PS[SPAN:SPAN + NST, 6, 0:256], zero_w, flat(CST[0:SPAN + NST, 0:2, :]))
                    else:
                        pe.wait_ge(sem("rb_ready"), U0 + base + s)
                        mm(PS[SPAN:SPAN + NST, 6, 0:256], rbm[1 - par].rearrange("p (n t) -> p n t", n=NST)[:, :, SPAN - 1],
                           ut[1 - par])
                    for m in range(HALVES):
                        ins = nc.tensor.transpose(PS[0:SPAN, 6, m * P:(m + 1) * P], us[par][:, m, :], ident)
                    ins.then_inc(sem("ut_ps"), 1)

                def sum_y(s, base):
                    pe.wait_ge(sem("folded"), 2 * (U0 + base + s) + 2)
                    if not (isinstance(base, int) and base + s == 0):
                        pe.wait_ge(sem("gated"), U0 + base + s)
                    at = (base + s) * SPAN
                    sl = slice(at, at + SPAN) if isinstance(at, int) else bass.ds(at, SPAN)
                    mm(PS[:, 7, 0:2 * SPAN], ident, Y[:, :, sl], True, False)
                    for n in range(4):
                        ins = mm(PS[:, 7, 0:2 * SPAN], ident, prod[s % 2][:, :, n, :], False, n == 3)
                    ins.then_inc(sem("y_ps"), 1)

                def pe_slot(s, base, turned=True):
                    par = s % 2
                    first = isinstance(base, int) and base + s == 0
                    pe.wait_ge(sem("ut_out"), U0 + base + s + 1)
                    pe.wait_ge(sem("rb_ready"), U0 + base + s + 1)
                    for m in range(HALVES):
                        if not first:
                            pe.wait_ge(sem(f"state{m}"), U0 + base + s)
                        for j in range(2):
                            nc.tensor.matmul(PS[:, 2 * m + j, :], ut[par][:, m * P:(m + 1) * P],
                                             rbm[par][:, j * CH:(j + 1) * CH], start=True, stop=False, skip_group_check=True)
                    pe.wait_ge(sem("carried"), U0 + L + base + s + 1)
                    for m in range(HALVES):
                        for j in range(2):
                            ins = nc.tensor.matmul(PS[:, 2 * m + j, :].rearrange("p (n t) -> p n t", t=SPAN)[:, :, 0], ident,
                                                   carry[:, m, 8 * j:8 * j + 8], start=False, stop=True, skip_group_check=True)
                        ins.then_inc(sem(f"v{m}_ps"), 1)
                    if not first:
                        pe.wait_ge(sem("readout"), U0 + base + s)
                    at = (base + s) * SPAN
                    sl = slice(at, at + SPAN) if isinstance(at, int) else bass.ds(at, SPAN)
                    for n in range(NST):
                        ins = mm(PS[:, 4 + n // 8, (n % 8) * SPAN:(n % 8 + 1) * SPAN], SEL[0:96, n, :], STK[0:96, sl])
                    ins.then_inc(sem("c_ps"), 1)
                    if not (isinstance(base, int) and base + s < 2):
                        sum_y(s - 2, base)
                    if turned:
                        turn(s + 2, base)

                turn(0, 0)
                turn(1, 0)
                pe_slot(0, 0)
                pe_slot(1, 0)
                with pe.Fori(0, B - 1) as b:
                    for s in range(2, UPB + 2):
                        pe_slot(s, UPB * b)
                for s in range(2, UPB):
                    pe_slot(s, UNITS - UPB, s + 2 < UPB)
                sum_y(UPB - 2, UNITS - UPB)
                sum_y(UPB - 1, UNITS - UPB)
                for c in range(NCH):
                    pe.wait_ge(sem("gated"), U0 + UPB * (c + 1))
                    for m in range(HALVES):
                        ins = mm(PS[:, c, :], WOUT[:, L, m, :], Y[:, m, c * CH:(c + 1) * CH], m == 0, m == HALVES - 1)
                    ins.then_inc(sem("outproj_ps"), 1)

            def moe(k):
                norm_pe(pe, 3 if k == 0 else 6)
                pe.wait_ge(sem("norm_out"), norm_done(3 if k == 0 else 6))
                for t in range(NBLK):
                    ins = mm(PS[:, 0, EXP * t:EXP * (t + 1)], XN[:, t * P:(t + 1) * P],
                             SMT[:, SM["gate"]:SM["gate"] + EXP])
                ins.then_inc(sem("logits_ps"), 1)
                for c in range(NCH):
                    for t in range(4):
                        ins = nc.tensor.transpose(PS[:, 4 + c, t * P:(t + 1) * P],
                                                  XN[:, (4 * c + t) * P:(4 * c + t + 1) * P], ident)
                    ins.then_inc(sem("rows_ps"), 1)
                pe.wait_ge(sem("chosen"), k + 1)
                mm(PS[:, 1, 0:P], CST[:, C_TRI, :], RT[:, 3, :])
                mm(PS[:, 2, 0:P], CST[:, C_ONE, :], RT[:, 3, :]).then_inc(sem("counts_ps"), 1)
                for t in range(NBLK):
                    pe.wait_ge(sem("row_hot"), NBLK * k + t + 1)
                    ins = mm(PS[:, 3, 0:ST], row_hot[:, t, :], tile_hot[:, t, :], t == 0, t == NBLK - 1)
                ins.then_inc(sem("index_ps"), 1)
                pe.wait_ge(sem("indices_ready"), k + 1)
                pe.wait_ge(sem("token_rows"), NCH * (k + 1))
                if k == 0:
                    pe.wait_ge(sem("experts_loaded"), 32)

                def turn_rows(g):
                    pe.wait_ge(sem(f"gathered{g}"), 16 * GS * (k + 1))
                    if g >= 2:
                        pe.wait_ge(sem("dispatched"), ST // GS * k + g - 1)
                    for i in range(GS):
                        ins = nc.tensor.transpose(PS[:, g % 2, i * P:(i + 1) * P], rows_in[:, GS * g + i, :], ident)
                    ins.then_inc(sem("disp_ps"), 1)

                turn_rows(0)
                for e in range(EXP):
                    if e + 1 < ST // GS:
                        turn_rows(e + 1)
                    pe.wait_ge(sem("dispatched"), ST // GS * k + ((e + 1) * CAP + CH - 1) // CH)
                    for j in range(FJ):
                        if e:
                            pe.wait_ge(sem("hidden"), FJ * (EXP * k + e - 1) + j + 1)
                        mm(PS[:, 2 + j, 0:CAP], W1[:, e, j * P:(j + 1) * P], xdisp[:, e * CAP:(e + 1) * CAP]
                           ).then_inc(sem("hid_ps"), 1)
                    pe.wait_ge(sem("hidden"), FJ * (EXP * k + e + 1))
                    if e >= 2:
                        pe.wait_ge(sem("rows_made"), NT * (EXP * k + e - 1))
                    for i, (_, a, n, s0) in enumerate(pieces(e)):
                        for j in range(FJ):
                            ins = mm(PS[a:a + n, 6 + e % 2, i * P:(i + 1) * P], hid[e % 2][:, j, s0:s0 + n], W2[:, e, j, :],
                                     j == 0, j == FJ - 1)
                    ins.then_inc(sem("rows2_ps"), 1)
                for c in range(NCH):
                    pe.wait_ge(sem(f"fetched{c}"), 16 * (k + 1))
                    pe.wait_ge(sem("diagonals"), NBLK * k + 4 * c + 4)
                    for t in range(4):
                        ins = mm(PS[:, 2 + c, t * P:(t + 1) * P], fetched[:, 4 * c + t, :], diag[:, 4 * c + t, :])
                    ins.then_inc(sem("moe_ps"), 1)

            moe(0)
            norm_pe(pe, 4)
            pe.wait_ge(sem("gla_loaded"), 32)
            pe.wait_ge(sem("norm_out"), norm_done(4))
            for c in range(NCH):
                mm(PS[0:16, c, :], GW[:, GG1:GG1 + 16], ch(XN[:, :], c)).then_inc(sem("rank16_ps"), 1)
            pe.wait_ge(sem("rank16"), 1)
            for c in range(NCH):
                mm(PS[0:HEADS * DK, 4 + c, :], WG2[0:16, :], ch(tile(5)[0:16, :], c)).then_inc(sem("kg_ps"), 1)
            for c in range(NCH):
                mm(PS[:, c, :], GW[:, GG:GG + P], ch(XN[:, :], c)).then_inc(sem("gate_ps"), 1)
            pe.wait_ge(sem("gate_out"), NCH)
            pe.wait_ge(sem("gla_decay0"), 1)

            def part(i, bank, w0):
                th, g = divmod(i, GT)
                for j in range(2):
                    a = th * QTOK + j * CH
                    ins = mm(PS[:, bank + j, :], GW[:, w0 + g * P:w0 + (g + 1) * P], XN[:, a:a + CH])
                return ins

            def read_out(i):
                th, g = divmod(i, GT)
                pe.wait_ge(sem("qs_done"), i + 1)
                if i == GT:
                    pe.wait_ge(sem("o_copied"), 1)
                for j in range(2):
                    ins = nc.tensor.matmul(PS[:, 6 + j, :], RED[:, g, :],
                                           tile(2)[:, (i % 2) * QTOK + j * CH:(i % 2) * QTOK + (j + 1) * CH],
                                           start=g == 0, stop=g == GT - 1)
                ins.then_inc(sem("o_part"), 1)
                if g == GT - 1:
                    pe.wait_ge(sem("o_part"), i + 1)
                    nc.tensor.matmul(PS[:, 5, 0:2], ident, ident[:, 0:2], start=True, stop=True).then_inc(sem("o_ps"), 1)

            for i in range(2 * GT):
                th, g = divmod(i, GT)
                if i >= 1:
                    pe.wait_ge(sem("v_out"), i)
                part(i, 2, GV).then_inc(sem("v_ps"), 1)
                if i >= 1:
                    pe.wait_ge(sem("qs_done"), i)
                part(i, 0, GK).then_inc(sem("k_ps"), 1)
                for j in range(2):
                    a = th * QTOK + j * CH
                    ins = mm(PS[:, 4 + j, :], SPR[0:HEADS * DK, g, :], tile(0)[0:HEADS * DK, a:a + CH])
                ins.then_inc(sem("decay_ps"), 1)
                pe.wait_ge(sem("kv_done"), i + 1)
                part(i, 0, GQ).then_inc(sem("q_ps"), 1)
                read_out(i)
            norm_pe(pe, 5)
            for c in range(NCH):
                pe.wait_ge(sem("o_gated"), c + 1)
                mm(PS[:, c, :], GW[:, GO:GO + P], ch(xs[:, 1, :], c)).then_inc(sem("attn_ps"), 1)
            moe(1)


_SHAPES = {
    "x": (P, TOK), "consts": (P, NCONST, P), "small": (P, SMALL), "w_in": (P, LAYERS, 4 * P),
    "w_x": (P, LAYERS, HALVES, XW), "w_dt": (DTR + 1, LAYERS, HALVES * P), "w_out": (P, LAYERS, HALVES, P),
    "sel": (96, NST * P), "momentum": (NST, NST * SPAN), "w1": (P, EXP, DFF), "w2": (P, EXP, FJ, P), "b2": (P, EXP * P),
    "w_gla": (P, GEND), "gla_consts": (P, 2 * GT * P + HEADS * DK),
}


def _constants():
    i = np.arange(P)
    c = np.zeros((P, NCONST, P), np.float32)
    c[:, C_ID] = np.eye(P)
    c[:, C_AVG] = 1.0 / D
    c[:, C_AVG8] = (i[:, None] // DV == i[None] // DV) / DV
    c[:, C_TRI] = i[:, None] <= i[None]
    c[:, C_ONE] = 1.0
    c[:, C_RAMP] = EXP - i % EXP
    lag = i[None, :SPAN] - i[:SPAN, None]
    c[:SPAN, C_MASK, :SPAN] = np.where(lag >= 0, BETA ** np.maximum(lag, 0).astype(np.float64), 0.0)
    momentum = np.eye(NST)[:, :, None] * BETA ** (1.0 + np.arange(SPAN))
    c[:, C_EBASE] = (i % EXP) * CAP - 1
    c[:, C_IOTA] = i[None]
    c[:, C_MASK, 64:64 + NBLK] = P * np.arange(NBLK)[None] + i[:, None] - FAR
    k, r = np.arange(96), np.arange(NST)
    sel = np.repeat((k[:, None] % 32 == NST + r[None]).astype(np.float32)[:, :, None], P, 2).reshape(96, -1)
    g, row = np.arange(GT), np.arange(P)
    head = g[:, None] * (P // (DK * DV)) + row[None] // (DK * DV)
    dk, dv = row // DV % DK, row % DV
    red = (head[:, :, None] * DV + dv[None, :, None] == i).astype(np.float32)
    spr = (head[:, None, :] * DK + dk[None, None, :] == i[None, :, None]).astype(np.float32)
    return (c, sel, momentum.astype(np.float32).reshape(NST, -1), red.transpose(1, 0, 2).reshape(P, -1),
            spr.transpose(1, 0, 2).reshape(P, -1))


def kernel(**inputs):
    import concourse.bacc as bacc
    from concourse.bass_utils import run_bass_kernel_spmd

    a = {k: np.asarray(v) for k, v in inputs.items()}
    ma = {k[len("L0_attn_a_"):]: v for k, v in a.items() if k.startswith("L0_attn_a_")}
    at = {k[len("L0_attn_b_"):]: v for k, v in a.items() if k.startswith("L0_attn_b_")}
    ff = {k[len("L0_ffn_"):]: v for k, v in a.items() if k.startswith("L0_ffn_")}
    consts, sel, momentum, red, spr = _constants()

    def halves(v):
        v = v.reshape(LAYERS, HALVES, P, -1)
        return v.transpose(2, 0, 1, 3).reshape(P, -1)

    small = np.concatenate([
        halves(ma["conv_w"]), halves(ma["conv_b"]), halves(ma["dt_b"]), halves(ma["Dp"]), ma["norm_w"].T,
        halves(ma["A_log"]), ff["b1"].reshape(EXP, FJ, P).transpose(2, 0, 1).reshape(P, -1),
        at["bg"].reshape(P, 1), ff["gate_w"].T], 1)
    xp = ma["x_proj_w"]
    bc = xp[:, DTR:]
    xw = np.concatenate([bc, bc, bc, xp[:, :DTR]], 1)
    rep_k = np.repeat(np.arange(HEADS * DK), DV)
    rep_v = (np.arange(HEADS)[:, None, None] * DV + np.zeros((1, DK, 1), int) + np.arange(DV)).reshape(-1)
    wg2 = np.zeros((P, HEADS * DK), np.float32)
    wg2[0:16] = at["Wg2"]
    arrays = {
        "x": ma["x"].reshape(TOK, D).T,
        "consts": consts,
        "small": small,
        "w_in": ma["in_proj_w"].transpose(2, 0, 1),
        "w_x": xw.reshape(LAYERS, XW, HALVES, P).transpose(3, 0, 2, 1),
        "w_dt": np.concatenate([ma["dt_w"].transpose(2, 0, 1), ma["dt_b"][None]], 0),
        "w_out": ma["out_w"].reshape(LAYERS, P, HALVES, P).transpose(3, 0, 2, 1),
        "sel": sel,
        "momentum": momentum,
        "w1": ff["w1"].transpose(1, 0, 2),
        "w2": ff["w2"].reshape(EXP, FJ, P, D).transpose(2, 0, 1, 3),
        "b2": np.repeat(ff["b2"].reshape(1, -1), P, 0),
        "w_gla": np.concatenate([at["Wq"][:, rep_k], at["Wk"][:, rep_k], at["Wv"][:, rep_v], at["Wg"], at["Wo"], at["Wg1"]], 1),
        "gla_consts": np.concatenate([red, spr, wg2], 1),
    }
    nc = bacc.Bacc("TRN2", target_bir_lowering=False, num_devices=1)
    io, host = {}, {}
    for name, shape in _SHAPES.items():
        host[f"in_{name}"] = np.ascontiguousarray(arrays[name])
        assert host[f"in_{name}"].shape == shape, (name, host[f"in_{name}"].shape, shape)
        io[name] = nc.dram_tensor(f"in_{name}", shape, F32, kind="ExternalInput").ap()
    io["out"] = nc.dram_tensor("out_x", (P, TOK), F32, kind="ExternalOutput").ap()
    build(nc, io)
    r = run_bass_kernel_spmd(nc, [host], core_ids=[0])
    return np.ascontiguousarray(r.results[0]["out_x"].T).reshape(B, SEQ, D)
```

```python
from contextlib import ExitStack

import numpy as np

import concourse.bass as bass
from concourse import mybir

P = 128
D = 128
B, SEQ = 4, 512
TOK = B * SEQ
NCH = 4
CH = TOK // NCH
LAYERS = 2
HALVES = 2
NST = 16
DTR = 8
KCONV = 4
BETA = 0.6
QTOK = 1024
SPAN = 64
UNITS = TOK // SPAN
UPB = SEQ // SPAN
GRP = 4
EXP, DFF, CAP = 8, 512, 320
SLOTS = EXP * CAP
NBLK = TOK // P
ST = SLOTS // P
GS = 4
NT = 3
FJ = DFF // P
HEADS, DK, DV = 16, 4, 8
GT = DK
EPS = 1e-5
FAR = 4096.0

F32 = mybir.dt.float32
BF16 = mybir.dt.bfloat16
U32 = mybir.dt.uint32
ALU = mybir.AluOpType
ACT = mybir.ActivationFunctionType
AX = mybir.AxisListType

SM = {}
_at = 0
for _name, _n in (("conv_w", LAYERS * HALVES * KCONV), ("conv_b", LAYERS * HALVES),
                  ("dp", LAYERS * HALVES), ("norm_w", LAYERS), ("a_log", LAYERS * HALVES * NST),
                  ("b1", EXP * FJ), ("bg", 1), ("gate", EXP)):
    SM[_name] = _at
    _at += _n
SMALL = _at
C_ID, C_AVG, C_AVG8, C_TRI, C_ONE, C_RAMP, C_EBASE, C_MASK, C_IOTA, C_CENTRE, C_CENTRE8 = range(11)
NCONST = 11
XW = 3 * 2 * NST + DTR
GQ, GK, GV, GG, GO, GG1, GEND = 0, 512, 1024, 1152, 1280, 1408, 1424
NORMS = [(True, None), (False, 0), (False, 1), (True, None), (True, None)]


def pieces(e):
    a = e * CAP
    out = []
    while a < (e + 1) * CAP:
        n = min(P - a % P, (e + 1) * CAP - a)
        out.append((a // P, a % P, n, a - e * CAP))
        a += n
    return out


def centred_before(k):
    return sum(c for c, _ in NORMS[:k])


def build(nc, io):
    with ExitStack() as ctx:
        def sb(name, shape, dt=F32):
            return ctx.enter_context(nc.sbuf_tensor(name, shape, dt))

        sems = {}

        def sem(name):
            if name not in sems:
                sems[name] = ctx.enter_context(nc.semaphore(name))
            return sems[name]

        X = sb("X", [P, TOK])
        F = sb("F", [P, 8 * TOK])
        BIG = sb("BIG", [P, 12 * TOK])
        STK = sb("STK", [P, TOK], BF16)
        SEL = sb("SEL", [P, NST, P], BF16)
        AUX = sb("AUX", [P, TOK])
        WIN = sb("WIN", [P, LAYERS, 4 * P])
        XPW = sb("XPW", [P, LAYERS, HALVES, XW])
        DTW = sb("DTW", [P, LAYERS, HALVES * P])
        WOUT = sb("WOUT", [P, LAYERS, HALVES, P])
        SMT = sb("SMT", [P, SMALL])
        CST = sb("CST", [P, NCONST, P])
        NEGA = sb("NEGA", [P, LAYERS * HALVES, NST])
        RTS = sb("RTS", [P, 9, NBLK])
        IDX = sb("IDX", [P, ST], U32)
        A0 = sb("A0", [P, HALVES * NST * (UNITS + 1)])
        PS = ctx.enter_context(nc.psum_tensor("PS", [P, 8, CH], F32))

        ident = CST[:, C_ID, :]
        avg_all = CST[:, C_AVG, :]

        W1 = BIG[:, 0:2 * TOK].rearrange("p (e f) -> p e f", e=EXP)
        W2 = BIG[:, 2 * TOK:4 * TOK].rearrange("p (e j d) -> p e j d", e=EXP, j=FJ)
        RT = AUX[:, 0:11 * P].rearrange("p (i d) -> p i d", d=P)

        def tile(k):
            return BIG[:, (4 + k) * TOK:(5 + k) * TOK]

        XN = tile(7)

        def small(name, k=0):
            return SMT[:, SM[name] + k:SM[name] + k + 1]

        def ch(ap, c):
            return ap[:, c * CH:(c + 1) * CH]

        def flat(ap):
            return ap.rearrange("p a b -> p (a b)")

        xs = F[:, 0:2 * TOK].rearrange("p (m t) -> p m t", m=HALVES)
        zs = F[:, 2 * TOK:4 * TOK].rearrange("p (m t) -> p m t", m=HALVES)
        delta = F[:, 4 * TOK:6 * TOK].rearrange("p (m t) -> p m t", m=HALVES)
        Y = F[:, 6 * TOK:8 * TOK].rearrange("p (m t) -> p m t", m=HALVES)

        def slot(par, k):
            return BIG[:, (9 * par + k) * 1024:(9 * par + k + 1) * 1024].rearrange("p (m t) -> p m t", m=HALVES)

        def xpad(par):
            return BIG[:, (9 * par + 7) * 1024:(9 * par + 7) * 1024 + HALVES * (SEQ + 3)].rearrange(
                "p (m t) -> p m t", m=HALVES)

        def split_rest(par):
            return slot(par, 6)[0:96, 0, :]

        def split_mid(par):
            return slot(par, 5)[0:96, 0, :].bitcast(BF16)[:, 0:CH]

        def b_rows(par):
            return slot(par, 5)[0:NST, 1, :]

        def rank(par):
            return slot(par, 6)[:, 1, :]

        dec = [BIG[:, g * 8192:(g + 1) * 8192].rearrange("p (m j n t) -> p m j n t", m=HALVES, j=GRP, n=NST) for g in (0, 1)]
        state = BIG[:, 16384:18432].rearrange("p (m n t) -> p m n t", m=HALVES, n=NST)
        prod = [BIG[:, 18432 + k * 2048:20480 + k * 2048].rearrange("p (m n t) -> p m n t", m=HALVES, n=NST) for k in (0, 1)]
        rbm = [BIG[:, 22528 + k * 1024:23552 + k * 1024] for k in (0, 1)]
        ut = [AUX[:, k * 256:(k + 1) * 256] for k in (0, 1)]
        us = [AUX[:, 512 + k * 128:640 + k * 128].rearrange("p (m t) -> p m t", m=HALVES) for k in (0, 1)]
        bt = AUX[0:SPAN, 768:768 + UNITS * NST].rearrange("p (i n) -> p i n", n=NST)
        carry = AUX[:, 1280:1312].rearrange("p (m n) -> p m n", m=HALVES)
        zero_w = AUX[0:SPAN + NST, 1312:1328]
        one_e = BIG[:, 9216:13312].rearrange("p (m t) -> p m t", m=HALVES)
        above = BIG[:, 18432:22528].rearrange("p (m t) -> p m t", m=HALVES)
        a0 = A0[:, :].rearrange("p (m n i) -> p m n i", m=HALVES, n=NST)
        rows_in = F[:, 0:SLOTS].rearrange("p (k d) -> p k d", d=P)
        rows_out = F[:, 3072:3072 + SLOTS].rearrange("p (k d) -> p k d", d=P)
        xdisp = F[:, 6144:6144 + SLOTS]
        hid = [F[:, 8704 + k * FJ * CAP:8704 + (k + 1) * FJ * CAP].rearrange("p (j s) -> p j s", j=FJ) for k in (0, 1)]
        xtok = F[:, 11264:11264 + TOK].rearrange("p (k d) -> p k d", d=P)
        fetched = F[:, 13312:13312 + TOK].rearrange("p (k d) -> p k d", d=P)
        diag = tile(3).rearrange("p (k d) -> p k d", d=P)
        row_hot = tile(0)[:, 0:TOK // 2].bitcast(BF16).rearrange("p (k d) -> p k d", d=P)
        passed = RT[:, 0:3, :].rearrange("p a b -> p (a b)")[:, 0:NBLK * (ST + 1)].rearrange("p (b h) -> p b h", h=ST + 1)
        tile_hot = RT[:, 3:6, :].rearrange("p a b -> p (a b)")[:, 0:NBLK * ST].bitcast(BF16).rearrange(
            "p (b i h) -> p b i h", i=2, h=ST)
        digits = CST[:, C_MASK, 64:64 + 2 * NBLK].rearrange("p (b i) -> p b i", i=2)
        centred = tile(4)
        sq_moe = tile(5)
        B2R = STK[:, :].bitcast(F32).rearrange("p (e d) -> p e d", e=EXP)
        GC = F[:, 8192:8192 + GT * P + HEADS * DK]
        GW = F[:, 9472:9472 + GEND]
        SPR = GC[:, 0:GT * P].rearrange("p (g m) -> p g m", g=GT)
        WG2 = GC[:, GT * P:GT * P + HEADS * DK]

        token_dram = [nc.dram_tensor(f"tokens{k}", (TOK, D), F32, kind="Internal").ap() for k in (0, 1)]
        result_dram = [nc.dram_tensor(f"results{k}", (TOK, D), F32, kind="Internal").ap() for k in (0, 1)]

        def norm_input(k, c):
            if k == 0:
                return [(sem(f"x_loaded{c}"), 16)]
            if k == 1:
                return [(sem("norm_out"), c + 1)]
            if k == 2:
                return [(sem("outproj_added"), c + 1)]
            if k == 3:
                return [(sem("moe_added"), c + 1)]
            return [(sem("summed"), (GT - 1) * (c // 2 + 1))]

        def norm_buffers(k):
            src = tile(6) if k == 4 else X[:, :]
            dst = X[:, :] if k == 0 else (tile(6) if k == 4 else XN[:, :])
            t = {1: 4, 2: 0}.get(k, 3)
            return src, dst, tile(t + 1), tile(t + 2)

        def norm_pe(pe, k):
            src, _, sq, _ = norm_buffers(k)
            avg = CST[:, C_AVG8, :] if k == 4 else avg_all
            centring = CST[:, C_CENTRE8 if k == 4 else C_CENTRE, :]
            if NORMS[k][0]:
                for c in range(NCH):
                    for s, v in norm_input(k, c):
                        pe.wait_ge(s, v)
                    pe.matmul(PS[:, c, :], centring, ch(src, c), start=True, stop=True).then_inc(sem("centred"), 1)
            if k == 0:
                pe.wait_ge(sem("consts_loaded"), 32)
            for c in range(NCH):
                pe.wait_ge(sem("squared"), NCH * k + c + 1)
                pe.matmul(PS[:, 4 + c, :], avg, ch(sq, c), start=True, stop=True).then_inc(sem("var_ps"), 1)

        def norm_act(act, k):
            src, _, sq, rs = norm_buffers(k)
            for c in range(NCH):
                if NORMS[k][0]:
                    act.wait_ge(sem("centred"), NCH * centred_before(k) + c + 1)
                    a = PS[:, c, :]
                else:
                    for s, v in norm_input(k, c):
                        act.wait_ge(s, v)
                    a = ch(src, c)
                nc.scalar.activation(ch(sq, c), a, ACT.Square).then_inc(sem("squared"), 1)
            for c in range(NCH):
                act.wait_ge(sem("var_ps"), NCH * k + c + 1)
                nc.scalar.activation(ch(rs, c), PS[:, 4 + c, :], ACT.Ln, bias=eps_col).then_inc(sem("log_var"), 1)
            for c in range(NCH):
                act.wait_ge(sem("log_var"), NCH * k + c + 1)
                nc.scalar.activation(ch(rs, c), ch(rs, c), ACT.Exp, scale=-0.5).then_inc(sem("rstd"), 1)

        def norm_dve(dve, k):
            src, dst, _, rs = norm_buffers(k)
            centre, w = NORMS[k]
            for c in range(NCH):
                dve.wait_ge(sem("rstd"), NCH * k + c + 1)
                if centre:
                    nc.vector.tensor_tensor(ch(dst, c), PS[:, c, :], ch(rs, c), ALU.mult).then_inc(sem("norm_out"), 1)
                else:
                    nc.vector.scalar_tensor_tensor(out=ch(dst, c), in0=ch(src, c), scalar=small("norm_w", w),
                                                   in1=ch(rs, c), op0=ALU.mult, op1=ALU.mult).then_inc(sem("norm_out"), 1)

        def rows_until(k, h):
            return NT * EXP * k + sum(1 for e in range(EXP) for tl, _, _, _ in pieces(e) if tl <= h)

        def norm_done(k, c=NCH - 1):
            return NCH * k + c + 1

        eps_tile = sb("EPSC", [P, 2])
        eps_col = eps_tile[:, 0:1]

        block = ctx.enter_context(nc.Block())

        @block.sync
        def _(sp):
            sp.dma_start(CST[:, C_CENTRE, :], io["consts"][:, C_CENTRE, :]).then_inc(sem("centring_loaded"), 16)
            for c in range(NCH):
                sp.dma_start(ch(X[:, :], c), io["x"][:, c * CH:(c + 1) * CH]).then_inc(sem(f"x_loaded{c}"), 16)
            sp.dma_start(CST[:, 0:C_CENTRE, :], io["consts"][:, 0:C_CENTRE, :]).then_inc(sem("consts_loaded"), 16)
            sp.dma_start(CST[:, C_CENTRE8, :], io["consts"][:, C_CENTRE8, :]).then_inc(sem("consts_loaded"), 16)
            sp.dma_start(SMT[:, :], io["small"]).then_inc(sem("small_loaded"), 16)
            sp.dma_start(WIN[:, :, :], io["w_in"]).then_inc(sem("mamba_loaded"), 16)
            sp.dma_start(XPW[:, :, :, :], io["w_x"]).then_inc(sem("mamba_loaded"), 16)
            sp.dma_start(DTW[96:96 + DTR + 1, :, :], io["w_dt"]).then_inc(sem("mamba_loaded"), 16)
            sp.dma_start(WOUT[:, :, :, :], io["w_out"]).then_inc(sem("mamba_loaded"), 16)
            sp.dma_start(F[0:96, 0:NST * P], io["sel"]).then_inc(sem("sel_loaded"), 16)
            sp.wait_ge(sem("zeros"), 1)
            for k in (0, 1):
                sp.dma_start(result_dram[k].rearrange("(p r) d -> p (r d)", p=P),
                             F[:, 6144:6144 + TOK]).then_inc(sem("results_zeroed"), 16)
            for L in range(LAYERS):
                sp.wait_ge(sem("z_ps"), HALVES * NCH * (L + 1))
                for k in (0, 1):
                    sp.dma_start(rbm[k][SPAN:P, :], io["momentum"]).then_inc(sem("momentum_rows"), 16)
            sp.wait_ge(sem("gated"), LAYERS * UNITS)
            sp.wait_ge(sem("state1"), LAYERS * UNITS)
            sp.dma_start(XN[:, :], io["x"]).then_inc(sem("x_again"), 16)
            sp.dma_start(W1[:, :, :], io["w1"]).then_inc(sem("experts_loaded"), 16)
            sp.dma_start(W2[:, :, :, :], io["w2"]).then_inc(sem("experts_loaded"), 16)
            sp.dma_start(flat(B2R), io["b2"]).then_inc(sem("b2_loaded"), 16)
            for k in (0, 1):
                for c in range(NCH):
                    sp.wait_ge(sem("token_rows"), NBLK * k + 4 * (c + 1))
                    sp.dma_start(token_dram[k][c * CH:(c + 1) * CH, :].rearrange("(j p) d -> p j d", p=P),
                                 xtok[:, 4 * c:4 * c + 4, :]).then_inc(sem("tokens_stored"), 16)
                sp.wait_ge(sem("scattered"), 16 * ST * (k + 1))
                for c in range(NCH):
                    sp.dma_start(fetched[:, 4 * c:4 * c + 4, :],
                                 result_dram[k][c * CH:(c + 1) * CH, :].rearrange("(j p) d -> p j d", p=P)
                                 ).then_inc(sem(f"fetched{c}"), 16)
                if k == 0:
                    sp.dma_start(GW, io["w_gla"]).then_inc(sem("gla_loaded"), 16)
                    sp.dma_start(GC, io["gla_consts"]).then_inc(sem("gla_loaded"), 16)
            for c in range(NCH):
                sp.wait_ge(sem("moe_added"), NCH + c + 1)
                sp.dma_start(io["out"][:, c * CH:(c + 1) * CH], ch(X[:, :], c)).then_inc(sem("out_stored"), 16)
            sp.wait_ge(sem("tokens_stored"), 16 * NCH * 2)
            sp.wait_ge(sem("results_zeroed"), 32)
            sp.wait_ge(sem("scattered"), 16 * ST * 2)
            sp.wait_ge(sem("out_stored"), 16 * NCH)

        @block.gpsimd
        def _(pool):
            nc.gpsimd.memset(eps_tile[:, :], EPS).then_inc(sem("eps_set"), 1)
            nc.gpsimd.memset(F[:, 6144:6144 + TOK], 0.0).then_inc(sem("zeros"), 1)
            pool.wait_ge(sem("sel_loaded"), 16)
            nc.gpsimd.tensor_copy(flat(SEL[0:96, :, :]), F[0:96, 0:NST * P]).then_inc(sem("sel_ready"), 1)
            for L in range(LAYERS):
                if L == 0:
                    pool.wait_ge(sem("norm_out"), norm_done(0))
                else:
                    pool.wait_ge(sem("state1"), L * UNITS)
                for par in (0, 1):
                    nc.gpsimd.memset(xpad(par)[:, :, 0:KCONV - 1], 0.0).then_inc(sem("pads_set"), 1)
                    pool.wait_ge(sem("pads_set"), 4 * L + 2 * par + 1)
                    nc.gpsimd.memset(rank(par)[96:P, :], 1.0).then_inc(sem("pads_set"), 1)
                    pool.wait_ge(sem("pads_set"), 4 * L + 2 * par + 2)
                if L == 0:
                    nc.gpsimd.memset(zero_w, 0.0).then_inc(sem("zero_set"), 1)
                    pool.wait_ge(sem("zero_set"), 1)
                    nc.gpsimd.memset(AUX[SPAN:P, 0:512], 0.0).then_inc(sem("zero_set"), 1)
                    pool.wait_ge(sem("zero_set"), 2)

                def split(c):
                    q = NCH * L + c
                    pool.wait_ge(sem("split_rest"), q + 1)
                    rest, mid = split_rest(c % 2), split_mid(c % 2)
                    part = slice(c * CH, (c + 1) * CH)
                    nc.gpsimd.tensor_copy(mid, rest).then_inc(sem("split_mid"), 1)
                    pool.wait_ge(sem("split_mid"), q + 1)
                    nc.gpsimd.tensor_copy(STK[32:64, part], mid[32:64, :]).then_inc(sem("split_done"), 1)
                    pool.wait_ge(sem("split_done"), 2 * q + 1)
                    nc.gpsimd.tensor_tensor(STK[64:96, part], rest[64:96, :], mid[64:96, :], ALU.subtract).then_inc(sem("split_done"), 1)
                    pool.wait_ge(sem("split_done"), 2 * q + 2)

                def sp_rest(c):
                    part = slice(c * CH, (c + 1) * CH)
                    pool.wait_ge(sem("sp_low"), NCH * L + c + 1)
                    pool.wait_ge(sem("sp_max"), NCH * L + c + 1)
                    nc.gpsimd.tensor_tensor(above[:, :, part], above[:, :, part], delta[:, :, part], ALU.subtract).then_inc(sem("sp_rest"), 1)

                for c in range(NCH - 1):
                    split(c)
                for c in range(NCH - 1):
                    sp_rest(c)
                split(NCH - 1)
                sp_rest(NCH - 1)
                U0 = L * UNITS

                def rows_of_b(s, base):
                    if not (isinstance(base, int) and base + s < 2):
                        pool.wait_ge(sem("v_ps"), U0 + base + s - 1)
                        pool.wait_ge(sem("ut_ps"), U0 + base + s)
                    row = bt[:, base + s, :] if isinstance(base, int) else bt[:, bass.ds(base + s, 1), :].rearrange("p a n -> p (a n)")
                    nc.gpsimd.tensor_tensor(rbm[s % 2][0:SPAN, :].rearrange("p (n t) -> p n t", n=NST),
                                            CST[0:SPAN, C_MASK, 0:SPAN].unsqueeze(1).to_broadcast([SPAN, NST, SPAN]),
                                            row.unsqueeze(2).to_broadcast([SPAN, NST, SPAN]),
                                            ALU.mult).then_inc(sem("rb_ready"), 1)

                def fold(s, base):
                    p = prod[s % 2]
                    pool.wait_ge(sem("readout"), U0 + base + s + 1)
                    for h in (8, 4):
                        nc.gpsimd.tensor_tensor(p[:, :, 0:h, :], p[:, :, 0:h, :], p[:, :, h:2 * h, :], ALU.add
                                                ).then_inc(sem("folded"), 1)
                        if h == 8:
                            pool.wait_ge(sem("folded"), 2 * (U0 + base + s) + 1)

                def pool_slot(s, base, more=True):
                    if more:
                        rows_of_b(s + 2, base)
                    if not (isinstance(base, int) and base + s == 0):
                        fold(s - 1, base)

                pool.wait_ge(sem("bt_ready"), NCH * (L + 1))
                pool.wait_ge(sem("z_ps"), HALVES * NCH * (L + 1))
                for s in (0, 1):
                    rows_of_b(s, 0)
                pool_slot(0, 0)
                pool_slot(1, 0)
                with pool.Fori(0, B - 1) as b:
                    for s in range(2, UPB + 2):
                        pool_slot(s, UPB * b)
                for s in range(2, UPB):
                    pool_slot(s, UNITS - UPB, s + 2 < UPB)
                fold(UPB - 1, UNITS - UPB)

            def sum_over_dk(th):
                o = tile(6)[:, th * QTOK:(th + 1) * QTOK]
                for g in range(1, GT):
                    i = GT * th + g
                    pool.wait_ge(sem("qs_done"), i + 1)
                    if g > 1:
                        pool.wait_ge(sem("summed"), (GT - 1) * th + g - 1)
                    first = tile(2)[:, 0:QTOK] if g == 1 else o
                    nc.gpsimd.tensor_tensor(o, first, tile(2)[:, (i % 2) * QTOK:(i % 2 + 1) * QTOK], ALU.add).then_inc(sem("summed"), 1)

            for k in (0, 1):
                if k:
                    sum_over_dk(0)
                    sum_over_dk(1)
                if k == 0:
                    pool.wait_ge(sem("gated"), LAYERS * UNITS)
                else:
                    pool.wait_ge(sem("attn_ps"), NCH)
                nc.gpsimd.memset(F[:, 0:SLOTS], 0.0).then_inc(sem("rows_zeroed"), 1)
                pool.wait_ge(sem("rows_zeroed"), k + 1)
                pool.wait_ge(sem("tokens_stored"), 16 * NCH * (k + 1))
                pool.wait_ge(sem("indices_ready"), k + 1)
                for h in range(ST):
                    nc.gpsimd.indirect_dma_start(
                        out=rows_in[:, h, :], out_offset=None,
                        in_=token_dram[k], in_offset=bass.IndirectOffsetOnAxis(ap=IDX[:, h:h + 1], axis=0),
                        bounds_check=TOK - 1, oob_is_err=False).then_inc(sem(f"gathered{h // GS}"), 16)
                pool.wait_ge(sem("results_zeroed"), 32)
                for h in range(ST):
                    pool.wait_ge(sem("rows_made"), rows_until(k, h))
                    nc.gpsimd.indirect_dma_start(
                        out=result_dram[k], out_offset=bass.IndirectOffsetOnAxis(ap=IDX[:, h:h + 1], axis=0),
                        in_=rows_out[:, h, :], in_offset=None, bounds_check=TOK - 1, oob_is_err=False
                    ).then_inc(sem("scattered"), 16)

        @block.scalar
        def _(act):
            chain = [0]

            def link(ins):
                chain[0] += 1
                ins.then_inc(sem("act_chain"), 1)
                act.wait_ge(sem("act_chain"), chain[0])

            act.wait_ge(sem("eps_set"), 1)
            act.wait_ge(sem("small_loaded"), 16)
            al = SM["a_log"]
            nc.scalar.activation(flat(NEGA[:, :, :]), SMT[:, al:al + LAYERS * HALVES * NST], ACT.Exp).then_inc(sem("a_exp"), 1)
            norm_act(act, 0)
            for L in range(LAYERS):
                norm_act(act, 1 + L)
                act.wait_ge(sem("pads_set"), 4 * (L + 1))
                if L == 0:
                    act.wait_ge(sem("results_zeroed"), 32)
                    act.wait_ge(sem("sel_ready"), 1)

                def inner_out(c):
                    q = NCH * L + c
                    for m in range(HALVES):
                        act.wait_ge(sem("inner_ps"), HALVES * q + m + 1)
                        if c >= 2:
                            act.wait_ge(sem("conv_done"), q - 1)
                        nc.scalar.activation(xpad(c % 2)[:, m, KCONV - 1:], PS[:, m, :], ACT.Copy).then_inc(sem("xb_out"), 1)

                def gate_out(c):
                    for m in range(HALVES):
                        act.wait_ge(sem("z_ps"), HALVES * (NCH * L + c) + m + 1)
                        nc.scalar.activation(ch(zs[:, m, :], c), PS[:, HALVES + m, :], ACT.Silu).then_inc(sem("z_out"), 1)

                def conv_out(c):
                    act.wait_ge(sem("conv_done"), NCH * L + c + 1)
                    nc.scalar.activation(xs[:, :, c * CH:(c + 1) * CH], slot(c % 2, 0), ACT.Silu).then_inc(sem("xs_ready"), 1)

                def small_out(c):
                    q = NCH * L + c
                    act.wait_ge(sem("xproj_ps"), q + 1)
                    nc.scalar.activation(rank(c % 2)[96:96 + DTR, :], PS[96:96 + DTR, 4, :], ACT.Copy).then_inc(sem("rank_ready"), 1)
                    nc.scalar.activation(b_rows(c % 2), PS[0:NST, 4, :], ACT.Copy).then_inc(sem("b_rows"), 1)

                def bt_out(c):
                    q = NCH * L + c
                    act.wait_ge(sem("bt_ps"), q + 1)
                    nc.scalar.activation(flat(bt[:, UPB * c:UPB * (c + 1), :]), PS[0:SPAN, 5, 0:UPB * NST], ACT.Copy
                                         ).then_inc(sem("bt_ready"), 1)

                def sp_abs(c):
                    act.wait_ge(sem("dt_ps"), NCH * L + c + 1)
                    nc.scalar.activation(delta[:, :, c * CH:(c + 1) * CH], PS[:, 6:8, :], ACT.Abs).then_inc(sem("sp_abs"), 1)

                def sp_max(c):
                    nc.scalar.activation(above[:, :, c * CH:(c + 1) * CH], PS[:, 6:8, :], ACT.Relu).then_inc(sem("sp_max"), 1)

                def sp_exp(c):
                    part = slice(c * CH, (c + 1) * CH)
                    act.wait_ge(sem("sp_abs"), NCH * L + c + 1)
                    nc.scalar.activation(delta[:, :, part], delta[:, :, part], ACT.Exp, scale=-1.0).then_inc(sem("sp_e"), 1)

                def skip_out(c):
                    act.wait_ge(sem("xs_ready"), NCH * L + c + 1)
                    for m in range(HALVES):
                        nc.scalar.activation(Y[:, m, c * CH:(c + 1) * CH], xs[:, m, c * CH:(c + 1) * CH], ACT.Copy,
                                             scale=small("dp", HALVES * L + m)).then_inc(sem("dx_ready"), 1)

                for c in range(NCH):
                    inner_out(c)
                    gate_out(c)
                    if c > 0:
                        small_out(c - 1)
                        sp_abs(c - 1)
                        sp_max(c - 1)
                        bt_out(c - 1)
                        skip_out(c - 1)
                    conv_out(c)
                for c in range(NCH - 1):
                    sp_exp(c)
                small_out(NCH - 1)
                sp_abs(NCH - 1)
                sp_exp(NCH - 1)
                bt_out(NCH - 1)
                for c in range(NCH):
                    part = slice(c * CH, (c + 1) * CH)
                    act.wait_ge(sem("sp_u"), NCH * L + c + 1)
                    act.wait_ge(sem("sp_low"), NCH * L + c + 1)
                    nc.scalar.activation(one_e[:, :, part], one_e[:, :, part], ACT.Ln).then_inc(sem("sp_log"), 1)
                    if c == 0:
                        sp_max(NCH - 1)
                act.wait_ge(sem("dec_zeroed"), 2 * L + 1)
                act.wait_ge(sem("delta_ready"), NCH * L + 1)
                U0 = L * UNITS

                def decays(gpar, part, tok0):
                    for j in range(8):
                        m, n = divmod(8 * part + j, NST)
                        sl = slice(tok0, tok0 + GRP * SPAN) if isinstance(tok0, int) else bass.ds(tok0, GRP * SPAN)
                        ins = nc.scalar.activation(
                            dec[gpar][:, m, :, n, 1:SPAN],
                            delta[:, m, sl].rearrange("p (j t) -> p j t", j=GRP)[:, :, 1:SPAN],
                            ACT.Exp, scale=NEGA[:, HALVES * L + m, n:n + 1])
                    if part == GRP - 1:
                        ins.then_inc(sem("decays_ready"), 1)

                def unit_inputs(s, base):
                    at = (base + s) * SPAN
                    sl = slice(at, at + SPAN) if isinstance(at, int) else bass.ds(at, SPAN)
                    nc.scalar.activation(us[s % 2], xs[:, :, sl], ACT.Copy).then_inc(sem("us_ready"), 1)

                def act_slot(s, base, group=True, turned=True, more=True):
                    if turned:
                        act.wait_ge(sem("ut_ps"), U0 + base + s + 3)
                        act.wait_ge(sem("v_ps"), U0 + base + s + 1)
                        nc.scalar.activation(ut[s % 2][0:SPAN + NST, :], PS[0:SPAN + NST, 6, 0:256], ACT.Copy).then_inc(sem("ut_out"), 1)
                        if more:
                            unit_inputs(s + 3, base)
                    if group:
                        g = s // GRP + 1
                        if s % GRP == 0 and not (isinstance(base, int) and base + s < GRP):
                            act.wait_ge(sem("state1"), U0 + base + s)
                        decays(g % 2, s % GRP, base * SPAN + g * GRP * SPAN)

                act.wait_ge(sem("zero_set"), 2)
                act.wait_ge(sem("inputs_scaled"), NCH * L + 1)
                unit_inputs(0, 0)
                unit_inputs(1, 0)
                for part in range(GRP):
                    decays(0, part, 0)
                    if part == 0:
                        skip_out(NCH - 1)
                    if part < 2:
                        act.wait_ge(sem("ut_ps"), U0 + part + 1)
                        nc.scalar.activation(ut[part][0:SPAN + NST, :], PS[0:SPAN + NST, 6, 0:256], ACT.Copy).then_inc(sem("ut_out"), 1)
                        if part == 0:
                            unit_inputs(2, 0)
                    if part == 2:
                        act.wait_ge(sem("dec_zeroed"), 2 * L + 2)
                        act.wait_ge(sem("a0_arg"), L + 1)
                        nc.scalar.activation(a0[:, :, :, 0:UNITS], a0[:, :, :, 0:UNITS], ACT.Exp).then_inc(sem("a0_exp"), 1)
                act.wait_ge(sem("inputs_scaled"), NCH * (L + 1))
                act_slot(0, 0)
                act_slot(1, 0)
                with act.Fori(0, B - 1) as b:
                    for s in range(2, UPB + 2):
                        act_slot(s, UPB * b)
                for s in range(2, UPB):
                    act_slot(s, UNITS - UPB, s < GRP, s + 2 < UPB, s + 3 < UPB)

            def moe(k):
                for c in range(NCH):
                    act.wait_ge(sem("centred_ps"), NCH * k + c + 1)
                    nc.scalar.activation(ch(sq_moe, c), PS[:, c, :], ACT.Square).then_inc(sem("moe_squared"), 1)
                act.wait_ge(sem("token_var_ps"), k + 1)
                nc.scalar.activation(RTS[:, 8, :], PS[:, 3, 256:256 + NBLK], ACT.Sqrt, bias=eps_col).then_inc(sem("token_std"), 1)
                act.wait_ge(sem("token_rstd"), k + 1)
                for t in range(NBLK):
                    act.wait_ge(sem("rows_ps"), NCH * k + t // 4 + 1)
                    nc.scalar.activation(xtok[:, t, :], PS[:, 4 + t // 4, t % 4 * P:(t % 4 + 1) * P], ACT.Copy,
                                         scale=RTS[:, 8, t:t + 1]).then_inc(sem("token_rows"), 1)
                act.wait_ge(sem("shifted"), k + 1)
                nc.scalar.activation(RT[:, 9, :], RT[:, 9, :], ACT.Exp).then_inc(sem("route_exp"), 1)
                for e in range(EXP):
                    for j in range(FJ):
                        act.wait_ge(sem("hid_ps"), FJ * (EXP * k + e) + j + 1)
                        if e >= 2 and j == 0:
                            act.wait_ge(sem("rows_made"), NT * (EXP * k + e - 1))
                        nc.scalar.activation(hid[e % 2][:, j, :], PS[:, 2 + j, 0:CAP], ACT.Relu,
                                             bias=small("b1", FJ * e + j)).then_inc(sem("hidden"), 1)

            moe(0)
            norm_act(act, 3)
            act.wait_ge(sem("gla_loaded"), 32)
            act.wait_ge(sem("rank16_ps"), 2)
            nc.scalar.activation(tile(5)[0:16, 0:QTOK], flat(PS[0:16, 0:2, :]), ACT.Copy).then_inc(sem("rank16"), 1)
            act.wait_ge(sem("kg_ps"), NCH)
            gates = tile(0)[:, 0:QTOK]
            link(nc.scalar.activation(gates, flat(PS[:, 4:6, :]), ACT.Abs))
            link(nc.scalar.activation(gates, gates, ACT.Exp, scale=-1.0))
            nc.scalar.activation(tile(1)[:, 0:QTOK], gates, ACT.Ln, bias=1.0).then_inc(sem("kg_log"), 1)

            def copy_v(th):
                act.wait_ge(sem("values_ps"), th + 1)
                nc.scalar.activation(zs[:, 0, th * QTOK:(th + 1) * QTOK], flat(PS[:, 6:8, :]), ACT.Copy).then_inc(sem("v_out"), 1)

            copy_v(0)
            act.wait_ge(sem("log_gate"), 1)
            nc.scalar.activation(gates, tile(2)[:, 0:QTOK], ACT.Exp, scale=1.0 / 16).then_inc(sem("gla_decay"), 1)
            copy_v(1)
            for c in range(NCH):
                act.wait_ge(sem("gate_ps"), c + 1)
                nc.scalar.activation(ch(xs[:, 0, :], c), PS[:, 6 + c % 2, :], ACT.Silu, bias=small("bg")).then_inc(sem("gate_out"), 1)
            norm_act(act, 4)
            moe(1)

        @block.vector
        def _(dve):
            chain = [0]

            def link(ins):
                chain[0] += 1
                ins.then_inc(sem("dve_chain"), 1)
                dve.wait_ge(sem("dve_chain"), chain[0])

            taps = [0]
            dve.wait_ge(sem("a_exp"), 1)
            nc.vector.tensor_scalar(flat(NEGA[:, :, :]), flat(NEGA[:, :, :]), -1.0, None, ALU.mult).then_inc(sem("nega"), 1)
            norm_dve(dve, 0)
            for L in range(LAYERS):
                norm_dve(dve, 1 + L)

                def scale_inputs(c):
                    part = slice(c * CH, (c + 1) * CH)
                    dve.wait_ge(sem("delta_ready"), NCH * L + c + 1)
                    dve.wait_ge(sem("dx_ready"), HALVES * (NCH * L + c + 1))
                    nc.vector.tensor_tensor(xs[:, :, part], xs[:, :, part], delta[:, :, part], ALU.mult).then_inc(sem("inputs_scaled"), 1)

                def sp_low(c):
                    q = NCH * L + c
                    part = slice(c * CH, (c + 1) * CH)
                    dve.wait_ge(sem("sp_e"), q + 1)
                    nc.vector.tensor_scalar(one_e[:, :, part], delta[:, :, part], 1.0, None, ALU.add).then_inc(sem("sp_u"), 1)
                    dve.wait_ge(sem("sp_u"), q + 1)
                    nc.vector.scalar_tensor_tensor(out=delta[:, :, part], in0=one_e[:, :, part], scalar=-1.0, in1=delta[:, :, part],
                                                   op0=ALU.add, op1=ALU.subtract).then_inc(sem("sp_low"), 1)

                for c in range(NCH + 1):
                    if c == NCH:
                        dve.wait_ge(sem("split_done"), 2 * (NCH * L + NCH - 1))
                        dve.wait_ge(sem("xs_ready"), NCH * (L + 1))
                        dve.wait_ge(sem("dt_ps"), NCH * (L + 1) - 1)
                        nc.vector.memset(BIG[:, 0:8192].rearrange("p (s t) -> p s t", t=SPAN)[:, :, 0:1], 0.0).then_inc(sem("dec_zeroed"), 1)
                        nc.vector.memset(carry, 0.0).then_inc(sem("carried"), 1)
                        for done in range(NCH - 1):
                            sp_low(done)
                    if c < NCH:
                        q = NCH * L + c
                        dve.wait_ge(sem("pads_set"), 4 * (L + 1))
                        if c >= 2:
                            dve.wait_ge(sem("xs_ready"), q - 1)
                        for j in range(KCONV):
                            for m in range(HALVES):
                                if j == 0:
                                    dve.wait_ge(sem("xb_out"), HALVES * q + m + 1)
                                tap = xpad(c % 2)[:, m, j:j + SEQ]
                                acc = slot(c % 2, 0)[:, m, :]
                                w = small("conv_w", KCONV * (HALVES * L + m) + j)
                                if j == 0:
                                    ins = nc.vector.tensor_scalar(acc, tap, w, small("conv_b", HALVES * L + m), ALU.mult, ALU.add)
                                else:
                                    ins = nc.vector.scalar_tensor_tensor(out=acc, in0=tap, scalar=w, in1=acc, op0=ALU.mult, op1=ALU.add)
                                if j < KCONV - 1:
                                    taps[0] += 1
                                    ins.then_inc(sem("taps"), 1)
                            if j < KCONV - 1:
                                dve.wait_ge(sem("taps"), taps[0])
                        ins.then_inc(sem("conv_done"), 1)
                    if c > 0:
                        q = NCH * L + c - 1
                        part = slice((c - 1) * CH, c * CH)
                        dve.wait_ge(sem("b_rows"), q + 1)
                        bc = PS[0:96, 4, :]
                        if c >= 3:
                            dve.wait_ge(sem("split_done"), 2 * (q - 1))
                        link(nc.vector.tensor_copy(STK[0:96, part], bc))
                        nc.vector.tensor_tensor(split_rest((c - 1) % 2), bc, STK[0:96, part], ALU.subtract).then_inc(sem("split_rest"), 1)
                sp_low(NCH - 1)
                for c in range(NCH):
                    q = NCH * L + c
                    part = slice(c * CH, (c + 1) * CH)
                    dve.wait_ge(sem("sp_log"), q + 1)
                    dve.wait_ge(sem("sp_rest"), q + 1)
                    nc.vector.tensor_tensor(delta[:, :, part], one_e[:, :, part], above[:, :, part], ALU.add).then_inc(sem("delta_ready"), 1)
                    if c == 0:
                        scale_inputs(0)
                dve.wait_ge(sem("delta_ready"), NCH * (L + 1))
                nc.vector.memset(BIG[:, 8192:16384].rearrange("p (s t) -> p s t", t=SPAN)[:, :, 0:1], 0.0).then_inc(sem("dec_zeroed"), 1)
                for m in range(HALVES):
                    ins = nc.vector.tensor_tensor(
                        a0[:, m, :, 0:UNITS],
                        delta[:, m, :].rearrange("p (i t) -> p i t", t=SPAN)[:, :, 0].unsqueeze(1).to_broadcast([P, NST, UNITS]),
                        NEGA[:, HALVES * L + m, :].unsqueeze(2).to_broadcast([P, NST, UNITS]), ALU.mult)
                ins.then_inc(sem("a0_arg"), 1)
                for c in range(1, NCH):
                    scale_inputs(c)
                dve.wait_ge(sem("a0_exp"), L + 1)
                nc.vector.memset(a0[:, :, :, 0:UNITS + 1:UPB], 0.0).then_inc(sem("a0_ready"), 1)
                dve.wait_ge(sem("a0_ready"), L + 1)
                U0 = L * UNITS

                def dve_slot(s, base, groups):
                    par = s % 2
                    if s % GRP == 0 or (isinstance(base, int) and base + s == 0):
                        dve.wait_ge(sem("decays_ready"), (U0 + s) // GRP + 1 + groups)
                    if not (isinstance(base, int) and base + s == 0):
                        dve.wait_ge(sem("readout"), U0 + base + s)
                    dve.wait_ge(sem("v_ps"), U0 + base + s + 1)
                    dve.wait_ge(sem("carried"), U0 + L + base + s + 1)
                    first_step = PS[:, 0:4, :].rearrange("p (m j) (n t) -> p m (j n) t", m=HALVES, t=SPAN)[:, :, :, 0]
                    nc.vector.tensor_tensor(first_step, first_step, carry, ALU.add).then_inc(sem("carry_added"), 1)
                    dve.wait_ge(sem("carry_added"), U0 + base + s + 1)
                    for m in range(HALVES):
                        nc.vector.tensor_tensor_scan(
                            state[:, m].rearrange("p n t -> p (n t)"),
                            dec[s // GRP % 2][:, m, s % GRP].rearrange("p n t -> p (n t)"),
                            flat(PS[:, 2 * m:2 * m + 2, :]), 0.0, ALU.mult, ALU.add).then_inc(sem(f"state{m}"), 1)
                    dve.wait_ge(sem("state0"), U0 + base + s + 1)
                    dve.wait_ge(sem("state1"), U0 + base + s + 1)
                    nxt = a0[:, :, :, base + s + 1] if isinstance(base, int) else a0[:, :, :, bass.ds(base + s + 1, 1)].rearrange("p m n i -> p m (n i)")
                    nc.vector.tensor_tensor(carry, nxt, state[:, :, :, SPAN - 1], ALU.mult).then_inc(sem("carried"), 1)
                    dve.wait_ge(sem("c_ps"), U0 + base + s + 1)
                    if not (isinstance(base, int) and base + s < 2):
                        dve.wait_ge(sem("y_ps"), U0 + base + s - 1)
                    nc.vector.tensor_tensor(prod[par].rearrange("p m n t -> p m (n t)"), state.rearrange("p m n t -> p m (n t)"),
                                            flat(PS[:, 4:6, :]).unsqueeze(1).to_broadcast([P, HALVES, NST * SPAN]),
                                            ALU.mult).then_inc(sem("readout"), 1)
                    if not (isinstance(base, int) and base + s < 2):
                        gate(s - 2, base)

                def gate(s, base):
                    dve.wait_ge(sem("y_ps"), U0 + base + s + 1)
                    at = (base + s) * SPAN
                    sl = slice(at, at + SPAN) if isinstance(at, int) else bass.ds(at, SPAN)
                    nc.vector.tensor_tensor(Y[:, :, sl], PS[:, 7, 0:2 * SPAN].rearrange("p (m t) -> p m t", m=HALVES), zs[:, :, sl],
                                            ALU.mult).then_inc(sem("gated"), 1)

                dve_slot(0, 0, 0)
                dve_slot(1, 0, 0)
                with dve.Fori(0, B - 1) as b:
                    for s in range(2, UPB + 2):
                        dve_slot(s, UPB * b, UPB // GRP * b)
                for s in range(2, UPB):
                    dve_slot(s, UNITS - UPB, (UNITS - UPB) // GRP)

                def add_projected(c):
                    dve.wait_ge(sem("outproj_ps"), NCH * L + c + 1)
                    nc.vector.tensor_tensor(ch(X[:, :], c), ch(X[:, :], c), PS[:, c, :], ALU.add).then_inc(sem("outproj_added"), 1)

                add_projected(0)
                gate(UPB - 2, UNITS - UPB)
                add_projected(1)
                add_projected(2)
                gate(UPB - 1, UNITS - UPB)
                add_projected(3)
            dve.wait_ge(sem("x_again"), 16)
            dve.wait_ge(sem("outproj_added"), NCH * LAYERS)
            for c in range(NCH):
                nc.vector.tensor_tensor(ch(X[:, :], c), ch(X[:, :], c), ch(XN, c), ALU.add).then_inc(sem("stream_added"), 1)

            def by_block(ap):
                return ap.rearrange("p (b e) -> p b e", e=EXP)

            def over(ap):
                return ap.unsqueeze(2).to_broadcast([P, NBLK, EXP])

            def moe(k):
                for c in range(NCH):
                    dve.wait_ge(sem("moe_squared"), NCH * k + c + 1)
                    nc.vector.tensor_copy(ch(centred, c), PS[:, c, :]).then_inc(sem("moe_centred"), 1)
                R = [RT[:, i, :] for i in range(11)]
                S = [RTS[:, i, :] for i in range(8)]
                dve.wait_ge(sem("logits_ps"), k + 1)
                lg = PS[:, 0, 0:P]
                link(nc.vector.tensor_reduce(S[0], by_block(lg), AX.X, ALU.max))
                link(nc.vector.tensor_tensor(by_block(R[10]), by_block(lg), over(S[0]), ALU.subtract))
                link(nc.vector.scalar_tensor_tensor(out=R[2], in0=R[10], scalar=0.0, in1=CST[:, C_RAMP, :],
                                                    op0=ALU.is_equal, op1=ALU.mult))
                link(nc.vector.tensor_reduce(S[1], by_block(R[2]), AX.X, ALU.max))
                nc.vector.tensor_tensor(by_block(R[3]), by_block(R[2]), over(S[1]), ALU.is_equal).then_inc(sem("chosen"), 1)
                link(nc.vector.memset(R[5], 1.0))
                link(nc.vector.memset(R[5].rearrange("p (e b) -> p e b", b=NBLK)[:, :, 0:1], 0.0))
                dve.wait_ge(sem("counts_ps"), k + 1)
                tot = by_block(PS[:, 2, 0:P]).rearrange("p b e -> p e b")
                link(nc.vector.tensor_copy(R[4].rearrange("p (e b) -> p e b", b=NBLK), tot))
                link(nc.vector.tensor_tensor_scan(R[6], R[5], R[4], 0.0, ALU.mult, ALU.add))
                link(nc.vector.tensor_tensor(R[6], R[6], R[4], ALU.subtract))
                link(nc.vector.tensor_tensor(by_block(R[7]), by_block(PS[:, 1, 0:P]),
                                             R[6].rearrange("p (e b) -> p b e", b=NBLK), ALU.add))
                link(nc.vector.scalar_tensor_tensor(out=R[8], in0=R[7], scalar=float(CAP), in1=R[3],
                                                    op0=ALU.is_le, op1=ALU.mult))
                link(nc.vector.tensor_tensor(R[7], R[7], CST[:, C_EBASE, :], ALU.add))
                link(nc.vector.tensor_tensor(R[7], R[7], R[8], ALU.mult))
                link(nc.vector.tensor_reduce(S[4], by_block(R[7]), AX.X, ALU.add))
                link(nc.vector.tensor_reduce(S[5], by_block(R[8]), AX.X, ALU.add))
                link(nc.vector.tensor_scalar(S[6], S[5], -FAR, FAR, ALU.mult, ALU.add))
                link(nc.vector.tensor_tensor(S[6], S[6], S[4], ALU.add))
                dve.wait_ge(sem("token_std"), k + 1)
                nc.vector.reciprocal(RTS[:, 8, :], RTS[:, 8, :]).then_inc(sem("token_rstd"), 1)
                dve.wait_ge(sem("token_rstd"), k + 1)
                nc.vector.tensor_tensor(by_block(R[9]), by_block(R[10]), over(RTS[:, 8, :]), ALU.mult).then_inc(sem("shifted"), 1)
                link(nc.vector.tensor_scalar(S[1], S[6], 1.0 / P, None, ALU.mult))
                link(nc.vector.tensor_tensor(passed, S[1].unsqueeze(2).to_broadcast([P, NBLK, ST + 1]),
                                             CST[:, C_IOTA, 0:ST + 1].unsqueeze(1).to_broadcast([P, NBLK, ST + 1]), ALU.is_ge))
                link(nc.vector.tensor_reduce(S[2], passed[:, :, 1:], AX.X, ALU.add))
                link(nc.vector.scalar_tensor_tensor(out=S[2], in0=S[2], scalar=-float(P), in1=S[6], op0=ALU.mult, op1=ALU.add))
                link(nc.vector.tensor_tensor(passed[:, :, 0:ST], passed[:, :, 0:ST], passed[:, :, 1:], ALU.subtract))
                link(nc.vector.tensor_tensor(tile_hot, passed[:, :, 0:ST].unsqueeze(2).to_broadcast([P, NBLK, 2, ST]),
                                             digits.unsqueeze(3).to_broadcast([P, NBLK, 2, ST]), ALU.mult))
                for t in range(NBLK):
                    nc.vector.tensor_scalar(row_hot[:, t, :], CST[:, C_IOTA, :], S[2][:, t:t + 1], None, ALU.is_equal
                                            ).then_inc(sem("row_hot"), 1)
                dve.wait_ge(sem("index_ps"), k + 1)
                link(nc.vector.tensor_copy(R[6][:, 0:ST], PS[:, 3, ST:2 * ST]))
                link(nc.vector.scalar_tensor_tensor(out=R[6][:, 0:ST], in0=PS[:, 3, 0:ST], scalar=64.0, in1=R[6][:, 0:ST],
                                                    op0=ALU.mult, op1=ALU.add))
                nc.vector.tensor_scalar(IDX[:, :], R[6][:, 0:ST], FAR, None, ALU.add).then_inc(sem("indices_ready"), 1)
                dve.wait_ge(sem("route_exp"), k + 1)
                link(nc.vector.tensor_reduce(S[7], by_block(R[9]), AX.X, ALU.add))
                link(nc.vector.reciprocal(S[3], S[7]))
                link(nc.vector.tensor_tensor(S[7], S[3], S[5], ALU.mult))
                for t in range(NBLK):
                    nc.vector.tensor_scalar(diag[:, t, :], ident, S[7][:, t:t + 1], None, ALU.mult).then_inc(sem("diagonals"), 1)

                def turned(g):
                    dve.wait_ge(sem("disp_ps"), ST // GS * k + g + 1)
                    nc.vector.tensor_copy(xdisp[:, g * CH:(g + 1) * CH], PS[:, g % 2, :]).then_inc(sem("dispatched"), 1)

                turned(0)
                turned(1)
                for e in range(EXP):
                    made(k, e)
                    if e + 2 < ST // GS:
                        turned(e + 2)
                for c in range(NCH):
                    dve.wait_ge(sem("moe_ps"), NCH * k + c + 1)
                    nc.vector.tensor_tensor(ch(X[:, :], c), ch(X[:, :], c), PS[:, 2 + c, :], ALU.add).then_inc(sem("moe_added"), 1)

            def made(k, e):
                if k == 0 and e == 0:
                    dve.wait_ge(sem("b2_loaded"), 16)
                dve.wait_ge(sem("rows2_ps"), EXP * k + e + 1)
                for i, (h, a, n, _) in enumerate(pieces(e)):
                    nc.vector.tensor_tensor(rows_out[a:a + n, h, :], PS[a:a + n, 6 + e % 2, i * P:(i + 1) * P],
                                            B2R[a:a + n, e, :], ALU.add).then_inc(sem("rows_made"), 1)

            moe(0)
            norm_dve(dve, 3)
            dve.wait_ge(sem("rank16_ps"), NCH)
            nc.vector.tensor_copy(tile(5)[0:16, QTOK:TOK], flat(PS[0:16, 2:4, :])).then_inc(sem("rank16"), 1)
            dve.wait_ge(sem("kg_log"), 1)
            nc.vector.scalar_tensor_tensor(out=tile(2)[:, 0:QTOK], in0=flat(PS[:, 4:6, :]), scalar=0.0,
                                           in1=tile(1)[:, 0:QTOK], op0=ALU.min, op1=ALU.subtract).then_inc(sem("log_gate"), 1)
            dve.wait_ge(sem("gla_decay"), 1)
            nc.vector.memset(tile(0)[:, 0:QTOK:SEQ], 0.0).then_inc(sem("gla_decay0"), 1)
            for i in range(2 * GT):
                th, g = divmod(i, GT)
                vt = zs[:, 0, th * QTOK:(th + 1) * QTOK]
                kv = tile(1)[:, 0:QTOK]
                st = tile(1)[:, QTOK:TOK]
                out = tile(2)[:, (i % 2) * QTOK:(i % 2 + 1) * QTOK]
                dve.wait_ge(sem("v_out"), th + 1)
                dve.wait_ge(sem("k_ps"), i + 1)
                nc.vector.scalar_tensor_tensor(out=kv, in0=flat(PS[:, 0:2, :]), scalar=DK ** -0.5, in1=vt,
                                               op0=ALU.mult, op1=ALU.mult).then_inc(sem("kv_done"), 1)
                dve.wait_ge(sem("decay_ps"), i + 1)
                dve.wait_ge(sem("kv_done"), i + 1)
                nc.vector.tensor_tensor_scan(st, flat(PS[:, 4:6, :]), kv, 0.0, ALU.mult, ALU.add).then_inc(sem("gla_state"), 1)
                dve.wait_ge(sem("q_ps"), i + 1)
                dve.wait_ge(sem("gla_state"), i + 1)
                if i >= 2:
                    dve.wait_ge(sem("summed"), (GT - 1) * ((i - 2) // GT) + max((i - 2) % GT, 1))
                nc.vector.tensor_tensor(out, st, flat(PS[:, 2:4, :]), ALU.mult).then_inc(sem("qs_done"), 1)
            norm_dve(dve, 4)
            dve.wait_ge(sem("gate_out"), NCH)
            dve.wait_ge(sem("norm_out"), norm_done(4))
            for c in range(NCH):
                nc.vector.tensor_tensor(ch(xs[:, 1, :], c), ch(tile(6), c), ch(xs[:, 0, :], c), ALU.mult).then_inc(sem("o_gated"), 1)
            for c in range(NCH):
                dve.wait_ge(sem("attn_ps"), c + 1)
                nc.vector.tensor_tensor(ch(X[:, :], c), ch(X[:, :], c), PS[:, c, :], ALU.add).then_inc(sem("attn_added"), 1)
            moe(1)

        @block.tensor
        def _(pe):
            def mm(out, lhsT, rhs, start=True, stop=True):
                return nc.tensor.matmul(out, lhsT, rhs, start=start, stop=stop)

            pe.wait_ge(sem("centring_loaded"), 16)
            norm_pe(pe, 0)
            for L in range(LAYERS):
                norm_pe(pe, 1 + L)
                if L == 0:
                    pe.wait_ge(sem("mamba_loaded"), 64)

                def in_proj(c, part):
                    q = NCH * L + c
                    pe.wait_ge(sem("norm_out"), norm_done(1 + L, c))
                    for m in range(HALVES):
                        if c > 0:
                            pe.wait_ge(sem("z_out" if part else "xb_out"), HALVES * (q - 1) + m + 1)
                        k = HALVES * part + m
                        mm(PS[:, k, :], WIN[:, L, k * P:(k + 1) * P], ch(XN, c)).then_inc(sem("z_ps" if part else "inner_ps"), 1)

                def x_proj(c):
                    q = NCH * L + c
                    part = slice(c * CH, (c + 1) * CH)
                    pe.wait_ge(sem("xs_ready"), q + 1)
                    if c:
                        pe.wait_ge(sem("rank_ready"), q)
                        pe.wait_ge(sem("split_rest"), q)
                        pe.wait_ge(sem("bt_ready"), q)
                    for m in range(HALVES):
                        ins = mm(PS[0:XW, 4, :], XPW[:, L, m, :], xs[:, m, part], m == 0, m == HALVES - 1)
                    ins.then_inc(sem("xproj_ps"), 1)

                def dt_proj(c):
                    q = NCH * L + c
                    pe.wait_ge(sem("rank_ready"), q + 1)
                    if c:
                        pe.wait_ge(sem("sp_abs"), q)
                        pe.wait_ge(sem("sp_max"), q)
                    for m in range(HALVES):
                        ins = mm(PS[:, 6 + m, :], DTW[96:96 + DTR + 1, L, m * P:(m + 1) * P], rank(c % 2)[96:96 + DTR + 1, :])
                    ins.then_inc(sem("dt_ps"), 1)
                    pe.wait_ge(sem("b_rows"), q + 1)
                    for k in range(UPB):
                        ins = nc.tensor.transpose(PS[0:SPAN, 5, k * NST:(k + 1) * NST], b_rows(c % 2)[:, k * SPAN:(k + 1) * SPAN],
                                                  ident[0:NST, 0:NST])
                    ins.then_inc(sem("bt_ps"), 1)

                in_proj(0, 0)
                in_proj(0, 1)
                for c in range(NCH):
                    if c + 1 < NCH:
                        in_proj(c + 1, 0)
                        in_proj(c + 1, 1)
                    x_proj(c)
                    dt_proj(c)
                pe.wait_ge(sem("zero_set"), 2)
                pe.wait_ge(sem("sp_abs"), NCH * (L + 1))
                pe.wait_ge(sem("sp_max"), NCH * (L + 1))
                pe.wait_ge(sem("momentum_rows"), 32 * (L + 1))
                U0 = L * UNITS

                def turn(s, base):
                    par = s % 2
                    pe.wait_ge(sem("us_ready"), U0 + base + s + 1)
                    if not (isinstance(base, int) and base + s == 0):
                        pe.wait_ge(sem("ut_out"), U0 + base + s)
                    if s % UPB == 0:
                        mm(PS[SPAN:SPAN + NST, 6, 0:256], zero_w, flat(CST[0:SPAN + NST, 0:2, :]))
                    else:
                        pe.wait_ge(sem("rb_ready"), U0 + base + s)
                        mm(PS[SPAN:SPAN + NST, 6, 0:256], rbm[1 - par].rearrange("p (n t) -> p n t", n=NST)[:, :, SPAN - 1],
                           ut[1 - par])
                    for m in range(HALVES):
                        ins = nc.tensor.transpose(PS[0:SPAN, 6, m * P:(m + 1) * P], us[par][:, m, :], ident)
                    ins.then_inc(sem("ut_ps"), 1)

                def sum_y(s, base):
                    pe.wait_ge(sem("folded"), 2 * (U0 + base + s) + 2)
                    if not (isinstance(base, int) and base + s == 0):
                        pe.wait_ge(sem("gated"), U0 + base + s)
                    at = (base + s) * SPAN
                    sl = slice(at, at + SPAN) if isinstance(at, int) else bass.ds(at, SPAN)
                    mm(PS[:, 7, 0:2 * SPAN], ident, Y[:, :, sl], True, False)
                    for n in range(4):
                        ins = mm(PS[:, 7, 0:2 * SPAN], ident, prod[s % 2][:, :, n, :], False, n == 3)
                    ins.then_inc(sem("y_ps"), 1)

                def out_proj(c):
                    pe.wait_ge(sem("gated"), U0 + UPB * (c + 1))
                    for m in range(HALVES):
                        ins = mm(PS[:, c, :], WOUT[:, L, m, :], Y[:, m, c * CH:(c + 1) * CH], m == 0, m == HALVES - 1)
                    ins.then_inc(sem("outproj_ps"), 1)

                def pe_slot(s, base, turned=True):
                    par = s % 2
                    first = isinstance(base, int) and base + s == 0
                    pe.wait_ge(sem("ut_out"), U0 + base + s + 1)
                    pe.wait_ge(sem("rb_ready"), U0 + base + s + 1)
                    for m in range(HALVES):
                        if not first:
                            pe.wait_ge(sem(f"state{m}"), U0 + base + s)
                        for j in range(2):
                            ins = mm(PS[:, 2 * m + j, :], ut[par][:, m * P:(m + 1) * P],
                                     rbm[par][:, j * CH:(j + 1) * CH])
                    ins.then_inc(sem("v_ps"), 1)
                    if not first:
                        pe.wait_ge(sem("readout"), U0 + base + s)
                    at = (base + s) * SPAN
                    sl = slice(at, at + SPAN) if isinstance(at, int) else bass.ds(at, SPAN)
                    for n in range(NST):
                        ins = mm(PS[:, 4 + n // 8, (n % 8) * SPAN:(n % 8 + 1) * SPAN], SEL[0:96, n, :], STK[0:96, sl])
                    ins.then_inc(sem("c_ps"), 1)
                    if not (isinstance(base, int) and base + s < 2):
                        sum_y(s - 2, base)
                    if turned:
                        turn(s + 2, base)

                turn(0, 0)
                turn(1, 0)
                pe.wait_ge(sem("split_done"), 2 * NCH * (L + 1))
                pe.wait_ge(sem("sel_ready"), 1)
                pe.wait_ge(sem("dx_ready"), HALVES * NCH * (L + 1))
                pe_slot(0, 0)
                pe_slot(1, 0)
                with pe.Fori(0, B - 1) as b:
                    for s in range(2, UPB + 2):
                        pe_slot(s, UPB * b)
                for s in range(2, UPB):
                    pe_slot(s, UNITS - UPB, s + 2 < UPB)
                pe.wait_ge(sem("state1"), U0 + UNITS)
                out_proj(0)
                sum_y(UPB - 2, UNITS - UPB)
                out_proj(1)
                out_proj(2)
                sum_y(UPB - 1, UNITS - UPB)
                out_proj(3)

            def moe(k):
                for c in range(NCH):
                    pe.wait_ge(sem("stream_added" if k == 0 else "attn_added"), c + 1)
                    mm(PS[:, c, :], CST[:, C_CENTRE, :], ch(X[:, :], c)).then_inc(sem("centred_ps"), 1)
                pe.wait_ge(sem("moe_centred"), NCH * (k + 1))
                for t in range(NBLK):
                    ins = mm(PS[:, 0, EXP * t:EXP * (t + 1)], centred[:, t * P:(t + 1) * P],
                             SMT[:, SM["gate"]:SM["gate"] + EXP])
                ins.then_inc(sem("logits_ps"), 1)
                pe.wait_ge(sem("chosen"), k + 1)
                mm(PS[:, 1, 0:P], CST[:, C_TRI, :], RT[:, 3, :])
                mm(PS[:, 2, 0:P], CST[:, C_ONE, :], RT[:, 3, :]).then_inc(sem("counts_ps"), 1)
                for t in range(NBLK):
                    ins = mm(PS[:, 3, 256 + t:257 + t], sq_moe[:, t * P:(t + 1) * P], CST[:, C_AVG, 0:1])
                ins.then_inc(sem("token_var_ps"), 1)
                for c in range(NCH):
                    for t in range(4):
                        ins = nc.tensor.transpose(PS[:, 4 + c, t * P:(t + 1) * P],
                                                  centred[:, (4 * c + t) * P:(4 * c + t + 1) * P], ident)
                    ins.then_inc(sem("rows_ps"), 1)
                for t in range(NBLK):
                    pe.wait_ge(sem("row_hot"), NBLK * k + t + 1)
                    ins = mm(PS[:, 3, 0:2 * ST], row_hot[:, t, :], tile_hot[:, t].rearrange("p i h -> p (i h)"),
                             t == 0, t == NBLK - 1)
                ins.then_inc(sem("index_ps"), 1)
                pe.wait_ge(sem("indices_ready"), k + 1)
                pe.wait_ge(sem("token_rows"), NBLK * (k + 1))
                if k == 0:
                    pe.wait_ge(sem("experts_loaded"), 32)

                def turn_rows(g):
                    pe.wait_ge(sem(f"gathered{g}"), 16 * GS * (k + 1))
                    if g >= 2:
                        pe.wait_ge(sem("dispatched"), ST // GS * k + g - 1)
                    for i in range(GS):
                        ins = nc.tensor.transpose(PS[:, g % 2, i * P:(i + 1) * P], rows_in[:, GS * g + i, :], ident)
                    ins.then_inc(sem("disp_ps"), 1)

                def first_layer(e):
                    pe.wait_ge(sem("dispatched"), ST // GS * k + ((e + 1) * CAP + CH - 1) // CH)
                    for j in range(FJ):
                        if e:
                            pe.wait_ge(sem("hidden"), FJ * (EXP * k + e - 1) + j + 1)
                        mm(PS[:, 2 + j, 0:CAP], W1[:, e, j * P:(j + 1) * P], xdisp[:, e * CAP:(e + 1) * CAP]
                           ).then_inc(sem("hid_ps"), 1)

                def second_layer(e):
                    pe.wait_ge(sem("hidden"), FJ * (EXP * k + e + 1))
                    if e >= 2:
                        pe.wait_ge(sem("rows_made"), NT * (EXP * k + e - 1))
                    for i, (_, a, n, s0) in enumerate(pieces(e)):
                        for j in range(FJ):
                            ins = mm(PS[a:a + n, 6 + e % 2, i * P:(i + 1) * P], hid[e % 2][:, j, s0:s0 + n], W2[:, e, j, :],
                                     j == 0, j == FJ - 1)
                    ins.then_inc(sem("rows2_ps"), 1)

                turn_rows(0)
                first_layer(0)
                turn_rows(1)
                for e in range(EXP):
                    if e + 1 < EXP:
                        first_layer(e + 1)
                    if e + 2 < ST // GS:
                        turn_rows(e + 2)
                    second_layer(e)
                for c in range(NCH):
                    pe.wait_ge(sem(f"fetched{c}"), 16 * (k + 1))
                    pe.wait_ge(sem("diagonals"), NBLK * k + 4 * c + 4)
                    for t in range(4):
                        ins = mm(PS[:, 2 + c, t * P:(t + 1) * P], fetched[:, 4 * c + t, :], diag[:, 4 * c + t, :])
                    ins.then_inc(sem("moe_ps"), 1)

            moe(0)
            norm_pe(pe, 3)
            pe.wait_ge(sem("gla_loaded"), 32)
            for c in range(NCH):
                pe.wait_ge(sem("norm_out"), norm_done(3, c))
                mm(PS[0:16, c, :], GW[:, GG1:GG1 + 16], ch(XN[:, :], c)).then_inc(sem("rank16_ps"), 1)
            pe.wait_ge(sem("norm_out"), norm_done(3))

            def gate(c):
                mm(PS[:, 6 + c % 2, :], GW[:, GG:GG + P], ch(XN[:, :], c)).then_inc(sem("gate_ps"), 1)

            pe.wait_ge(sem("rank16"), 2)
            kr = HEADS * DK
            for c in range(NCH):
                mm(PS[c // 2 * kr:(c // 2 + 1) * kr, 4 + c % 2, :], WG2[0:16, :], ch(tile(5)[0:16, :], c)).then_inc(sem("kg_ps"), 1)

            def part(i, bank, w0):
                th, g = divmod(i, GT)
                for j in range(2):
                    a = th * QTOK + j * CH
                    ins = mm(PS[:, bank + j, :], GW[:, w0 + g * P:w0 + (g + 1) * P], XN[:, a:a + CH])
                return ins

            def values(th):
                for j in range(2):
                    ins = mm(PS[:, 6 + j, :], GW[:, GV:GV + P], ch(XN[:, :], 2 * th + j))
                ins.then_inc(sem("values_ps"), 1)

            def keys(i):
                if i:
                    pe.wait_ge(sem("kv_done"), i)
                part(i, 0, GK).then_inc(sem("k_ps"), 1)

            def decay(i):
                th, g = divmod(i, GT)
                if i:
                    pe.wait_ge(sem("gla_state"), i)
                for j in range(2):
                    ins = mm(PS[:, 4 + j, :], SPR[th * kr:(th + 1) * kr, g, :],
                             tile(0)[th * kr:(th + 1) * kr, j * CH:(j + 1) * CH])
                ins.then_inc(sem("decay_ps"), 1)

            def queries(i):
                if i:
                    pe.wait_ge(sem("qs_done"), i)
                part(i, 2, GQ).then_inc(sem("q_ps"), 1)

            values(0)
            keys(0)
            queries(0)
            pe.wait_ge(sem("gla_decay0"), 1)
            decay(0)
            pe.wait_ge(sem("v_out"), 1)
            values(1)
            pe.wait_ge(sem("v_out"), 2)
            for i in range(1, 2 * GT):
                keys(i)
                decay(i)
                queries(i)
                if i == 1:
                    gate(0)
                    gate(1)
                if i == 2:
                    pe.wait_ge(sem("gate_out"), 2)
                    gate(2)
                    gate(3)
            pe.wait_ge(sem("qs_done"), 2 * GT)
            norm_pe(pe, 4)
            for c in range(NCH):
                pe.wait_ge(sem("o_gated"), c + 1)
                mm(PS[:, c, :], GW[:, GO:GO + P], ch(xs[:, 1, :], c)).then_inc(sem("attn_ps"), 1)
            moe(1)


_SHAPES = {
    "x": (P, TOK), "consts": (P, NCONST, P), "small": (P, SMALL), "w_in": (P, LAYERS, 4 * P),
    "w_x": (P, LAYERS, HALVES, XW), "w_dt": (DTR + 1, LAYERS, HALVES * P), "w_out": (P, LAYERS, HALVES, P),
    "sel": (96, NST * P), "momentum": (P - SPAN, NST * SPAN), "w1": (P, EXP, DFF), "w2": (P, EXP, FJ, P), "b2": (P, EXP * P),
    "w_gla": (P, GEND), "gla_consts": (P, GT * P + HEADS * DK),
}


def _constants():
    i = np.arange(P)
    c = np.zeros((P, NCONST, P), np.float32)
    c[:, C_ID] = np.eye(P)
    c[:, C_AVG] = 1.0 / D
    c[:, C_AVG8] = (i[:, None] // DV == i[None] // DV) / DV
    c[:, C_TRI] = i[:, None] <= i[None]
    c[:, C_ONE] = 1.0
    c[:, C_RAMP] = EXP - i % EXP
    lag = i[None, :SPAN] - i[:SPAN, None]
    c[:SPAN, C_MASK, :SPAN] = np.where(lag >= 0, BETA ** np.maximum(lag, 0).astype(np.float64), 0.0)
    momentum = np.eye(NST)[:, :, None] * BETA ** (1.0 + np.arange(SPAN))
    c[:, C_EBASE] = (i % EXP) * CAP - 1
    c[:, C_IOTA] = i[None]
    c[:, C_CENTRE] = np.eye(P) - 1.0 / D
    c[:, C_CENTRE8] = np.eye(P) - (i[:, None] // DV == i[None] // DV) / DV
    number = P * np.arange(NBLK)[None] + i[:, None] - FAR
    c[:, C_MASK, 64:64 + 2 * NBLK] = np.stack([number // 64, number % 64], 2).reshape(P, -1)
    k, r = np.arange(96), np.arange(NST)
    sel = np.repeat((k[:, None] % 32 == NST + r[None]).astype(np.float32)[:, :, None], P, 2).reshape(96, -1)
    g = np.arange(GT)
    spr = (i[None, None, :] // DV * DK + g[:, None, None] == i[None, :, None] % (HEADS * DK)).astype(np.float32)
    momentum = np.concatenate([momentum.reshape(NST, -1), np.zeros((P - SPAN - NST, NST * SPAN))])
    return c, sel, momentum.astype(np.float32), spr.transpose(1, 0, 2).reshape(P, -1)


def kernel(**inputs):
    import concourse.bacc as bacc
    from concourse.bass_utils import run_bass_kernel_spmd

    a = {k: np.asarray(v) for k, v in inputs.items()}
    ma = {k[len("L0_attn_a_"):]: v for k, v in a.items() if k.startswith("L0_attn_a_")}
    at = {k[len("L0_attn_b_"):]: v for k, v in a.items() if k.startswith("L0_attn_b_")}
    ff = {k[len("L0_ffn_"):]: v for k, v in a.items() if k.startswith("L0_ffn_")}
    consts, sel, momentum, spr = _constants()

    def halves(v):
        v = v.reshape(LAYERS, HALVES, P, -1)
        return v.transpose(2, 0, 1, 3).reshape(P, -1)

    small = np.concatenate([
        halves(ma["conv_w"]), halves(ma["conv_b"]), halves(ma["Dp"]), ma["norm_w"].T,
        halves(ma["A_log"]), ff["b1"].reshape(EXP, FJ, P).transpose(2, 0, 1).reshape(P, -1),
        at["bg"].reshape(P, 1), ff["gate_w"].T], 1)
    xp = ma["x_proj_w"]
    bc = xp[:, DTR:]
    xw = np.concatenate([bc, bc, bc, xp[:, :DTR]], 1)
    rep_k = (np.arange(DK)[:, None, None] + DK * np.arange(HEADS)[None, :, None] + np.zeros((1, 1, DV), int)).reshape(-1)
    wg2 = np.zeros((P, HEADS * DK), np.float32)
    wg2[0:16] = at["Wg2"]
    arrays = {
        "x": ma["x"].reshape(TOK, D).T,
        "consts": consts,
        "small": small,
        "w_in": ma["in_proj_w"].transpose(2, 0, 1),
        "w_x": xw.reshape(LAYERS, XW, HALVES, P).transpose(3, 0, 2, 1),
        "w_dt": np.concatenate([ma["dt_w"].transpose(2, 0, 1), ma["dt_b"][None]], 0),
        "w_out": ma["out_w"].reshape(LAYERS, P, HALVES, P).transpose(3, 0, 2, 1),
        "sel": sel,
        "momentum": momentum,
        "w1": ff["w1"].transpose(1, 0, 2),
        "w2": ff["w2"].reshape(EXP, FJ, P, D).transpose(2, 0, 1, 3),
        "b2": np.repeat(ff["b2"].reshape(1, -1), P, 0),
        "w_gla": np.concatenate([at["Wq"][:, rep_k], at["Wk"][:, rep_k], at["Wv"], at["Wg"], at["Wo"], at["Wg1"]], 1),
        "gla_consts": np.concatenate([spr, wg2], 1),
    }
    nc = bacc.Bacc("TRN2", target_bir_lowering=False, num_devices=1)
    io, host = {}, {}
    for name, shape in _SHAPES.items():
        host[f"in_{name}"] = np.ascontiguousarray(arrays[name])
        assert host[f"in_{name}"].shape == shape, (name, host[f"in_{name}"].shape, shape)
        io[name] = nc.dram_tensor(f"in_{name}", shape, F32, kind="ExternalInput").ap()
    io["out"] = nc.dram_tensor("out_x", (P, TOK), F32, kind="ExternalOutput").ap()
    build(nc, io)
    r = run_bass_kernel_spmd(nc, [host], core_ids=[0])
    return np.ascontiguousarray(r.results[0]["out_x"].T).reshape(B, SEQ, D)
```
